# Optimizing a Trainium2 kernel written in Bass

```python
import numpy as np
import jax
import jax.numpy as jnp

def _softmax(x, axis=-1):
    return jax.nn.softmax(x, axis=axis)

def _gelu(x):
    return jax.nn.gelu(x, approximate=True)

def _silu(x):
    return jax.nn.silu(x)

def _sigmoid(x):
    return jax.nn.sigmoid(x)

def _layernorm(x, axis=-1, eps=1e-05):
    m = jnp.mean(x, axis=axis, keepdims=True)
    v = jnp.var(x, axis=axis, keepdims=True)
    return (x - m) / jnp.sqrt(v + eps)

def _scatter_add(tgt, idx, src, axis=0):
    return tgt.at[idx].add(src)

def _segment_sum(src, seg, n):
    return jax.ops.segment_sum(src, seg, n)
kernel_name = 'mk_xattn_seq_d4_seqx_r8_26235d'

def setup_inputs(seed: int=0):
    np.random.seed(seed)
    _w = jnp.asarray

    def _rec_inputs():
        import jax
        import jax.numpy as jnp
        _rk = jax.random.key(seed)
        x = 7.22e-05 + 1 * jax.random.normal(jax.random.fold_in(_rk, 1), (16, 128, 256), jnp.float32)
        _lenS = 128 - jax.random.randint(jax.random.fold_in(_rk, 7), (16,), 0, max(1, 128 // 4) + 1, jnp.int32)
        _lenS2 = 128 - jax.random.randint(jax.random.fold_in(_rk, 8), (16,), 0, max(1, 128 // 4) + 1, jnp.int32)
        _ctx_2048P = jax.random.normal(jax.random.fold_in(_rk, 11), (16, 16, 256), jnp.float32)
        _ctx_2048c = jax.random.dirichlet(jax.random.fold_in(_rk, 511), 0.3 * jnp.ones((16,), jnp.float32), (16, 128))
        _ctx_2048t = jnp.einsum('bsk,bkd->bsd', _ctx_2048c, _ctx_2048P)
        _ctx_2048t = _ctx_2048t * jax.lax.rsqrt(jnp.mean(jnp.square(_ctx_2048t)) + 1e-12) * 0.953939
        ctx_2048 = 0.000189249 + 0.0999589 * (_ctx_2048t + 0.3 * jax.random.normal(jax.random.fold_in(_rk, 611), (16, 128, 256), jnp.float32))
        _validS = jnp.arange(128)[None, :] < _lenS[:, None]
        _validS2 = jnp.arange(128)[None, :] < _lenS2[:, None]
        _causal = jnp.tril(jnp.ones((128, 128), dtype=bool))
        mask_BxS2_ik0 = jnp.where(jnp.broadcast_to(_validS2[:, :], (16, 128)), 0, 1).astype(jnp.int32)
        mask_1x1xSxS2_fc1 = jnp.where(jnp.broadcast_to(_validS2[0:1, None, None, :], (1, 1, 128, 128)), 1.0, 0.0).astype(jnp.float32)
        mask_Bx1xSxS2_ff1 = jnp.where(jnp.ones((16, 1, 128, 128), dtype=bool), 1.0, 0.0).astype(jnp.float32)
        return (x, ctx_2048, mask_BxS2_ik0, mask_1x1xSxS2_fc1, mask_Bx1xSxS2_ff1)
    x, ctx_2048, mask_BxS2_ik0, mask_1x1xSxS2_fc1, mask_Bx1xSxS2_ff1 = _rec_inputs()

    def _L0_xattn_setup():
        import jax, jax.numpy as jnp
        import numpy as np
        E, H, L, B = (256, 32, 128, 4)
        S = E // H
        DM, DD = (32, 64)

        def _ln(x, w, b, eps=1e-05):
            m = x.mean(-1, keepdims=True)
            v = ((x - m) ** 2).mean(-1, keepdims=True)
            return (x - m) / jnp.sqrt(v + eps) * w + b

        def _block(x, state, ln1_w, ln1_b, ln2_w, ln2_b, maa_x, maa_w1, maa_w2, maa_stack, time_decay, td_w1, td_w2, u, Wr, Wk, Wv, Wg, Wo, gn_w, gn_b, ffn_maa_k, ffn_maa_r, Wfk, Wfr, Wfv):
            b, l, e = x.shape
            h = u.shape[0]
            s_ = e // h
            xa = _ln(x, ln1_w, ln1_b)
            sx = jnp.concatenate([state[:, 1:2] - xa[:, :1], xa[:, :-1] - xa[:, 1:]], axis=1)
            xxx = jnp.tanh((xa + sx * maa_x) @ maa_w1).reshape(b, l, 5, DM)
            xxx = jnp.einsum('blfd,fde->blfe', xxx, maa_w2)
            xm = xa[:, :, None] + sx[:, :, None] * (maa_stack + xxx)
            xk, xw, xv, xr, xg = (xm[:, :, j] for j in range(5))
            w = jnp.exp(-jnp.exp(time_decay + jnp.tanh(xw @ td_w1) @ td_w2)).reshape(b, l, h, s_)
            r = (xr @ Wr.T).reshape(b, l, h, s_)
            k = (xk @ Wk.T).reshape(b, l, h, s_)
            v = (xv @ Wv.T).reshape(b, l, h, s_)
            g = jax.nn.silu(xg @ Wg.T)
            s0 = state[:, 2:2 + s_].reshape(b, h, s_, s_)

            def step(s, rkvw):
                r_t, k_t, v_t, w_t = rkvw
                a = k_t[..., :, None] * v_t[..., None, :]
                out = jnp.einsum('bhi,bhij->bhj', r_t, u * a + s)
                s = a + w_t[..., :, None] * s
                return (s, out)
            rkvw = tuple((jnp.moveaxis(t, 1, 0) for t in (r, k, v, w)))
            _, out = jax.lax.scan(step, s0, rkvw)
            out = jnp.moveaxis(out, 0, 1).reshape(b, l, e)
            og = out.reshape(b, l, h, s_)
            m = og.mean(-1, keepdims=True)
            va = ((og - m) ** 2).mean(-1, keepdims=True)
            og = ((og - m) / jnp.sqrt(va + 1e-05)).reshape(b, l, e) * gn_w + gn_b
            x1 = x + og * g @ Wo.T
            xc = _ln(x1, ln2_w, ln2_b)
            sx2 = jnp.concatenate([state[:, 0:1] - xc[:, :1], xc[:, :-1] - xc[:, 1:]], axis=1)
            xk2 = xc + sx2 * ffn_maa_k
            xr2 = xc + sx2 * ffn_maa_r
            rr = jax.nn.sigmoid(xr2 @ Wfr.T)
            kk = jnp.square(jax.nn.relu(xk2 @ Wfk.T))
            return x1 + rr * (kk @ Wfv.T)
        key = jax.random.key(seed)
        ks = jax.random.split(key, 24)
        sc = 0.02
        d = {'x': jax.random.normal(ks[0], (B, L, E), jnp.float32), 'state': jax.random.normal(ks[1], (B, 2 + S, E), jnp.float32) * 0.1, 'ln1_w': jnp.ones((E,), jnp.float32), 'ln1_b': jnp.zeros((E,), jnp.float32), 'ln2_w': jnp.ones((E,), jnp.float32), 'ln2_b': jnp.zeros((E,), jnp.float32), 'maa_x': jax.random.normal(ks[2], (E,), jnp.float32) * 0.1, 'maa_w1': jax.random.normal(ks[3], (E, 5 * DM), jnp.float32) * sc, 'maa_w2': jax.random.normal(ks[4], (5, DM, E), jnp.float32) * sc, 'maa_stack': jax.random.normal(ks[5], (1, 5, E), jnp.float32) * 0.1, 'time_decay': jax.random.normal(ks[6], (E,), jnp.float32) * 0.5, 'td_w1': jax.random.normal(ks[7], (E, DD), jnp.float32) * sc, 'td_w2': jax.random.normal(ks[8], (DD, E), jnp.float32) * sc, 'u': jax.random.normal(ks[9], (H, S, 1), jnp.float32) * 0.1, 'Wr': jax.random.normal(ks[10], (E, E), jnp.float32) * sc, 'Wk': jax.random.normal(ks[11], (E, E), jnp.float32) * sc, 'Wv': jax.random.normal(ks[12], (E, E), jnp.float32) * sc, 'Wg': jax.random.normal(ks[13], (E, E), jnp.float32) * sc, 'Wo': jax.random.normal(ks[14], (E, E), jnp.float32) * sc, 'gn_w': jnp.ones((E,), jnp.float32), 'gn_b': jnp.zeros((E,), jnp.float32), 'ffn_maa_k': jax.random.normal(ks[15], (E,), jnp.float32) * 0.1, 'ffn_maa_r': jax.random.normal(ks[16], (E,), jnp.float32) * 0.1, 'Wfk': jax.random.normal(ks[17], (E, E), jnp.float32) * sc, 'Wfr': jax.random.normal(ks[18], (E, E), jnp.float32) * sc, 'Wfv': jax.random.normal(ks[19], (E, E), jnp.float32) * sc}
        return d
    _L0_xattn_all = _L0_xattn_setup()
    _L0_xattn_in = {k: v for k, v in _L0_xattn_all.items() if k in ('ln1_w', 'ln1_b', 'ln2_w', 'ln2_b', 'maa_x', 'maa_w1', 'maa_w2', 'maa_stack', 'time_decay', 'td_w1', 'td_w2', 'u', 'Wr', 'Wk', 'Wv', 'Wg', 'Wo', 'gn_w', 'gn_b', 'ffn_maa_k', 'ffn_maa_r', 'Wfk', 'Wfr', 'Wfv')}
    del _L0_xattn_all

    def _L1_xattn_setup():
        import jax, jax.numpy as jnp
        import numpy as np
        B, P, K, H, NH = (4, 256, 32, 256, 16)
        DH = H // NH
        EPS = 1e-06

        def rmsnorm(x, w):
            var = jnp.mean(jnp.square(x), axis=-1, keepdims=True)
            return x * jax.lax.rsqrt(var + EPS) * w
        key = jax.random.key(seed)
        ks = jax.random.split(key, 12)
        s = 0.02
        return {'x': jax.random.normal(ks[0], (B, P, H), jnp.float32), 'latents': jax.random.normal(ks[1], (B, K, H), jnp.float32), 'attention_mask': jax.random.randint(ks[2], (B, P), 0, 2, jnp.int32), 'q_w': s * jax.random.normal(ks[3], (H, H), jnp.float32), 'q_b': jnp.zeros((H,), jnp.float32), 'kv_w': s * jax.random.normal(ks[4], (H, 2 * H), jnp.float32), 'kv_b': jnp.zeros((2 * H,), jnp.float32), 'out_w': s * jax.random.normal(ks[5], (H, H), jnp.float32), 'out_b': jnp.zeros((H,), jnp.float32), 'postnorm_w': jnp.ones((H,), jnp.float32), 'mlp_w1': s * jax.random.normal(ks[6], (H, 4 * H), jnp.float32), 'mlp_b1': jnp.zeros((4 * H,), jnp.float32), 'mlp_w2': s * jax.random.normal(ks[7], (4 * H, H), jnp.float32), 'mlp_b2': jnp.zeros((H,), jnp.float32)}
    _L1_xattn_all = _L1_xattn_setup()
    _L1_xattn_in = {k: v for k, v in _L1_xattn_all.items() if k in ('q_w', 'q_b', 'kv_w', 'kv_b', 'out_w', 'out_b', 'postnorm_w', 'mlp_w1', 'mlp_b1', 'mlp_w2', 'mlp_b2')}
    del _L1_xattn_all

    def _L2_xattn_setup():
        import jax, jax.numpy as jnp
        import numpy as np
        H = 256
        NH = 16
        HD = H // NH
        EPS = 1e-05

        def gelu(x):
            return 0.5 * x * (1.0 + jnp.tanh(0.7978845608028654 * x * (1.0 + 0.044715 * x * x)))

        def layernorm(x, scale, bias):
            m = jnp.mean(x, axis=-1, keepdims=True)
            v = jnp.mean(jnp.square(x - m), axis=-1, keepdims=True)
            return (x - m) * jax.lax.rsqrt(v + EPS) * scale + bias

        def split_heads(x):
            b, s, _ = x.shape
            return x.reshape(b, s, NH, HD).transpose(0, 2, 1, 3)

        def merge_heads(x):
            b, nh, s, hd = x.shape
            return x.transpose(0, 2, 1, 3).reshape(b, s, nh * hd)

        def attention(q, k, v, mask):
            scores = jnp.einsum('bhqd,bhkd->bhqk', q, k) / jnp.sqrt(jnp.float32(HD))
            scores = scores * mask - 10000.0 * (1.0 - mask)
            probs = jax.nn.softmax(scores, axis=-1)
            return jnp.einsum('bhqk,bhkd->bhqd', probs, v)
        key = jax.random.key(seed)
        ks = jax.random.split(key, 16)
        b, s, t = (2, 128, 128)
        w = lambda k, i, o: jax.random.normal(k, (i, o), jnp.float32) * 0.02
        inp = {'hidden_states': jax.random.normal(ks[0], (b, s, H), jnp.float32), 'encoder_states': jax.random.normal(ks[1], (b, t, H), jnp.float32), 'ltor_mask': jnp.tril(jnp.ones((1, 1, s, s), jnp.float32)), 'cross_mask': jnp.ones((b, 1, s, t), jnp.float32), 'ln1_s': jnp.ones((H,), jnp.float32), 'ln1_b': jnp.zeros((H,), jnp.float32), 'w_qkv': w(ks[2], H, 3 * H), 'b_qkv': jnp.zeros((3 * H,), jnp.float32), 'w_ao': w(ks[3], H, H), 'b_ao': jnp.zeros((H,), jnp.float32), 'ln2_s': jnp.ones((H,), jnp.float32), 'ln2_b': jnp.zeros((H,), jnp.float32), 'w_q': w(ks[4], H, H), 'b_q': jnp.zeros((H,), jnp.float32), 'w_kv': w(ks[5], H, 2 * H), 'b_kv': jnp.zeros((2 * H,), jnp.float32), 'w_co': w(ks[6], H, H), 'b_co': jnp.zeros((H,), jnp.float32), 'ln3_s': jnp.ones((H,), jnp.float32), 'ln3_b': jnp.zeros((H,), jnp.float32), 'w1': w(ks[7], H, 4 * H), 'b1': jnp.zeros((4 * H,), jnp.float32), 'w2': w(ks[8], 4 * H, H), 'b2': jnp.zeros((H,), jnp.float32)}
        return inp
    _L2_xattn_all = _L2_xattn_setup()
    _L2_xattn_in = {k: v for k, v in _L2_xattn_all.items() if k in ('ln1_s', 'ln1_b', 'w_qkv', 'b_qkv', 'w_ao', 'b_ao', 'ln2_s', 'ln2_b', 'w_q', 'b_q', 'w_kv', 'b_kv', 'w_co', 'b_co', 'ln3_s', 'ln3_b', 'w1', 'b1', 'w2', 'b2')}
    del _L2_xattn_all

    def _L3_xattn_setup():
        import jax, jax.numpy as jnp
        import numpy as np
        N_HEAD = 32
        EPS = 1e-05

        def _ln(x, w, b):
            m = jnp.mean(x, axis=-1, keepdims=True)
            v = jnp.mean((x - m) ** 2, axis=-1, keepdims=True)
            return (x - m) * jax.lax.rsqrt(v + EPS) * w + b

        def _forward(x, state, i, ln1_w, ln1_b, ln2_w, ln2_b, maa_x, maa_w, maa_k, maa_v, maa_r, maa_g, maa_w1, maa_w2, time_decay, decay_w1, decay_w2, faaaa, Wr, Wk, Wv, Wg, Wo, gn_w, gn_b, fmaa_k, fmaa_r, fWk, fWr, fWv):
            B, L, C = x.shape
            H = N_HEAD
            S = C // H
            i0 = (2 + S) * i
            xa = _ln(x, ln1_w, ln1_b)
            sx = jnp.concatenate([state[:, i0 + 1][:, None], xa[:, :-1]], axis=1) - xa
            xxx = xa + sx * maa_x
            t = jnp.tanh(xxx @ maa_w1).reshape(B, L, 5, -1)
            m = jnp.einsum('blfd,fdc->blfc', t, maa_w2)
            mw, mk, mv, mr, mg = (m[:, :, j] for j in range(5))
            xw = xa + sx * (maa_w + mw)
            xk = xa + sx * (maa_k + mk)
            xv = xa + sx * (maa_v + mv)
            xr = xa + sx * (maa_r + mr)
            xg = xa + sx * (maa_g + mg)
            w = time_decay + jnp.tanh(xw @ decay_w1) @ decay_w2
            w = jnp.exp(-jnp.exp(w)).reshape(B, L, H, S)
            r = (xr @ Wr.T).reshape(B, L, H, S)
            k = (xk @ Wk.T).reshape(B, L, H, S)
            v = (xv @ Wv.T).reshape(B, L, H, S)
            g = jax.nn.silu(xg @ Wg.T)
            s0 = state[:, i0 + 2:i0 + 2 + S].reshape(B, H, S, S)

            def step(s, inp):
                k_l, v_l, w_l, r_l = inp
                a = k_l[..., :, None] * v_l[..., None, :]
                out = jnp.einsum('bhs,bhst->bht', r_l, faaaa * a + s)
                s_new = a + w_l[..., None] * s
                return (s_new, out)
            seq = tuple((z.transpose(1, 0, 2, 3) for z in (k, v, w, r)))
            _, outs = jax.lax.scan(step, s0, seq)
            y = outs.transpose(1, 0, 2, 3)
            gm = jnp.mean(y, axis=-1, keepdims=True)
            gv = jnp.mean((y - gm) ** 2, axis=-1, keepdims=True)
            y = ((y - gm) * jax.lax.rsqrt(gv + EPS)).reshape(B, L, C) * gn_w + gn_b
            x = x + y * g @ Wo.T
            xc = _ln(x, ln2_w, ln2_b)
            sxc = jnp.concatenate([state[:, i0][:, None], xc[:, :-1]], axis=1) - xc
            xk2 = xc + sxc * fmaa_k
            xr2 = xc + sxc * fmaa_r
            rr = jax.nn.sigmoid(xr2 @ fWr.T)
            kk = jnp.square(jax.nn.relu(xk2 @ fWk.T))
            x = x + rr * (kk @ fWv.T)
            return x
        key = jax.random.key(seed)
        B, L, C, H = (8, 64, 256, N_HEAD)
        S = C // H
        DM, DD = (32, 64)
        ks = jax.random.split(key, 32)
        n = lambda k, shp, s=1.0: jax.random.normal(k, shp, dtype=jnp.float32) * s
        u = lambda k, shp: jax.random.uniform(k, shp, dtype=jnp.float32)
        inp = {'x': n(ks[0], (B, L, C)), 'state': n(ks[1], (B, 2 + S, C), 0.1), 'i': 0, 'ln1_w': jnp.ones((C,), jnp.float32), 'ln1_b': jnp.zeros((C,), jnp.float32), 'ln2_w': jnp.ones((C,), jnp.float32), 'ln2_b': jnp.zeros((C,), jnp.float32), 'maa_x': u(ks[2], (C,)), 'maa_w': u(ks[3], (C,)), 'maa_k': u(ks[4], (C,)), 'maa_v': u(ks[5], (C,)), 'maa_r': u(ks[6], (C,)), 'maa_g': u(ks[7], (C,)), 'maa_w1': n(ks[8], (C, 5 * DM), 0.02), 'maa_w2': n(ks[9], (5, DM, C), 0.02), 'time_decay': n(ks[10], (C,), 0.5), 'decay_w1': n(ks[11], (C, DD), 0.02), 'decay_w2': n(ks[12], (DD, C), 0.02), 'faaaa': n(ks[13], (H, S, 1), 0.1), 'Wr': n(ks[14], (C, C), 0.02), 'Wk': n(ks[15], (C, C), 0.02), 'Wv': n(ks[16], (C, C), 0.02), 'Wg': n(ks[17], (C, C), 0.02), 'Wo': n(ks[18], (C, C), 0.02), 'gn_w': jnp.ones((C,), jnp.float32), 'gn_b': jnp.zeros((C,), jnp.float32), 'fmaa_k': u(ks[19], (C,)), 'fmaa_r': u(ks[20], (C,)), 'fWk': n(ks[21], (C, C), 0.02), 'fWr': n(ks[22], (C, C), 0.02), 'fWv': n(ks[23], (C, C), 0.02)}
        return inp
    _L3_xattn_all = _L3_xattn_setup()
    _L3_xattn_in = {k: v for k, v in _L3_xattn_all.items() if k in ('ln1_w', 'ln1_b', 'ln2_w', 'ln2_b', 'maa_x', 'maa_w', 'maa_k', 'maa_v', 'maa_r', 'maa_g', 'maa_w1', 'maa_w2', 'time_decay', 'decay_w1', 'decay_w2', 'faaaa', 'Wr', 'Wk', 'Wv', 'Wg', 'Wo', 'gn_w', 'gn_b', 'fmaa_k', 'fmaa_r', 'fWk', 'fWr', 'fWv')}
    del _L3_xattn_all
    return {'x': x, 'ctx_2048': ctx_2048, 'mask_BxS2_ik0': mask_BxS2_ik0, 'mask_1x1xSxS2_fc1': mask_1x1xSxS2_fc1, 'mask_Bx1xSxS2_ff1': mask_Bx1xSxS2_ff1, 'L0_xattn_ln1_w': _L0_xattn_in['ln1_w'], 'L0_xattn_ln1_b': _L0_xattn_in['ln1_b'], 'L0_xattn_ln2_w': _L0_xattn_in['ln2_w'], 'L0_xattn_ln2_b': _L0_xattn_in['ln2_b'], 'L0_xattn_maa_x': _L0_xattn_in['maa_x'], 'L0_xattn_maa_w1': _L0_xattn_in['maa_w1'], 'L0_xattn_maa_w2': _L0_xattn_in['maa_w2'], 'L0_xattn_maa_stack': _L0_xattn_in['maa_stack'], 'L0_xattn_time_decay': _L0_xattn_in['time_decay'], 'L0_xattn_td_w1': _L0_xattn_in['td_w1'], 'L0_xattn_td_w2': _L0_xattn_in['td_w2'], 'L0_xattn_u': _L0_xattn_in['u'], 'L0_xattn_Wr': _L0_xattn_in['Wr'], 'L0_xattn_Wk': _L0_xattn_in['Wk'], 'L0_xattn_Wv': _L0_xattn_in['Wv'], 'L0_xattn_Wg': _L0_xattn_in['Wg'], 'L0_xattn_Wo': _L0_xattn_in['Wo'], 'L0_xattn_gn_w': _L0_xattn_in['gn_w'], 'L0_xattn_gn_b': _L0_xattn_in['gn_b'], 'L0_xattn_ffn_maa_k': _L0_xattn_in['ffn_maa_k'], 'L0_xattn_ffn_maa_r': _L0_xattn_in['ffn_maa_r'], 'L0_xattn_Wfk': _L0_xattn_in['Wfk'], 'L0_xattn_Wfr': _L0_xattn_in['Wfr'], 'L0_xattn_Wfv': _L0_xattn_in['Wfv'], 'L1_xattn_q_w': _L1_xattn_in['q_w'], 'L1_xattn_q_b': _L1_xattn_in['q_b'], 'L1_xattn_kv_w': _L1_xattn_in['kv_w'], 'L1_xattn_kv_b': _L1_xattn_in['kv_b'], 'L1_xattn_out_w': _L1_xattn_in['out_w'], 'L1_xattn_out_b': _L1_xattn_in['out_b'], 'L1_xattn_postnorm_w': _L1_xattn_in['postnorm_w'], 'L1_xattn_mlp_w1': _L1_xattn_in['mlp_w1'], 'L1_xattn_mlp_b1': _L1_xattn_in['mlp_b1'], 'L1_xattn_mlp_w2': _L1_xattn_in['mlp_w2'], 'L1_xattn_mlp_b2': _L1_xattn_in['mlp_b2'], 'L2_xattn_ln1_s': _L2_xattn_in['ln1_s'], 'L2_xattn_ln1_b': _L2_xattn_in['ln1_b'], 'L2_xattn_w_qkv': _L2_xattn_in['w_qkv'], 'L2_xattn_b_qkv': _L2_xattn_in['b_qkv'], 'L2_xattn_w_ao': _L2_xattn_in['w_ao'], 'L2_xattn_b_ao': _L2_xattn_in['b_ao'], 'L2_xattn_ln2_s': _L2_xattn_in['ln2_s'], 'L2_xattn_ln2_b': _L2_xattn_in['ln2_b'], 'L2_xattn_w_q': _L2_xattn_in['w_q'], 'L2_xattn_b_q': _L2_xattn_in['b_q'], 'L2_xattn_w_kv': _L2_xattn_in['w_kv'], 'L2_xattn_b_kv': _L2_xattn_in['b_kv'], 'L2_xattn_w_co': _L2_xattn_in['w_co'], 'L2_xattn_b_co': _L2_xattn_in['b_co'], 'L2_xattn_ln3_s': _L2_xattn_in['ln3_s'], 'L2_xattn_ln3_b': _L2_xattn_in['ln3_b'], 'L2_xattn_w1': _L2_xattn_in['w1'], 'L2_xattn_b1': _L2_xattn_in['b1'], 'L2_xattn_w2': _L2_xattn_in['w2'], 'L2_xattn_b2': _L2_xattn_in['b2'], 'L3_xattn_ln1_w': _L3_xattn_in['ln1_w'], 'L3_xattn_ln1_b': _L3_xattn_in['ln1_b'], 'L3_xattn_ln2_w': _L3_xattn_in['ln2_w'], 'L3_xattn_ln2_b': _L3_xattn_in['ln2_b'], 'L3_xattn_maa_x': _L3_xattn_in['maa_x'], 'L3_xattn_maa_w': _L3_xattn_in['maa_w'], 'L3_xattn_maa_k': _L3_xattn_in['maa_k'], 'L3_xattn_maa_v': _L3_xattn_in['maa_v'], 'L3_xattn_maa_r': _L3_xattn_in['maa_r'], 'L3_xattn_maa_g': _L3_xattn_in['maa_g'], 'L3_xattn_maa_w1': _L3_xattn_in['maa_w1'], 'L3_xattn_maa_w2': _L3_xattn_in['maa_w2'], 'L3_xattn_time_decay': _L3_xattn_in['time_decay'], 'L3_xattn_decay_w1': _L3_xattn_in['decay_w1'], 'L3_xattn_decay_w2': _L3_xattn_in['decay_w2'], 'L3_xattn_faaaa': _L3_xattn_in['faaaa'], 'L3_xattn_Wr': _L3_xattn_in['Wr'], 'L3_xattn_Wk': _L3_xattn_in['Wk'], 'L3_xattn_Wv': _L3_xattn_in['Wv'], 'L3_xattn_Wg': _L3_xattn_in['Wg'], 'L3_xattn_Wo': _L3_xattn_in['Wo'], 'L3_xattn_gn_w': _L3_xattn_in['gn_w'], 'L3_xattn_gn_b': _L3_xattn_in['gn_b'], 'L3_xattn_fmaa_k': _L3_xattn_in['fmaa_k'], 'L3_xattn_fmaa_r': _L3_xattn_in['fmaa_r'], 'L3_xattn_fWk': _L3_xattn_in['fWk'], 'L3_xattn_fWr': _L3_xattn_in['fWr'], 'L3_xattn_fWv': _L3_xattn_in['fWv']}

def reference(x, ctx_2048, mask_BxS2_ik0, mask_1x1xSxS2_fc1, mask_Bx1xSxS2_ff1, L0_xattn_ln1_w, L0_xattn_ln1_b, L0_xattn_ln2_w, L0_xattn_ln2_b, L0_xattn_maa_x, L0_xattn_maa_w1, L0_xattn_maa_w2, L0_xattn_maa_stack, L0_xattn_time_decay, L0_xattn_td_w1, L0_xattn_td_w2, L0_xattn_u, L0_xattn_Wr, L0_xattn_Wk, L0_xattn_Wv, L0_xattn_Wg, L0_xattn_Wo, L0_xattn_gn_w, L0_xattn_gn_b, L0_xattn_ffn_maa_k, L0_xattn_ffn_maa_r, L0_xattn_Wfk, L0_xattn_Wfr, L0_xattn_Wfv, L1_xattn_q_w, L1_xattn_q_b, L1_xattn_kv_w, L1_xattn_kv_b, L1_xattn_out_w, L1_xattn_out_b, L1_xattn_postnorm_w, L1_xattn_mlp_w1, L1_xattn_mlp_b1, L1_xattn_mlp_w2, L1_xattn_mlp_b2, L2_xattn_ln1_s, L2_xattn_ln1_b, L2_xattn_w_qkv, L2_xattn_b_qkv, L2_xattn_w_ao, L2_xattn_b_ao, L2_xattn_ln2_s, L2_xattn_ln2_b, L2_xattn_w_q, L2_xattn_b_q, L2_xattn_w_kv, L2_xattn_b_kv, L2_xattn_w_co, L2_xattn_b_co, L2_xattn_ln3_s, L2_xattn_ln3_b, L2_xattn_w1, L2_xattn_b1, L2_xattn_w2, L2_xattn_b2, L3_xattn_ln1_w, L3_xattn_ln1_b, L3_xattn_ln2_w, L3_xattn_ln2_b, L3_xattn_maa_x, L3_xattn_maa_w, L3_xattn_maa_k, L3_xattn_maa_v, L3_xattn_maa_r, L3_xattn_maa_g, L3_xattn_maa_w1, L3_xattn_maa_w2, L3_xattn_time_decay, L3_xattn_decay_w1, L3_xattn_decay_w2, L3_xattn_faaaa, L3_xattn_Wr, L3_xattn_Wk, L3_xattn_Wv, L3_xattn_Wg, L3_xattn_Wo, L3_xattn_gn_w, L3_xattn_gn_b, L3_xattn_fmaa_k, L3_xattn_fmaa_r, L3_xattn_fWk, L3_xattn_fWr, L3_xattn_fWv):
    import jax
    import jax.numpy as jnp

    def _L0_xattn_ref(x, state, ln1_w, ln1_b, ln2_w, ln2_b, maa_x, maa_w1, maa_w2, maa_stack, time_decay, td_w1, td_w2, u, Wr, Wk, Wv, Wg, Wo, gn_w, gn_b, ffn_maa_k, ffn_maa_r, Wfk, Wfr, Wfv):
        import jax, jax.numpy as jnp
        import numpy as np
        E, H, L, B = (256, 32, 128, 4)
        S = E // H
        DM, DD = (32, 64)

        def _ln(x, w, b, eps=1e-05):
            m = x.mean(-1, keepdims=True)
            v = ((x - m) ** 2).mean(-1, keepdims=True)
            return (x - m) / jnp.sqrt(v + eps) * w + b

        def _block(x, state, ln1_w, ln1_b, ln2_w, ln2_b, maa_x, maa_w1, maa_w2, maa_stack, time_decay, td_w1, td_w2, u, Wr, Wk, Wv, Wg, Wo, gn_w, gn_b, ffn_maa_k, ffn_maa_r, Wfk, Wfr, Wfv):
            b, l, e = x.shape
            h = u.shape[0]
            s_ = e // h
            xa = _ln(x, ln1_w, ln1_b)
            sx = jnp.concatenate([state[:, 1:2] - xa[:, :1], xa[:, :-1] - xa[:, 1:]], axis=1)
            xxx = jnp.tanh((xa + sx * maa_x) @ maa_w1).reshape(b, l, 5, DM)
            xxx = jnp.einsum('blfd,fde->blfe', xxx, maa_w2)
            xm = xa[:, :, None] + sx[:, :, None] * (maa_stack + xxx)
            xk, xw, xv, xr, xg = (xm[:, :, j] for j in range(5))
            w = jnp.exp(-jnp.exp(time_decay + jnp.tanh(xw @ td_w1) @ td_w2)).reshape(b, l, h, s_)
            r = (xr @ Wr.T).reshape(b, l, h, s_)
            k = (xk @ Wk.T).reshape(b, l, h, s_)
            v = (xv @ Wv.T).reshape(b, l, h, s_)
            g = jax.nn.silu(xg @ Wg.T)
            s0 = state[:, 2:2 + s_].reshape(b, h, s_, s_)

            def step(s, rkvw):
                r_t, k_t, v_t, w_t = rkvw
                a = k_t[..., :, None] * v_t[..., None, :]
                out = jnp.einsum('bhi,bhij->bhj', r_t, u * a + s)
                s = a + w_t[..., :, None] * s
                return (s, out)
            rkvw = tuple((jnp.moveaxis(t, 1, 0) for t in (r, k, v, w)))
            _, out = jax.lax.scan(step, s0, rkvw)
            out = jnp.moveaxis(out, 0, 1).reshape(b, l, e)
            og = out.reshape(b, l, h, s_)
            m = og.mean(-1, keepdims=True)
            va = ((og - m) ** 2).mean(-1, keepdims=True)
            og = ((og - m) / jnp.sqrt(va + 1e-05)).reshape(b, l, e) * gn_w + gn_b
            x1 = x + og * g @ Wo.T
            xc = _ln(x1, ln2_w, ln2_b)
            sx2 = jnp.concatenate([state[:, 0:1] - xc[:, :1], xc[:, :-1] - xc[:, 1:]], axis=1)
            xk2 = xc + sx2 * ffn_maa_k
            xr2 = xc + sx2 * ffn_maa_r
            rr = jax.nn.sigmoid(xr2 @ Wfr.T)
            kk = jnp.square(jax.nn.relu(xk2 @ Wfk.T))
            return x1 + rr * (kk @ Wfv.T)
        return _block(x, state, ln1_w, ln1_b, ln2_w, ln2_b, maa_x, maa_w1, maa_w2, maa_stack, time_decay, td_w1, td_w2, u, Wr, Wk, Wv, Wg, Wo, gn_w, gn_b, ffn_maa_k, ffn_maa_r, Wfk, Wfr, Wfv)

    def _L1_xattn_ref(x, latents, attention_mask, q_w, q_b, kv_w, kv_b, out_w, out_b, postnorm_w, mlp_w1, mlp_b1, mlp_w2, mlp_b2):
        import jax, jax.numpy as jnp
        import numpy as np
        B, P, K, H, NH = (4, 256, 32, 256, 16)
        DH = H // NH
        EPS = 1e-06

        def rmsnorm(x, w):
            var = jnp.mean(jnp.square(x), axis=-1, keepdims=True)
            return x * jax.lax.rsqrt(var + EPS) * w
        b, p, _ = x.shape
        k_len = latents.shape[1]
        residual = latents
        h = jnp.concatenate([x, latents], axis=1)
        q = (latents @ q_w + q_b).reshape(b, k_len, NH, DH)
        kv = (h @ kv_w + kv_b).reshape(b, p + k_len, NH, DH, 2)
        kmat, v = (kv[..., 0], kv[..., 1])
        attn = jnp.einsum('bkhd,bnhd->bhkn', q, kmat) / DH
        full_mask = jnp.concatenate([attention_mask.astype(bool), jnp.ones((b, k_len), bool)], axis=-1)
        attn = jnp.where(full_mask[:, None, None, :], attn, -jnp.inf)
        attn = jax.nn.softmax(attn.astype(jnp.float32), axis=-1).astype(q.dtype)
        attn_out = jnp.einsum('bhkn,bnhd->bkhd', attn, v).reshape(b, k_len, H)
        attn_out = attn_out @ out_w + out_b + residual
        out = rmsnorm(attn_out, postnorm_w)
        out = jax.nn.gelu(out @ mlp_w1 + mlp_b1) @ mlp_w2 + mlp_b2
        return out + residual

    def _L2_xattn_ref(hidden_states, encoder_states, ltor_mask, cross_mask, ln1_s, ln1_b, w_qkv, b_qkv, w_ao, b_ao, ln2_s, ln2_b, w_q, b_q, w_kv, b_kv, w_co, b_co, ln3_s, ln3_b, w1, b1, w2, b2):
        import jax, jax.numpy as jnp
        import numpy as np
        H = 256
        NH = 16
        HD = H // NH
        EPS = 1e-05

        def gelu(x):
            return 0.5 * x * (1.0 + jnp.tanh(0.7978845608028654 * x * (1.0 + 0.044715 * x * x)))

        def layernorm(x, scale, bias):
            m = jnp.mean(x, axis=-1, keepdims=True)
            v = jnp.mean(jnp.square(x - m), axis=-1, keepdims=True)
            return (x - m) * jax.lax.rsqrt(v + EPS) * scale + bias

        def split_heads(x):
            b, s, _ = x.shape
            return x.reshape(b, s, NH, HD).transpose(0, 2, 1, 3)

        def merge_heads(x):
            b, nh, s, hd = x.shape
            return x.transpose(0, 2, 1, 3).reshape(b, s, nh * hd)

        def attention(q, k, v, mask):
            scores = jnp.einsum('bhqd,bhkd->bhqk', q, k) / jnp.sqrt(jnp.float32(HD))
            scores = scores * mask - 10000.0 * (1.0 - mask)
            probs = jax.nn.softmax(scores, axis=-1)
            return jnp.einsum('bhqk,bhkd->bhqd', probs, v)
        ln_out = layernorm(hidden_states, ln1_s, ln1_b)
        qkv = ln_out @ w_qkv + b_qkv
        q, k, v = jnp.split(qkv, 3, axis=-1)
        ctx = merge_heads(attention(split_heads(q), split_heads(k), split_heads(v), ltor_mask))
        attn_out = ctx @ w_ao + b_ao
        x = hidden_states + attn_out
        ln_out = layernorm(x, ln2_s, ln2_b)
        q = ln_out @ w_q + b_q
        kv = encoder_states @ w_kv + b_kv
        k, v = jnp.split(kv, 2, axis=-1)
        ctx = merge_heads(attention(split_heads(q), split_heads(k), split_heads(v), cross_mask))
        cross_out = ctx @ w_co + b_co
        x = x + cross_out
        ln_out = layernorm(x, ln3_s, ln3_b)
        mlp_out = gelu(ln_out @ w1 + b1) @ w2 + b2
        return x + mlp_out

    def _L3_xattn_ref(x, state, i, ln1_w, ln1_b, ln2_w, ln2_b, maa_x, maa_w, maa_k, maa_v, maa_r, maa_g, maa_w1, maa_w2, time_decay, decay_w1, decay_w2, faaaa, Wr, Wk, Wv, Wg, Wo, gn_w, gn_b, fmaa_k, fmaa_r, fWk, fWr, fWv):
        import jax, jax.numpy as jnp
        import numpy as np
        N_HEAD = 32
        EPS = 1e-05

        def _ln(x, w, b):
            m = jnp.mean(x, axis=-1, keepdims=True)
            v = jnp.mean((x - m) ** 2, axis=-1, keepdims=True)
            return (x - m) * jax.lax.rsqrt(v + EPS) * w + b

        def _forward(x, state, i, ln1_w, ln1_b, ln2_w, ln2_b, maa_x, maa_w, maa_k, maa_v, maa_r, maa_g, maa_w1, maa_w2, time_decay, decay_w1, decay_w2, faaaa, Wr, Wk, Wv, Wg, Wo, gn_w, gn_b, fmaa_k, fmaa_r, fWk, fWr, fWv):
            B, L, C = x.shape
            H = N_HEAD
            S = C // H
            i0 = (2 + S) * i
            xa = _ln(x, ln1_w, ln1_b)
            sx = jnp.concatenate([state[:, i0 + 1][:, None], xa[:, :-1]], axis=1) - xa
            xxx = xa + sx * maa_x
            t = jnp.tanh(xxx @ maa_w1).reshape(B, L, 5, -1)
            m = jnp.einsum('blfd,fdc->blfc', t, maa_w2)
            mw, mk, mv, mr, mg = (m[:, :, j] for j in range(5))
            xw = xa + sx * (maa_w + mw)
            xk = xa + sx * (maa_k + mk)
            xv = xa + sx * (maa_v + mv)
            xr = xa + sx * (maa_r + mr)
            xg = xa + sx * (maa_g + mg)
            w = time_decay + jnp.tanh(xw @ decay_w1) @ decay_w2
            w = jnp.exp(-jnp.exp(w)).reshape(B, L, H, S)
            r = (xr @ Wr.T).reshape(B, L, H, S)
            k = (xk @ Wk.T).reshape(B, L, H, S)
            v = (xv @ Wv.T).reshape(B, L, H, S)
            g = jax.nn.silu(xg @ Wg.T)
            s0 = state[:, i0 + 2:i0 + 2 + S].reshape(B, H, S, S)

            def step(s, inp):
                k_l, v_l, w_l, r_l = inp
                a = k_l[..., :, None] * v_l[..., None, :]
                out = jnp.einsum('bhs,bhst->bht', r_l, faaaa * a + s)
                s_new = a + w_l[..., None] * s
                return (s_new, out)
            seq = tuple((z.transpose(1, 0, 2, 3) for z in (k, v, w, r)))
            _, outs = jax.lax.scan(step, s0, seq)
            y = outs.transpose(1, 0, 2, 3)
            gm = jnp.mean(y, axis=-1, keepdims=True)
            gv = jnp.mean((y - gm) ** 2, axis=-1, keepdims=True)
            y = ((y - gm) * jax.lax.rsqrt(gv + EPS)).reshape(B, L, C) * gn_w + gn_b
            x = x + y * g @ Wo.T
            xc = _ln(x, ln2_w, ln2_b)
            sxc = jnp.concatenate([state[:, i0][:, None], xc[:, :-1]], axis=1) - xc
            xk2 = xc + sxc * fmaa_k
            xr2 = xc + sxc * fmaa_r
            rr = jax.nn.sigmoid(xr2 @ fWr.T)
            kk = jnp.square(jax.nn.relu(xk2 @ fWk.T))
            x = x + rr * (kk @ fWv.T)
            return x
        return _forward(x, state, i, ln1_w, ln1_b, ln2_w, ln2_b, maa_x, maa_w, maa_k, maa_v, maa_r, maa_g, maa_w1, maa_w2, time_decay, decay_w1, decay_w2, faaaa, Wr, Wk, Wv, Wg, Wo, gn_w, gn_b, fmaa_k, fmaa_r, fWk, fWr, fWv)
    x = _L0_xattn_ref(x, ctx_2048, L0_xattn_ln1_w, L0_xattn_ln1_b, L0_xattn_ln2_w, L0_xattn_ln2_b, L0_xattn_maa_x, L0_xattn_maa_w1, L0_xattn_maa_w2, L0_xattn_maa_stack, L0_xattn_time_decay, L0_xattn_td_w1, L0_xattn_td_w2, L0_xattn_u, L0_xattn_Wr, L0_xattn_Wk, L0_xattn_Wv, L0_xattn_Wg, L0_xattn_Wo, L0_xattn_gn_w, L0_xattn_gn_b, L0_xattn_ffn_maa_k, L0_xattn_ffn_maa_r, L0_xattn_Wfk, L0_xattn_Wfr, L0_xattn_Wfv)
    x = _L1_xattn_ref(ctx_2048, x, mask_BxS2_ik0, L1_xattn_q_w, L1_xattn_q_b, L1_xattn_kv_w, L1_xattn_kv_b, L1_xattn_out_w, L1_xattn_out_b, L1_xattn_postnorm_w, L1_xattn_mlp_w1, L1_xattn_mlp_b1, L1_xattn_mlp_w2, L1_xattn_mlp_b2)
    x = _L2_xattn_ref(x, ctx_2048, mask_1x1xSxS2_fc1, mask_Bx1xSxS2_ff1, L2_xattn_ln1_s, L2_xattn_ln1_b, L2_xattn_w_qkv, L2_xattn_b_qkv, L2_xattn_w_ao, L2_xattn_b_ao, L2_xattn_ln2_s, L2_xattn_ln2_b, L2_xattn_w_q, L2_xattn_b_q, L2_xattn_w_kv, L2_xattn_b_kv, L2_xattn_w_co, L2_xattn_b_co, L2_xattn_ln3_s, L2_xattn_ln3_b, L2_xattn_w1, L2_xattn_b1, L2_xattn_w2, L2_xattn_b2)
    x = _L3_xattn_ref(x, ctx_2048, 0, L3_xattn_ln1_w, L3_xattn_ln1_b, L3_xattn_ln2_w, L3_xattn_ln2_b, L3_xattn_maa_x, L3_xattn_maa_w, L3_xattn_maa_k, L3_xattn_maa_v, L3_xattn_maa_r, L3_xattn_maa_g, L3_xattn_maa_w1, L3_xattn_maa_w2, L3_xattn_time_decay, L3_xattn_decay_w1, L3_xattn_decay_w2, L3_xattn_faaaa, L3_xattn_Wr, L3_xattn_Wk, L3_xattn_Wv, L3_xattn_Wg, L3_xattn_Wo, L3_xattn_gn_w, L3_xattn_gn_b, L3_xattn_fmaa_k, L3_xattn_fmaa_r, L3_xattn_fWk, L3_xattn_fWr, L3_xattn_fWv)
    return x

_drawn_inputs = setup_inputs


def setup_inputs(seed=0):
    import zlib

    import numpy as np

    out = dict(_drawn_inputs(seed))
    spreads = {'L0_xattn_ln1_w': (1.0, 0.563),
     'L0_xattn_ln1_b': (0.0, 0.569),
     'L0_xattn_ln2_w': (1.0, 0.6),
     'L0_xattn_ln2_b': (0.0, 0.8),
     'L0_xattn_gn_w': (1.0, 0.6),
     'L0_xattn_gn_b': (0.0, 0.8),
     'L1_xattn_q_b': (0.0, 0.8),
     'L1_xattn_kv_b': (0.0, 2.0),
     'L1_xattn_out_b': (0.0, 2.0),
     'L1_xattn_postnorm_w': (1.0, 0.6),
     'L1_xattn_mlp_b1': (0.0, 0.385),
     'L1_xattn_mlp_b2': (0.0, 0.1),
     'L2_xattn_ln1_s': (1.0, 0.6),
     'L2_xattn_ln1_b': (0.0, 0.8),
     'L2_xattn_b_qkv': (0.0, 0.273),
     'L2_xattn_b_ao': (0.0, 0.1),
     'L2_xattn_ln2_s': (1.0, 0.6),
     'L2_xattn_ln2_b': (0.0, 0.8),
     'L2_xattn_b_q': (0.0, 0.8),
     'L2_xattn_b_kv': (0.0, 0.8),
     'L2_xattn_b_co': (0.0, 0.355),
     'L2_xattn_ln3_s': (1.0, 0.6),
     'L2_xattn_ln3_b': (0.0, 0.647),
     'L2_xattn_b1': (0.0, 0.473),
     'L2_xattn_b2': (0.0, 0.352),
     'L3_xattn_ln1_w': (1.0, 0.6),
     'L3_xattn_ln1_b': (0.0, 0.549),
     'L3_xattn_ln2_w': (1.0, 0.6),
     'L3_xattn_ln2_b': (0.0, 0.8),
     'L3_xattn_gn_w': (1.0, 0.6),
     'L3_xattn_gn_b': (0.0, 0.8)}
    factors = {'ctx_2048': 6.327,
     'L0_xattn_maa_x': 8.0,
     'L0_xattn_maa_w1': 6.97,
     'L0_xattn_maa_w2': 6.966,
     'L0_xattn_maa_stack': 2.692,
     'L0_xattn_time_decay': 2.781,
     'L0_xattn_td_w1': 8.0,
     'L0_xattn_td_w2': 8.0,
     'L0_xattn_u': 5.458,
     'L0_xattn_ffn_maa_k': 8.0,
     'L0_xattn_ffn_maa_r': 8.0,
     'L0_xattn_Wfk': 3.026,
     'L0_xattn_Wfr': 8.0,
     'L0_xattn_Wfv': 2.802,
     'L1_xattn_q_w': 8.0,
     'L1_xattn_kv_w': 8.0,
     'L1_xattn_out_w': 8.0,
     'L2_xattn_w_qkv': 3.146,
     'L2_xattn_w_q': 8.0,
     'L2_xattn_w_kv': 8.0,
     'L3_xattn_maa_x': 8.0,
     'L3_xattn_maa_w': 8.0,
     'L3_xattn_maa_w1': 8.0,
     'L3_xattn_maa_w2': 8.0,
     'L3_xattn_time_decay': 3.632,
     'L3_xattn_decay_w1': 8.0,
     'L3_xattn_decay_w2': 8.0,
     'L3_xattn_faaaa': 6.918,
     'L3_xattn_fmaa_k': 6.976,
     'L3_xattn_fmaa_r': 8.0,
     'L3_xattn_fWk': 4.004,
     'L3_xattn_fWr': 8.0,
     'L3_xattn_fWv': 3.652}
    for name, (base, spread) in spreads.items():
        noise = np.random.default_rng([zlib.crc32(name.encode()), seed]).standard_normal(out[name].shape)
        drawn = base * np.exp(spread * noise) if base else spread * noise
        out[name] = jnp.asarray(drawn.astype(out[name].dtype))
    for name, factor in factors.items():
        out[name] = (out[name] * factor).astype(out[name].dtype)
    return out
```

```python
from contextlib import ExitStack

import numpy as np

import concourse.bass as bass
from concourse import mybir

F32 = mybir.dt.float32
I32 = mybir.dt.int32
ALU = mybir.AluOpType
ACT = mybir.ActivationFunctionType
AX = mybir.AxisListType

P = 128
B, T, C = 16, 128, 256
NC_ = C // P
GB = 2
N = GB * T
GROUPS = B // GB
S8 = 8
NH, HD = 16, 16
HID = 4 * C
SLOT = 32
TQ = NH * SLOT // P
BLK = N // 4
MASKED = -1e30



def _columns(fields):
    at, out = 0, {}
    for name, width in fields:
        out[name] = (at, width)
        at += width
    return out, at


CONST, CONST_W = _columns([
    ("mean", P), ("spread_ln", P), ("sel", S8 * P), ("red", S8 * P), ("head_sum", P), ("head_mean", P),
    ("narrow_gn", 2 * SLOT), ("spread_gn", 2 * P), ("narrow_sm", TQ * SLOT), ("spread_sm", TQ * P),
    ("ident", P), ("block", 4), ("maskrow", P), ("eps5", 1), ("eps6", 1), ("even", 1), ("odd", 1)])
LIN = NC_ * C
RWKV, RWKV_W = _columns(
    [("w1", NC_ * 160), ("w2", C), ("w2b", C), ("td1", NC_ * 64), ("td2", C)]
    + [(w, LIN) for w in ("Wr", "Wk", "Wv", "Wg", "Wo", "Fk", "Fr", "Fv")]
    + [(v, NC_) for v in ("ln1_w", "ln1_b", "ln2_w", "ln2_b", "maa_x", "td", "u", "gn_w", "gn_b", "fk", "fr")]
    + [("maa", 5 * NC_)])
PERC, PERC_W = _columns([
    ("q", NC_ * TQ * P), ("k", NC_ * TQ * P), ("v", LIN), ("o", TQ * C), ("m1", NC_ * HID), ("m2", HID // P * C),
    ("qb", TQ), ("kb", TQ), ("vb", C), ("ob", NC_), ("norm_w", NC_), ("b1", HID // P), ("b2", NC_)])
DEC, DEC_W = _columns(
    [(f"{w}{a}", LIN) for a in (0, 1) for w in "qkv"] + [(f"o{a}", TQ * C) for a in (0, 1)]
    + [("m1", NC_ * HID), ("m2", HID // P * C)]
    + [(f"{w}b{a}", NC_) for a in (0, 1) for w in "qko"] + [(f"vb{a}", C) for a in (0, 1)]
    + [(f"ln{n}_{x}", NC_) for n in (1, 2, 3) for x in "wb"] + [("b1", HID // P), ("b2", NC_)])
ORDER = (("k", "w", "v", "r", "g"), ("w", "k", "v", "r", "g"))


def _constants():
    p = np.arange(P)[:, None]
    m = np.arange(P)[None, :]
    s = np.arange(SLOT)[None, :]
    part = {
        "mean": np.full((P, P), 1.0 / C),
        "spread_ln": np.full((P, P), 1.0 / SLOT),
        "sel": np.concatenate([p == S8 * (m // S8) + j for j in range(S8)], 1),
        "red": np.concatenate([m == S8 * (p // S8) + j for j in range(S8)], 1),
        "head_sum": p // S8 == m // S8,
        "head_mean": (p // S8 == m // S8) / S8,
        "narrow_gn": np.concatenate([(s == P // S8 * c + p // S8) / S8 for c in range(2)], 1),
        "spread_gn": np.concatenate([p % SLOT == P // S8 * c + m // S8 for c in range(2)], 1),
        "narrow_sm": np.concatenate([(p % SLOT == HD) & (s % NH == 4 * t + p // SLOT) for t in range(TQ)], 1),
        "spread_sm": np.concatenate([p % SLOT == 4 * t + m // SLOT for t in range(TQ)], 1),
        "ident": p == m,
        "block": p // SLOT == np.arange(4)[None, :],
        "maskrow": np.broadcast_to(m % SLOT == HD, (P, P)),
        "eps5": np.full((P, 1), 1e-5), "eps6": np.full((P, 1), 1e-6),
        "even": (p // HD % 2 == 0) / 4.0, "odd": (p // HD % 2 == 1) / 4.0,
    }
    return np.concatenate([np.asarray(part[k], np.float32) for k in CONST], 1)




def psum_tiles():

    def norm(i, mean=True):
        if mean:
            yield f"mean{i}", 1, "V"
        yield f"var{i}", 1, "A"
        yield f"scale{i}", 1, "V"

    def rwkv(l, i):
        yield from norm(i)
        yield f"mix{l}", 1, "A"
        for f in range(5):
            yield f"maa{l}.{f}", 1, "V"
        yield f"td1.{l}", 1, "A"
        yield f"td2.{l}", 1, "A"
        for x in "kvr":
            yield f"{x}{l}", 1, "A"
        yield f"g{l}", 1, "V"
        yield f"bonus{l}", 1, "V"
        for c in range(2):
            for j in range(0, S8, 2):
                yield f"vb{l}.{c}.{j}", 1, "V"
        yield f"y{l}", 1, "V"
        yield f"gmean{l}", 1, "V"
        yield f"gvar{l}", 1, "A"
        yield f"gscale{l}", 1, "V"
        yield f"wo{l}", 1, "V"
        yield from norm(i + 1)
        yield f"fr{l}", 1, "A"
        yield f"fk{l}", 1, "A"
        yield f"fv{l}", 1, "V"

    def softmax(a):
        yield f"den{a}", 1, "V"
        for h in range(2):
            yield f"inv{a}.{h}", 1, "V"
        yield f"o{a}", 1, "V"

    def mlp(m):
        for n in range(HID // P // 2):
            yield f"hid{m}.{n}", 1, "A"
        yield f"down{m}", 1, "V"

    yield from rwkv(0, 0)
    for h in range(2):
        yield f"pq{h}", 1, "A"
    for t in range(TQ):
        yield f"pk{t}", 1, "A"
    for b in range(GB):
        yield f"pv{b}", 1, "V"
    for b in range(GB):
        for u in range(2):
            yield f"ps{b}.{u}", 4, "V"
        yield f"pm{b}", 1, "V"
        for kt in range(2):
            yield f"pt{b}.{kt}", 4, "A"
        yield f"pc{b}", 1, "A"
    yield from softmax(0)
    yield from norm(2, mean=False)
    yield from mlp(0)
    for a in range(2):
        yield from norm(3 + a)
        yield f"dq{a}", 1, "A"
        yield f"dk{a}", 1, "A"
        yield f"dv{a}", 1, "V"
        for b in range(GB):
            yield f"ds{a}.{b}", 4, "V"
            yield f"dt{a}.{b}", 4, "A"
            yield f"dc{a}.{b}", 1, "A"
        yield from softmax(1 + a)
    yield from norm(5)
    yield from mlp(1)
    yield from rwkv(1, 6)


class PsumPlan:

    def __init__(self):
        self.bank, self.fill, self.read, self.before = {}, {}, {}, {}
        self.total = {"A": 0, "V": 0}
        last, at = [None] * 8, 0
        for n, (name, banks, reader) in enumerate(psum_tiles()):
            at = -(-at // banks) * banks % 8
            need = {}
            for k in range(at, at + banks):
                if last[k] is not None:
                    need[last[k][0]] = max(need.get(last[k][0], 0), last[k][1])
            self.total[reader] += 1
            self.bank[name], self.fill[name] = at, n + 1
            self.read[name] = (reader, self.total[reader])
            self.before[name] = need
            for k in range(at, at + banks):
                last[k] = self.read[name]
            at = (at + banks) % 8
        self.fills = n + 1


NORMS, STATS, SOFTMAXES, MLPS = 8, 13, 3, 2


def build_program(nc, x_in, ctx_in, s0_in, pmask_in, cross_in, ltor_in, const_in, rwkv0_in, perc_in, dec_in, rwkv1_in,
                  out):
    plan = PsumPlan()
    with ExitStack() as ctx:
        def sb(name, *shape, dt=F32):
            return ctx.enter_context(nc.sbuf_tensor(name, list(shape), dt))

        class Signal:

            def __init__(self, name, per=1, base=0):
                self.sem, self.per, self.base = ctx.enter_context(nc.semaphore(name)), per, base

            def __call__(self, g, n=0):
                return self.sem, g * self.per + (self.base + n + 1)

            def all_before(self, g):
                assert self.base > 0
                return self.sem, g * self.per + self.base

        cst = sb("cst", P, CONST_W)
        wr = [sb("w_rwkv0", P, RWKV_W), sb("w_rwkv1", P, RWKV_W)]
        wp = sb("w_perc", P, PERC_W)
        wd = sb("w_dec", P, DEC_W)
        s0 = sb("s0", P, NC_ * GB * S8)
        ltor = sb("ltor", P, T)
        ltor_add = sb("ltor_add", P, T)
        prep = sb("prep", P, TQ + 4 * NC_)

        xin = sb("xin", P, NC_ * N)
        cin = sb("cin", P, NC_ * N)
        s0in = sb("s0in", P, NC_ * GB * S8)
        mcin = sb("mcin", P, GB, T)
        pmin = sb("pmin", 1, N, dt=I32)
        X = sb("X", P, NC_, N)
        CX = sb("CX", P, NC_, N)
        mc = sb("mc", P, GB, T)
        mc_add = sb("mc_add", P, GB, T)
        pmask = sb("pmask", 1, N)

        xc = sb("xc", P, NC_, N)
        sq = sb("sq", P, NC_, N)
        sd = sb("sd", P, BLK)
        rs = sb("rs", P, BLK)
        rm = sb("rm", P, 4, BLK)
        xn = sb("xn", P, NC_, N)
        xout = sb("xout", P, NC_, N)

        ws = sb("ws", P, NC_, GB, T)
        va = sb("va", P, 2 * GB, NH, SLOT)
        mxp = sb("mxp", P, TQ, P)

        ARENA = 11780
        arena = sb("arena", P, ARENA)
        at = [0]

        def cut(*shape):
            size = int(np.prod(shape))
            flat = arena[:, at[0]:at[0] + size]
            at[0] += size
            assert at[0] <= ARENA, at[0]
            if len(shape) == 1:
                return flat
            names = "abc"[:len(shape)]
            return flat.rearrange(f"p ({' '.join(names)}) -> p {' '.join(names)}",
                                  **dict(zip(names[1:], shape[1:])))

        xap = cut(NC_ * GB, T + 1)
        sx = cut(NC_ * GB, T)
        mi = cut(NC_, N)
        tm = cut(N)
        tmb = cut(N)
        tw, e1 = tm, mi.rearrange("p c (b t) -> p (c b) t", b=GB)
        tmp = [cut(NC_, N), cut(NC_, N)]
        xf = [cut(NC_, N) for _ in range(5)]
        rr, kk, vv, g2 = [cut(NC_, N) for _ in range(4)]
        ruk, tg = tmp
        kv = [cut(S8, N), cut(S8, N)]
        bv, yy, yc, yn = xf[:4]
        ki, ri, tr, rl, k2 = xf
        ff = tmp[0]
        og = mi

        at[0] = 0
        qa = cut(TQ, N)
        ka = cut(TQ, 2 * GB, T)
        qb = cut(TQ, T)
        pt = cut(2, NH, T)
        ca = cut(TQ, N)
        cn = cut(TQ, N)
        hd = cut(HID // P, N)
        at[0] = TQ * N
        qe, qo, ks = [cut(NC_, N) for _ in range(3)]
        mx = sb("mx", P, NH)
        tt = hd.rearrange("p a b -> p (a b)").rearrange("p (h k) -> p h k", h=NH)
        p2 = pt[:, 0]

        ps = ctx.enter_context(nc.psum_tensor("ps", [P, 8, 512], F32))

        weights_in = Signal("weights_in")
        prepared = Signal("prepared")
        inputs_in = Signal("inputs_in", 5 * 16)
        stored = Signal("stored", 16, base=16)
        filled = Signal("filled", plan.fills)
        act_read = Signal("act_read", plan.total["A"], base=1)
        dve_read = Signal("dve_read", plan.total["V"], base=1)
        x_ready = Signal("x_ready", 2)
        xout_ready = Signal("xout_ready", base=1)
        ctx_ready = Signal("ctx_ready", base=1)
        pmask_ready = Signal("pmask_ready", base=1)
        cross_ready = Signal("cross_ready")
        squared = Signal("squared", NORMS + 2)
        inverted = Signal("inverted", NORMS + 2)
        spread = Signal("spread", STATS)
        normed = Signal("normed", NORMS - 1)
        state_in = Signal("state_in", 4)
        shifted = Signal("shifted", 4)
        mixed_in = Signal("mixed_in", 2)
        xf_ready = Signal("xf_ready", 10)
        decay = Signal("decay", 2)
        g_tanh = Signal("g_tanh", 2)
        ruk_ready = Signal("ruk_ready", 2)
        s0_placed = Signal("s0_placed", 4)
        scanned = Signal("scanned", 4)
        r_state = Signal("r_state", 4)
        gated = Signal("gated", 2)
        ffn_in = Signal("ffn_in", 4)
        ffn_sq = Signal("ffn_sq", 2)
        max_ready = Signal("max_ready", 2 * GB)
        s_add = Signal("s_add", 2 * GB)
        s_sub = Signal("s_sub", 2 * GB)
        probs = Signal("probs", 2 * GB)

        def done(g, name):
            reader, count = plan.read[name]
            return (act_read if reader == "A" else dve_read)(g, count - 1)

        def const(name, i=0, w=P, rows=slice(0, P)):
            a = CONST[name][0] + i * w
            return cst[rows, a:a + w]

        def vec(pack, fields, name, i=0):
            a = fields[name][0] + i
            return pack[:, a:a + 1]

        def tile_of(name, banks=1):
            b = plan.bank[name]
            return ps[:, b, :] if banks == 1 else ps[:, b:b + banks, :]

        def pair(name):
            return tile_of(name).rearrange("p (c n) -> p c n", c=2)

        def wide(ap, k):
            n = ap.shape[-1]
            return ap.rearrange("p (o n) -> p o n", o=1).to_broadcast([ap.shape[0], k, n])

        def inner(ap, n):
            return ap.rearrange("p (k o) -> p k o", o=1).to_broadcast([ap.shape[0], ap.shape[-1], n])

        block = ctx.enter_context(nc.Block())

        @block.sync
        def _(sp):
            for dst, src in ((cst, const_in), (wr[0], rwkv0_in), (wp, perc_in), (wd, dec_in), (wr[1], rwkv1_in),
                             (ltor, ltor_in)):
                sp.dma_start(dst[:, :], src).then_inc(weights_in.sem, 16)
            sp.sem_inc(stored.sem, stored.base)
            with sp.Fori(0, GROUPS) as g:
                sp.wait_ge(*pmask_ready.all_before(g))
                sp.wait_ge(*ctx_ready.all_before(g))
                sp.dma_start(xin[:, :], x_in[bass.ds(g, 1)].rearrange("g p n -> (g p) n")).then_inc(inputs_in.sem, 16)
                sp.dma_start(cin[:, :], ctx_in[bass.ds(g, 1)].rearrange("g p n -> (g p) n")).then_inc(inputs_in.sem, 16)
                sp.dma_start(s0in[:, :], s0_in[bass.ds(g, 1)].rearrange("g p n -> (g p) n")).then_inc(inputs_in.sem, 16)
                sp.dma_start(mcin[:, :, :], cross_in[bass.ds(g, 1)].rearrange("g p b k -> (g p) b k")).then_inc(
                    inputs_in.sem, 16)
                sp.dma_start(pmin[:, :], pmask_in[bass.ds(g, 1)]).then_inc(inputs_in.sem, 16)
                sp.wait_ge(*xout_ready(g))
                sp.dma_start(out[bass.ds(g, 1)].rearrange("g p n -> (g p) n"),
                             xout[:, :, :].rearrange("p c n -> p (c n)")).then_inc(stored.sem, 16)
            sp.wait_ge(stored.sem, 16 * GROUPS + stored.base)

        @block.tensor
        def _(pe):
            def fill(g, name, banks=1):
                for reader, count in plan.before[name].items():
                    freed = act_read if reader == "A" else dve_read
                    pe.wait_ge(*freed(g, count - 1))
                return tile_of(name, banks)

            def mm(o, lhsT, rhs, start=True, stop=True, pos=None):
                return pe.matmul(o, lhsT, rhs, start=start, stop=stop, skip_group_check=True)

            def linear(o, pack, fields, name, rhs, n_out, k_tiles=NC_):
                a, w = fields[name]
                width = w // k_tiles
                for m in range(n_out):
                    for k in range(k_tiles):
                        i = mm(o[:, m], pack[:, a + k * width + m * P:a + k * width + (m + 1) * P], rhs[:, k],
                               start=(k == 0), stop=(k == k_tiles - 1))
                return i

            def narrow(g, name, ready, z, lhs, src, k_tiles):
                o = fill(g, name)
                pe.wait_ge(*ready)
                for k in range(k_tiles):
                    for q in range(4):
                        i = mm(o[SLOT * q:SLOT * (q + 1), 0:BLK], lhs(k), src[:, k, q * BLK:(q + 1) * BLK],
                               start=(k == 0), stop=(k == k_tiles - 1))
                i.then_inc(filled.sem, 1)

            def norm(g, i, z, src, mean=True):
                if mean:
                    o = fill(g, f"mean{i}")
                    for c in range(NC_):
                        m = mm(o[:, 0:N], const("mean"), src[:, c], start=(c == 0), stop=(c == 1))
                    m.then_inc(filled.sem, 1)
                narrow(g, f"var{i}", squared(g, SQ_AT[i]), z, lambda k: const("mean")[:, 0:SLOT], sq, NC_)
                o = fill(g, f"scale{i}")
                pe.wait_ge(*spread(g, z))
                mm(o[:, 0:N], const("spread_ln"), rm[:, :, :]).then_inc(filled.sem, 1)

            def rwkv(g, l, i, z):
                w, R = wr[l], RWKV
                pe.wait_ge(*(x_ready(g, 0) if l == 0 else done(g, "down1")))
                norm(g, i, z, X)
                o = fill(g, f"mix{l}")
                pe.wait_ge(*mixed_in(g, l))
                a = R["w1"][0]
                for k in range(NC_):
                    mm(o[:, 0:N], w[:, a + 160 * k:a + 160 * k + P], mi[:, k], start=(k == 0), stop=(k == 1))
                for k in range(NC_):
                    m = mm(o[0:32, N:2 * N], w[:, a + 160 * k + P:a + 160 * (k + 1)], mi[:, k], start=(k == 0),
                           stop=(k == 1))
                m.then_inc(filled.sem, 1)
                for f in range(5):
                    o = fill(g, f"maa{l}.{f}")
                    if f == 0:
                        pe.wait_ge(*done(g, f"mix{l}"))
                    a = R["w2" if f < 4 else "w2b"][0]
                    r = slice(32 * f, 32 * f + 32) if f < 4 else slice(0, 32)
                    src = tm if f < 4 else tmb
                    for c in range(NC_):
                        m = mm(o[:, c * N:(c + 1) * N], w[r, a + c * P:a + (c + 1) * P], src[r, :])
                    m.then_inc(filled.sem, 1)
                at_f = {x: ORDER[l].index(x) for x in ORDER[l]}
                o = fill(g, f"td1.{l}")
                pe.wait_ge(*xf_ready(g, 5 * l + at_f["w"]))
                a = R["td1"][0]
                for k in range(NC_):
                    m = mm(o[0:64, 0:N], w[:, a + 64 * k:a + 64 * (k + 1)], xf[at_f["w"]][:, k], start=(k == 0),
                           stop=(k == 1))
                m.then_inc(filled.sem, 1)
                o = fill(g, f"td2.{l}")
                pe.wait_ge(*done(g, f"td1.{l}"))
                a = R["td2"][0]
                for c in range(NC_):
                    m = mm(o[:, c * N:(c + 1) * N], w[0:64, a + c * P:a + (c + 1) * P], tw[0:64, :])
                m.then_inc(filled.sem, 1)
                for x in "kvrg":
                    fill(g, f"{x}{l}")
                    pe.wait_ge(*xf_ready(g, 5 * l + at_f[x]))
                    linear(pair(f"{x}{l}"), w, R, "W" + x, xf[at_f[x]], 2).then_inc(filled.sem, 1)
                fill(g, f"bonus{l}")
                pe.wait_ge(*ruk_ready(g, l))
                o = pair(f"bonus{l}")
                for c in range(NC_):
                    m = mm(o[:, c], const("head_sum"), ruk[:, c])
                m.then_inc(filled.sem, 1)
                pe.wait_ge(*done(g, f"v{l}"))
                for c in range(NC_):
                    for j in range(0, S8, 2):
                        fill(g, f"vb{l}.{c}.{j}")
                        o = pair(f"vb{l}.{c}.{j}")
                        for h in range(2):
                            m = mm(o[:, h], const("sel", j + h), vv[:, c])
                        m.then_inc(filled.sem, 1)
                fill(g, f"y{l}")
                o = pair(f"y{l}")
                for c in range(NC_):
                    pe.wait_ge(*r_state(g, 2 * l + c))
                    for j in range(S8):
                        m = mm(o[:, c], const("red", j), kv[c][:, j], start=(j == 0), stop=(j == S8 - 1))
                m.then_inc(filled.sem, 1)
                fill(g, f"gmean{l}")
                pe.wait_ge(*done(g, f"y{l}"))
                o = pair(f"gmean{l}")
                for c in range(NC_):
                    m = mm(o[:, c], const("head_mean"), yy[:, c])
                m.then_inc(filled.sem, 1)
                narrow(g, f"gvar{l}", squared(g, GN_SQ_AT[l]), z + 1, lambda k: const("narrow_gn", k, SLOT), sq, NC_)
                fill(g, f"gscale{l}")
                pe.wait_ge(*spread(g, z + 1))
                o = pair(f"gscale{l}")
                for c in range(NC_):
                    m = mm(o[:, c], const("spread_gn", c), rm[:, :, :])
                m.then_inc(filled.sem, 1)
                fill(g, f"wo{l}")
                pe.wait_ge(*gated(g, l))
                linear(pair(f"wo{l}"), w, R, "Wo", og, 2).then_inc(filled.sem, 1)
                pe.wait_ge(*done(g, f"wo{l}"))
                norm(g, i + 1, z + 2, X)
                fill(g, f"fr{l}")
                pe.wait_ge(*ffn_in(g, 2 * l))
                linear(pair(f"fr{l}"), w, R, "Fr", ri, 2).then_inc(filled.sem, 1)
                fill(g, f"fk{l}")
                pe.wait_ge(*ffn_in(g, 2 * l + 1))
                linear(pair(f"fk{l}"), w, R, "Fk", ki, 2).then_inc(filled.sem, 1)
                fill(g, f"fv{l}")
                pe.wait_ge(*ffn_sq(g, l))
                linear(pair(f"fv{l}"), w, R, "Fv", k2, 2).then_inc(filled.sem, 1)

            def softmax_out(g, a, z, pack, fields, name):
                narrow(g, f"den{a}", done(g, ("pc1", "dc0.1", "dc1.1")[a]), z, lambda k: const("narrow_sm", k, SLOT), ca, TQ)
                for h in range(2):
                    fill(g, f"inv{a}.{h}")
                    if h == 0:
                        pe.wait_ge(*spread(g, z))
                    o = pair(f"inv{a}.{h}")
                    for t in range(2):
                        m = mm(o[:, t], const("spread_sm", 2 * h + t), rm[:, :, :])
                    m.then_inc(filled.sem, 1)
                fill(g, f"o{a}")
                pe.wait_ge(*done(g, f"inv{a}.1"))
                linear(pair(f"o{a}"), pack, fields, name, cn, 2, k_tiles=TQ).then_inc(filled.sem, 1)

            def mlp(g, m, pack, fields):
                a = fields["m1"][0]
                for n in range(HID // P // 2):
                    fill(g, f"hid{m}.{n}")
                    o = pair(f"hid{m}.{n}")
                    for h in range(2):
                        for k in range(NC_):
                            w0 = a + k * HID + (2 * n + h) * P
                            i = mm(o[:, h], pack[:, w0:w0 + P], xn[:, k], start=(k == 0), stop=(k == 1))
                    i.then_inc(filled.sem, 1)
                fill(g, f"down{m}")
                pe.wait_ge(*done(g, f"hid{m}.3"))
                linear(pair(f"down{m}"), pack, fields, "m2", hd, 2, k_tiles=HID // P).then_inc(filled.sem, 1)

            def values(g, name, src, weight, fields, wname):
                fill(g, name)
                o = pair(name)
                a = fields[wname][0]
                for s, (buf, b) in enumerate(src):
                    for k in range(NC_):
                        m = mm(o[:, s], buf[:, k, b * T:(b + 1) * T], weight[:, a + k * C:a + (k + 1) * C],
                               start=(k == 0), stop=(k == 1))
                m.then_inc(filled.sem, 1)

            def perceiver(g):
                pe.wait_ge(*x_ready(g, 1))
                a = PERC["q"][0]
                for h in range(2):
                    fill(g, f"pq{h}")
                    o = pair(f"pq{h}")
                    for t in range(2):
                        for k in range(NC_):
                            w0 = a + k * TQ * P + (2 * h + t) * P
                            m = mm(o[:, t], wp[:, w0:w0 + P], X[:, k], start=(k == 0), stop=(k == 1))
                    m.then_inc(filled.sem, 1)
                a = PERC["k"][0]
                pe.wait_ge(*ctx_ready(g))
                pe.wait_ge(*pmask_ready(g))
                for t in range(TQ):
                    fill(g, f"pk{t}")
                    o = pair(f"pk{t}")
                    for s, buf in enumerate((CX, X)):
                        for k in range(NC_):
                            w0 = a + k * TQ * P + t * P
                            m = mm(o[:, s], wp[:, w0:w0 + P], buf[:, k], start=(k == 0), stop=(s == 1 and k == 1))
                        if s == 0:
                            mm(o[:, s], const("maskrow", rows=slice(0, 1)), pmask[:, :], start=False)
                    m.then_inc(filled.sem, 1)
                for b in range(GB):
                    values(g, f"pv{b}", ((CX, b), (X, b)), wp, PERC, "v")
                pe.wait_ge(*done(g, "pq1"))
                pe.wait_ge(*done(g, "pk3"))
                for b in range(GB):
                    for u in range(2):
                        o = fill(g, f"ps{b}.{u}", 4)
                        for t in range(2):
                            for j in range(4):
                                r = slice(SLOT * j, SLOT * (j + 1))
                                m = mm(o[:, j, t * 2 * T:(t + 1) * 2 * T], qa[r, 2 * u + t, b * T:(b + 1) * T],
                                       ka[r, 2 * u + t, 2 * b:2 * b + 2, :])
                        m.then_inc(filled.sem, 1)
                    o = fill(g, f"pm{b}")
                    pe.wait_ge(*done(g, f"ps{b}.1"))
                    for t in range(TQ):
                        m = pe.transpose(o[:, t * T:(t + 1) * T], mxp[:, t, :], const("ident"))
                    m.then_inc(filled.sem, 1)
                    for kt in range(2):
                        o = fill(g, f"pt{b}.{kt}", 4)
                        if kt == 0:
                            pe.wait_ge(*done(g, f"pm{b}"))
                        for t in range(TQ):
                            for j in range(4):
                                r = slice(SLOT * j, SLOT * (j + 1))
                                m = mm(o[:, j, t * T:(t + 1) * T], ka[r, t, 2 * b + kt, :], qb[r, t, :])
                        m.then_inc(filled.sem, 1)
                    o = fill(g, f"pc{b}")
                    pe.wait_ge(*done(g, f"pv{b}"))
                    pe.wait_ge(*done(g, f"pt{b}.1"))
                    for t in range(TQ):
                        for kt in range(2):
                            for j in range(4):
                                m = mm(o[SLOT * j:SLOT * (j + 1), t * T:(t + 1) * T], va[:, 2 * b + kt, 4 * t + j, :],
                                       pt[:, kt, 4 * j + t, :], start=(kt == 0), stop=(kt == 1))
                    m.then_inc(filled.sem, 1)
                softmax_out(g, 0, 3, wp, PERC, "o")
                norm(g, 2, 4, None, mean=False)
                pe.wait_ge(*done(g, "scale2"))
                mlp(g, 0, wp, PERC)

            def attention(g, a, i, z):
                pe.wait_ge(*done(g, "down0" if a == 0 else "o1"))
                norm(g, i, z, X)
                src = xn if a == 0 else CX
                pe.wait_ge(*normed(g, NORMED_AT[i]))
                fill(g, f"dq{a}")
                linear(pair(f"dq{a}"), wd, DEC, f"q{a}", xn, 2).then_inc(filled.sem, 1)
                fill(g, f"dk{a}")
                linear(pair(f"dk{a}"), wd, DEC, f"k{a}", src, 2).then_inc(filled.sem, 1)
                values(g, f"dv{a}", ((src, 0), (src, 1)), wd, DEC, f"v{a}")
                pe.wait_ge(*done(g, f"dq{a}"))
                pe.wait_ge(*done(g, f"dk{a}"))
                for b in range(GB):
                    o = fill(g, f"ds{a}.{b}", 4)
                    for t in range(TQ):
                        for j in range(4):
                            r = slice(SLOT * j, SLOT * (j + 1))
                            q = qe if t % 2 == 0 else qo
                            m = mm(o[:, j, t * T:(t + 1) * T], q[r, t // 2, b * T:(b + 1) * T],
                                   ks[r, t // 2, b * T:(b + 1) * T])
                    m.then_inc(filled.sem, 1)
                    o = fill(g, f"dt{a}.{b}", 4)
                    pe.wait_ge(*probs(g, GB * a + b))
                    for h in range(NH):
                        m = pe.transpose(o[:, h // 4, (h % 4) * T:(h % 4 + 1) * T], tt[:, h, :], const("ident"))
                    m.then_inc(filled.sem, 1)
                    o = fill(g, f"dc{a}.{b}")
                    pe.wait_ge(*done(g, f"dt{a}.{b}"))
                    if b == 0:
                        pe.wait_ge(*done(g, f"dv{a}"))
                    for t in range(TQ):
                        for j in range(4):
                            h = 8 * (t // 2) + 2 * j + t % 2
                            m = mm(o[SLOT * j:SLOT * (j + 1), t * T:(t + 1) * T], va[:, b, h, :], p2[:, 4 * j + t, :])
                    m.then_inc(filled.sem, 1)
                softmax_out(g, 1 + a, z + 1, wd, DEC, f"o{a}")

            pe.wait_ge(weights_in.sem, 6 * 16)
            pe.wait_ge(*prepared(0))
            with pe.Fori(0, GROUPS) as g:
                pe.wait_ge(*act_read.all_before(g))
                pe.wait_ge(*dve_read.all_before(g))
                rwkv(g, 0, 0, 0)
                perceiver(g)
                attention(g, 0, 3, 5)
                attention(g, 1, 4, 7)
                pe.wait_ge(*done(g, "o2"))
                norm(g, 5, 9, X)
                pe.wait_ge(*normed(g, NORMED_AT[5]))
                mlp(g, 1, wd, DEC)
                rwkv(g, 1, 6, 10)

        @block.scalar
        def _(act):
            seen = [0]

            def full(g, name):
                assert plan.read[name][0] != "A" or plan.read[name][1] >= seen[0]
                act.wait_ge(filled.sem, g * plan.fills + plan.fill[name])

            def f(o, i, fn, **kw):
                return nc.scalar.activation(o, i, fn, **kw)

            def norm(g, i, z, bias, dst, src=None, mean=True):
                if mean:
                    act.wait_ge(*done(g, f"mean{i}"))
                f(sq[:, :, :], (xc if src is None else src)[:, :, :], ACT.Square).then_inc(squared.sem, 1)
                full(g, f"var{i}")
                f(sd[:, :], tile_of(f"var{i}")[:, 0:BLK], ACT.Sqrt, bias=const("eps5" if mean else "eps6", w=1)
                  ).then_inc(act_read.sem, 1)
                if bias is None:
                    return
                act.wait_ge(*done(g, f"scale{i}"))
                for c in range(NC_):
                    m = f(dst(c), dst(c), ACT.Identity, bias=bias(c))
                m.then_inc(normed.sem, 1)

            def state(part):
                f(xap[:, :, 0:1], CX[:, :, 1 - part::T].rearrange("p c (b o) -> p (c b) o", o=1), ACT.Copy).then_inc(
                    state_in.sem, 1)

            def plain(c):
                return xn[:, c]

            def padded(c):
                return xap[:, c * GB:(c + 1) * GB, 1:T + 1]

            def rwkv(g, l, i, z):
                w, R = wr[l], RWKV
                act.wait_ge(*(xout_ready.all_before(g) if l == 0 else done(g, "down1")))
                state(0)
                for c in range(NC_):
                    f(kv[c].rearrange("p j (b t) -> p j b t", b=GB)[:, :, :, 0],
                      s0[:, c * GB * S8:(c + 1) * GB * S8].rearrange("p (j b) -> p j b", b=GB), ACT.Copy).then_inc(
                        s0_placed.sem, 1)
                norm(g, i, z, lambda c: vec(w, R, "ln1_b", c), padded)
                o = tile_of(f"mix{l}")
                full(g, f"mix{l}")
                f(tm, o[:, 0:N], ACT.Tanh)
                f(tmb[0:32, :], o[0:32, N:2 * N], ACT.Tanh).then_inc(act_read.sem, 1)
                full(g, f"td1.{l}")
                f(tw[0:64, :], tile_of(f"td1.{l}")[0:64, 0:N], ACT.Tanh).then_inc(act_read.sem, 1)
                full(g, f"td2.{l}")
                for c in range(NC_):
                    m = f(e1[:, c * GB:(c + 1) * GB, :].rearrange("p b t -> p (b t)"), pair(f"td2.{l}")[:, c], ACT.Exp,
                          bias=vec(w, R, "td", c))
                m.then_inc(act_read.sem, 1)
                act.wait_ge(*done(g, f"td2.{l}"))
                f(ws[:, :, :, 1:T].rearrange("p c b t -> p (c b) t"), e1[:, :, 0:T - 1], ACT.Exp,
                  scale=-1.0).then_inc(decay.sem, 1)
                for x, dst in (("k", kk), ("v", vv), ("r", rr)):
                    full(g, f"{x}{l}")
                    f(dst[:, :, :], pair(f"{x}{l}"), ACT.Copy).then_inc(act_read.sem, 1)
                full(g, f"g{l}")
                f(tg[:, :, :], pair(f"g{l}"), ACT.Tanh, scale=0.5).then_inc(g_tanh.sem, 1)
                act.wait_ge(*done(g, f"gmean{l}"))
                f(sq[:, :, :], yc[:, :, :], ACT.Square).then_inc(squared.sem, 1)
                full(g, f"gvar{l}")
                f(sd[:, :], tile_of(f"gvar{l}")[:, 0:BLK], ACT.Sqrt, bias=const("eps5", w=1)).then_inc(act_read.sem, 1)
                act.wait_ge(*done(g, f"wo{l}"))
                state(1)
                norm(g, i + 1, z + 2, lambda c: vec(w, R, "ln2_b", c), padded)
                full(g, f"fr{l}")
                f(tr[:, :, :], pair(f"fr{l}"), ACT.Tanh, scale=0.5).then_inc(act_read.sem, 1)
                full(g, f"fk{l}")
                f(rl[:, :, :], pair(f"fk{l}"), ACT.Relu).then_inc(act_read.sem, 1)
                act.wait_ge(*done(g, f"fk{l}"))
                f(k2[:, :, :], rl[:, :, :], ACT.Square).then_inc(ffn_sq.sem, 1)

            def mlp(g, m, pack, fields):
                for n in range(HID // P // 2):
                    full(g, f"hid{m}.{n}")
                    for h in range(2):
                        i = f(hd[:, 2 * n + h], pair(f"hid{m}.{n}")[:, h], ACT.Gelu_apprx_tanh,
                              bias=vec(pack, fields, "b1", 2 * n + h))
                    i.then_inc(act_read.sem, 1)

            def heads_out(g, name, b):
                full(g, name)
                f(ca[:, :, b * T:(b + 1) * T], tile_of(name).rearrange("p (t q) -> p t q", t=TQ), ACT.Copy).then_inc(act_read.sem, 1)

            def perceiver(g):
                for h in range(2):
                    full(g, f"pq{h}")
                    for t in range(2):
                        m = f(qa[:, 2 * h + t], pair(f"pq{h}")[:, t], ACT.Identity, scale=1.0 / HD,
                              bias=prep[:, 2 * h + t:2 * h + t + 1])
                    m.then_inc(act_read.sem, 1)
                for t in range(TQ):
                    full(g, f"pk{t}")
                    for s in range(2):
                        m = f(ka[:, t, s::2, :], pair(f"pk{t}")[:, s].rearrange("p (b k) -> p b k", b=GB),
                              ACT.Identity, bias=vec(wp, PERC, "kb", t))
                    m.then_inc(act_read.sem, 1)
                for b in range(GB):
                    for kt in range(2):
                        full(g, f"pt{b}.{kt}")
                        f(pt[:, kt].rearrange("p h q -> p (h q)"),
                          tile_of(f"pt{b}.{kt}", 4).rearrange("p j n -> p (j n)"), ACT.Exp).then_inc(act_read.sem, 1)
                    heads_out(g, f"pc{b}", b)
                act.wait_ge(*done(g, "o0"))
                norm(g, 2, 4, None, None, src=xc, mean=False)
                mlp(g, 0, wp, PERC)

            def attention(g, a, i, z):
                norm(g, i, z, lambda c: vec(wd, DEC, f"ln{1 + a}_b", c), plain)
                full(g, f"dq{a}")
                for c in range(NC_):
                    for e, (dst, m) in enumerate(((qe, "even"), (qo, "odd"))):
                        at_ = TQ + (2 * a + e) * NC_ + c
                        m = f(dst[:, c], pair(f"dq{a}")[:, c], ACT.Identity, scale=const(m, w=1),
                              bias=prep[:, at_:at_ + 1])
                m.then_inc(act_read.sem, 1)
                full(g, f"dk{a}")
                for c in range(NC_):
                    m = f(ks[:, c], pair(f"dk{a}")[:, c], ACT.Identity, bias=vec(wd, DEC, f"kb{a}", c))
                m.then_inc(act_read.sem, 1)
                for b in range(GB):
                    act.wait_ge(*s_sub(g, GB * a + b))
                    f(tt[:, :, :], tt[:, :, :], ACT.Exp).then_inc(probs.sem, 1)
                    full(g, f"dt{a}.{b}")
                    f(p2.rearrange("p h q -> p (h q)"), tile_of(f"dt{a}.{b}", 4).rearrange("p j n -> p (j n)"),
                      ACT.Copy).then_inc(act_read.sem, 1)
                    heads_out(g, f"dc{a}.{b}", b)

            act.wait_ge(weights_in.sem, 6 * 16)
            act.wait_ge(*prepared(0))
            for s in (act_read, ctx_ready):
                act.sem_inc(s.sem, s.base)
            with act.Fori(0, GROUPS) as g:
                act.wait_ge(*inputs_in(g, 5 * 16 - 1))
                act.wait_ge(*xout_ready.all_before(g))
                f(s0[:, :], s0in[:, :], ACT.Copy)
                f(mc[:, :, :], mcin[:, :, :], ACT.Copy).then_inc(cross_ready.sem, 1)
                f(CX[:, :, :], cin[:, :].rearrange("p (c n) -> p c n", c=NC_), ACT.Copy).then_inc(ctx_ready.sem, 1)
                act.wait_ge(*ctx_ready(g))
                rwkv(g, 0, 0, 0)
                perceiver(g)
                attention(g, 0, 3, 5)
                attention(g, 1, 4, 7)
                norm(g, 5, 9, lambda c: vec(wd, DEC, "ln3_b", c), plain)
                mlp(g, 1, wd, DEC)
                rwkv(g, 1, 6, 10)

        @block.vector
        def _(dve):
            V = nc.vector

            def full(g, name):
                dve.wait_ge(filled.sem, g * plan.fills + plan.fill[name])

            def invert(g, z, n, src):
                V.reciprocal(rs[:, :], src).then_inc(inverted.sem, 1)
                dve.wait_ge(*inverted(g, n))
                return V.tensor_tensor(rm[:, :, :], wide(rs[:, :], 4), inner(const("block", w=4), BLK),
                                       ALU.mult).then_inc(spread.sem, 1)

            def norm(g, i, z, weight, dst, src=xc, mean=True):
                if mean:
                    full(g, f"mean{i}")
                    V.tensor_tensor(xc[:, :, :], X[:, :, :], wide(tile_of(f"mean{i}")[:, 0:N], NC_),
                                    ALU.subtract).then_inc(dve_read.sem, 1)
                dve.wait_ge(*done(g, f"var{i}"))
                invert(g, z, SQ_AT[i], sd[:, :])
                full(g, f"scale{i}")
                for c in range(NC_):
                    m = V.scalar_tensor_tensor(dst(c), by_row(xc[:, c]), weight(c),
                                               by_row(tile_of(f"scale{i}")[:, 0:N]), ALU.mult, ALU.mult)
                m.then_inc(dve_read.sem, 1)

            def shift(g, n, i):
                dve.wait_ge(*normed(g, NORMED_AT[i]))
                dve.wait_ge(*state_in(g, n))
                V.tensor_tensor(sx, xap[:, :, 0:T], xap[:, :, 1:T + 1], ALU.subtract).then_inc(shifted.sem, 1)
                dve.wait_ge(*shifted(g, n))

            def sxc(c):
                return sx[:, c * GB:(c + 1) * GB, :]

            def xac(c):
                return xap[:, c * GB:(c + 1) * GB, 1:T + 1]

            def xnc(c):
                return by_row(xn[:, c])

            def by_row(ap):
                return ap.rearrange("p (b t) -> p b t", b=GB)

            def rwkv(g, l, i, z):
                w, R = wr[l], RWKV
                norm(g, i, z, lambda c: vec(w, R, "ln1_w", c), xac)
                shift(g, 2 * l, i)
                for c in range(NC_):
                    m = V.scalar_tensor_tensor(by_row(mi[:, c]), sxc(c), vec(w, R, "maa_x", c), xac(c), ALU.mult,
                                               ALU.add)
                m.then_inc(mixed_in.sem, 1)
                for n in range(5):
                    full(g, f"maa{l}.{n}")
                    if n >= 2:
                        dve.wait_ge(*xf_ready(g, 5 * l + n - 2))
                    for c in range(NC_):
                        m = V.scalar_tensor_tensor(by_row(tmp[n % 2][:, c]), by_row(pair(f"maa{l}.{n}")[:, c]),
                                                   vec(w, R, "maa", 2 * n + c), sxc(c), ALU.add, ALU.mult)
                    m.then_inc(dve_read.sem, 1)
                full(g, f"g{l}")
                dve.wait_ge(*g_tanh(g, l))
                V.scalar_tensor_tensor(g2, tg, 1.0, pair(f"g{l}"), ALU.add, ALU.mult).then_inc(dve_read.sem, 1)
                dve.wait_ge(*done(g, f"r{l}"))
                dve.wait_ge(*done(g, f"k{l}"))
                for c in range(NC_):
                    m = V.scalar_tensor_tensor(ruk[:, c], rr[:, c], vec(w, R, "u", c), kk[:, c], ALU.mult, ALU.mult)
                m.then_inc(ruk_ready.sem, 1)
                full(g, f"bonus{l}")
                dve.wait_ge(*done(g, f"v{l}"))
                V.tensor_tensor(bv, vv, pair(f"bonus{l}"), ALU.mult).then_inc(dve_read.sem, 1)
                for c in range(NC_):
                    for j in range(0, S8, 2):
                        full(g, f"vb{l}.{c}.{j}")
                        for h in range(2):
                            m = V.tensor_tensor(by_row(kv[c][:, j + h])[:, :, 1:T], by_row(kk[:, c])[:, :, 0:T - 1],
                                                by_row(pair(f"vb{l}.{c}.{j}")[:, h])[:, :, 0:T - 1], ALU.mult)
                        m.then_inc(dve_read.sem, 1)
                    dve.wait_ge(*done(g, f"vb{l}.{c}.{S8 - 2}"))
                    dve.wait_ge(*s0_placed(g, 2 * l + c))
                    dve.wait_ge(*decay(g, l))
                    for j in range(S8):
                        m = V.tensor_tensor_scan(kv[c][:, j], ws[:, c].rearrange("p b t -> p (b t)"), kv[c][:, j], 0.0,
                                                 ALU.mult, ALU.add)
                    m.then_inc(scanned.sem, 1)
                    dve.wait_ge(*scanned(g, 2 * l + c))
                    V.tensor_tensor(kv[c], kv[c], wide(rr[:, c], S8), ALU.mult).then_inc(r_state.sem, 1)
                full(g, f"y{l}")
                dve.wait_ge(*done(g, f"bonus{l}"))
                V.tensor_tensor(yy, bv, pair(f"y{l}"), ALU.add).then_inc(dve_read.sem, 1)
                full(g, f"gmean{l}")
                dve.wait_ge(*done(g, f"y{l}"))
                V.tensor_tensor(yc, yy, pair(f"gmean{l}"), ALU.subtract).then_inc(dve_read.sem, 1)
                dve.wait_ge(*done(g, f"gvar{l}"))
                invert(g, z + 1, GN_SQ_AT[l], sd[:, :])
                full(g, f"gscale{l}")
                for c in range(NC_):
                    m = V.scalar_tensor_tensor(yn[:, c], yc[:, c], vec(w, R, "gn_w", c), pair(f"gscale{l}")[:, c],
                                               ALU.mult, ALU.mult)
                m.then_inc(dve_read.sem, 1)
                dve.wait_ge(*done(g, f"gscale{l}"))
                for c in range(NC_):
                    m = V.scalar_tensor_tensor(og[:, c], yn[:, c], vec(w, R, "gn_b", c), g2[:, c], ALU.add, ALU.mult)
                m.then_inc(gated.sem, 1)
                full(g, f"wo{l}")
                V.scalar_tensor_tensor(X[:, :, :], pair(f"wo{l}"), 0.5, X[:, :, :], ALU.mult, ALU.add).then_inc(dve_read.sem, 1)
                dve.wait_ge(*done(g, f"wo{l}"))
                norm(g, i + 1, z + 2, lambda c: vec(w, R, "ln2_w", c), xac)
                shift(g, 2 * l + 1, i + 1)
                for dst, v in ((ri, "fr"), (ki, "fk")):
                    for c in range(NC_):
                        m = V.scalar_tensor_tensor(by_row(dst[:, c]), sxc(c), vec(w, R, v, c), xac(c), ALU.mult,
                                                   ALU.add)
                    m.then_inc(ffn_in.sem, 1)
                full(g, f"fv{l}")
                dve.wait_ge(*done(g, f"fr{l}"))
                V.scalar_tensor_tensor(ff, tr, 1.0, pair(f"fv{l}"), ALU.add, ALU.mult).then_inc(dve_read.sem, 1)
                dve.wait_ge(*done(g, f"fv{l}"))
                if l == 1:
                    dve.wait_ge(*stored.all_before(g))
                V.scalar_tensor_tensor((X if l == 0 else xout)[:, :, :], ff, 0.5, X[:, :, :], ALU.mult,
                                       ALU.add).then_inc((x_ready if l == 0 else xout_ready).sem, 1)

            def softmax_out(g, a, z):
                full(g, f"den{a}")
                dve.wait_ge(*done(g, ("pc1", "dc0.1", "dc1.1")[a]))
                V.reciprocal(rs[:, :], tile_of(f"den{a}")[:, 0:BLK]).then_inc(dve_read.sem, 1)
                dve.wait_ge(*done(g, f"den{a}"))
                V.tensor_tensor(rm[:, :, :], wide(rs[:, :], 4), inner(const("block", w=4), BLK), ALU.mult).then_inc(
                    spread.sem, 1)
                for h in range(2):
                    full(g, f"inv{a}.{h}")
                    V.tensor_tensor(cn[:, 2 * h:2 * h + 2], ca[:, 2 * h:2 * h + 2], pair(f"inv{a}.{h}"),
                                        ALU.mult).then_inc(dve_read.sem, 1)

            def add_out(g, name, pack, fields, bias, dst):
                full(g, name)
                for c in range(NC_):
                    m = V.scalar_tensor_tensor(dst[:, c], pair(name)[:, c], vec(pack, fields, bias, c), X[:, c],
                                               ALU.add, ALU.add)
                m.then_inc(dve_read.sem, 1)

            def values(g, name, slots, pack, fields, vb):
                full(g, name)
                o = tile_of(name).rearrange("p (s h d) -> p s h d", s=2, h=NH)
                a = fields[vb][0]
                for s in range(2):
                    m = V.tensor_tensor(va[:, slots + s, :, 0:HD], o[:, s],
                                        pack[:, a:a + C].rearrange("p (h d) -> p h d", h=NH), ALU.add)
                m.then_inc(dve_read.sem, 1)

            def perceiver(g):
                for b in range(GB):
                    values(g, f"pv{b}", 2 * b, wp, PERC, "vb")
                for b in range(GB):
                    for u in range(2):
                        full(g, f"ps{b}.{u}")
                        V.tensor_reduce(mxp[:, 2 * u:2 * u + 2, HD + 1::SLOT].rearrange("p t j -> p j t"),
                                        tile_of(f"ps{b}.{u}", 4).rearrange("p j (t k) -> p j t k", t=2), AX.X, ALU.max,
                                        negate=True).then_inc(dve_read.sem, 1)
                    full(g, f"pm{b}")
                    if b == 0:
                        dve.wait_ge(*done(g, "pq1"))
                    else:
                        full(g, f"pt{b - 1}.1")
                    V.tensor_tensor(qb, qa[:, :, b * T:(b + 1) * T],
                                    tile_of(f"pm{b}").rearrange("p (t q) -> p t q", t=TQ), ALU.add).then_inc(dve_read.sem, 1)
                softmax_out(g, 0, 3)
                add_out(g, "o0", wp, PERC, "ob", xc)
                dve.wait_ge(*done(g, "o0"))
                norm(g, 2, 4, lambda c: vec(wp, PERC, "norm_w", c), xnc, mean=False)
                add_out(g, "down0", wp, PERC, "b2", X)

            def attention(g, a, i, z):
                dve.wait_ge(*done(g, "down0" if a == 0 else "o1"))
                norm(g, i, z, lambda c: vec(wd, DEC, f"ln{1 + a}_w", c), xnc)
                values(g, f"dv{a}", 0, wd, DEC, f"vb{a}")
                for b in range(GB):
                    m = ltor[:, :] if a == 0 else mc[:, b, :]
                    full(g, f"ds{a}.{b}")
                    if b > 0:
                        full(g, f"dt{a}.{b - 1}")
                    if a == 1 and b == 0:
                        dve.wait_ge(*cross_ready(g, 0))
                    V.tensor_tensor(tt, tile_of(f"ds{a}.{b}", 4).rearrange("p j (t k) -> p (j t) k", t=TQ),
                                    wide(m, NH), ALU.mult).then_inc(dve_read.sem, 1)
                    n = GB * a + b
                    dve.wait_ge(*s_add(g, n))
                    V.tensor_reduce(mx[:, :], tt, AX.X, ALU.max).then_inc(max_ready.sem, 1)
                    dve.wait_ge(*max_ready(g, n))
                    V.tensor_tensor(tt, tt, inner(mx[:, :], T), ALU.subtract).then_inc(s_sub.sem, 1)
                softmax_out(g, 1 + a, z + 1)
                add_out(g, f"o{1 + a}", wd, DEC, f"ob{a}", X)

            dve.wait_ge(weights_in.sem, 6 * 16)
            a = PERC["qb"][0]
            V.tensor_scalar(prep[:, 0:TQ], wp[:, a:a + TQ], 1.0 / HD, None, ALU.mult)
            for i in range(2):
                a = DEC[f"qb{i}"][0]
                for e, m in enumerate(("even", "odd")):
                    s = TQ + (2 * i + e) * NC_
                    V.tensor_scalar(prep[:, s:s + NC_], wd[:, a:a + NC_], const(m, w=1), None, ALU.mult)
            V.tensor_scalar(ltor_add[:, :], ltor[:, :], -1.0, 10000.0, ALU.add, ALU.mult)
            V.memset(ws[:, :, :, 0:1], 0.0)
            V.memset(mxp[:, :, :], 0.0)
            V.memset(va[:, :, :, HD:HD + 1], 1.0)
            V.memset(va[:, :, :, HD + 1:], 0.0).then_inc(prepared.sem, 1)
            dve.wait_ge(*prepared(0))
            for s in (dve_read, xout_ready, pmask_ready):
                dve.sem_inc(s.sem, s.base)
            with dve.Fori(0, GROUPS) as g:
                dve.wait_ge(*inputs_in(g, 5 * 16 - 1))
                V.tensor_copy(X[:, :, :], xin[:, :].rearrange("p (c n) -> p c n", c=NC_)).then_inc(x_ready.sem, 1)
                V.tensor_scalar(mc_add[:, :, :], mcin[:, :, :], -1.0, 10000.0, ALU.add, ALU.mult)
                V.tensor_scalar(pmask[:, :], pmin[:, :], 0, MASKED, ALU.is_equal, ALU.mult).then_inc(
                    pmask_ready.sem, 1)
                dve.wait_ge(*x_ready(g, 0))
                rwkv(g, 0, 0, 0)
                perceiver(g)
                attention(g, 0, 3, 5)
                attention(g, 1, 4, 7)
                dve.wait_ge(*done(g, "o2"))
                norm(g, 5, 9, lambda c: vec(wd, DEC, "ln3_w", c), xnc)
                add_out(g, "down1", wd, DEC, "b2", X)
                dve.wait_ge(*done(g, "down1"))
                rwkv(g, 1, 6, 10)

        @block.gpsimd
        def _(pool):
            G = nc.gpsimd

            def rwkv(g, l):
                for n in range(5):
                    pool.wait_ge(*done(g, f"maa{l}.{n}"))
                    G.tensor_tensor(xf[n].rearrange("p c (b t) -> p (c b) t", b=GB),
                                    tmp[n % 2].rearrange("p c (b t) -> p (c b) t", b=GB), xap[:, :, 1:T + 1],
                                    ALU.add).then_inc(xf_ready.sem, 1)

            with pool.Fori(0, GROUPS) as g:
                rwkv(g, 0)
                for n in range(2 * GB):
                    pool.wait_ge(*done(g, f"ds{n // GB}.{n % GB}"))
                    m = ltor_add[:, :] if n < GB else mc_add[:, n % GB, :]
                    G.tensor_tensor(tt, tt, wide(m, NH), ALU.add).then_inc(s_add.sem, 1)
                rwkv(g, 1)


SQ_AT = (0, 2, 3, 4, 5, 6, 7, 9)
GN_SQ_AT = (1, 8)
NORMED_AT = (0, 1, None, 2, 3, 4, 5, 6)




def _k_tiles(w, k=NC_):
    return np.ascontiguousarray(w.reshape(k, P, -1).transpose(1, 0, 2)).reshape(P, -1)


def _vec(v):
    return np.ascontiguousarray(v.reshape(-1, P).T)


def _rows(w):
    return np.concatenate([w, np.zeros((P - w.shape[0], w.shape[1]), np.float32)], 0)


def _pack(fields, part):
    for name, (_, width) in fields.items():
        assert part[name].shape == (P, width), (name, part[name].shape, width)
    return np.ascontiguousarray(np.concatenate([part[name] for name in fields], 1))


def _slots(w, heads, fill=None):
    out = np.zeros((w.shape[0], NH, SLOT), np.float32)
    out[:, :, :HD] = w.reshape(-1, NH, HD)[:, heads]
    if fill:
        for k, v in fill.items():
            out[:, :, k] = v
    return out.reshape(-1, NH * SLOT)


def _rwkv_pack(a, l):
    names = dict(zip(("td1", "td2", "u", "fk", "fr", "Fk", "Fr", "Fv"),
                     ("td_w1", "td_w2", "u", "ffn_maa_k", "ffn_maa_r", "Wfk", "Wfr", "Wfv") if l == 0 else
                     ("decay_w1", "decay_w2", "faaaa", "fmaa_k", "fmaa_r", "fWk", "fWr", "fWv")))
    if l == 0:
        maa = a["maa_stack"].reshape(5, C)
    else:
        maa = np.stack([a["maa_" + x] for x in ORDER[1]])
    w2 = a["maa_w2"].reshape(160, C)
    part = {
        "w1": _k_tiles(a["maa_w1"]), "w2": w2[:P], "w2b": _rows(w2[P:]), "td1": _k_tiles(a[names["td1"]]),
        "td2": _rows(a[names["td2"]]), "maa": _vec(maa), "td": _vec(a["time_decay"]), "u": _vec(a[names["u"]]),
        "fk": _vec(a[names["fk"]]), "fr": _vec(a[names["fr"]]),
    }
    for w in ("Wr", "Wk", "Wv", "Wg", "Wo"):
        part[w] = _k_tiles(a[w].T)
    for w in ("Fk", "Fr", "Fv"):
        part[w] = _k_tiles(a[names[w]].T)
    for v in ("ln1_w", "ln1_b", "ln2_w", "ln2_b", "maa_x", "gn_w", "gn_b"):
        part[v] = _vec(a[v])
    return _pack(RWKV, part)


def kernel(**inputs):
    import concourse.bacc as _bacc
    from concourse.bass_utils import run_bass_kernel_spmd as _run

    a = {k: np.asarray(v) for k, v in inputs.items()}

    def layer(n):
        return {k.split("_xattn_")[1]: v for k, v in a.items() if k.startswith(f"L{n}_")}

    def tokens(v):
        v = v.reshape(GROUPS, N, NC_, P).transpose(0, 3, 2, 1)
        return np.ascontiguousarray(v).reshape(GROUPS, P, NC_ * N)

    ctxt = a["ctx_2048"]
    s0 = ctxt[:, 2:2 + S8].reshape(GROUPS, GB, NC_, P, S8).transpose(0, 3, 2, 4, 1)

    plain = list(range(NH))
    paired = [8 * (t // 2) + 2 * j + t % 2 for t in range(TQ) for j in range(4)]

    def out_rows(w, heads):
        return _k_tiles(np.ascontiguousarray(_slots(np.ascontiguousarray(w.T), heads).T), TQ)

    p1 = layer(1)
    kvw = p1["kv_w"].reshape(C, NH * HD, 2)
    kvb = p1["kv_b"].reshape(NH * HD, 2)

    def all_rows(v):
        return np.ascontiguousarray(np.broadcast_to(v.reshape(1, -1), (P, v.size)))

    perc = _pack(PERC, {
        "q": _k_tiles(_slots(p1["q_w"], plain)), "k": _k_tiles(_slots(kvw[..., 0], plain)),
        "v": _k_tiles(np.ascontiguousarray(kvw[..., 1])), "o": out_rows(p1["out_w"], plain),
        "m1": _k_tiles(p1["mlp_w1"]), "m2": _k_tiles(p1["mlp_w2"], HID // P),
        "qb": _vec(_slots(p1["q_b"].reshape(1, -1), plain, {HD: float(HD)})),
        "kb": _vec(_slots(kvb[:, 0].reshape(1, -1), plain, {HD + 1: 1.0})),
        "vb": all_rows(kvb[:, 1]), "ob": _vec(p1["out_b"]), "norm_w": _vec(p1["postnorm_w"]),
        "b1": _vec(p1["mlp_b1"]), "b2": _vec(p1["mlp_b2"])})
    d = layer(2)
    part = {"m1": _k_tiles(d["w1"]), "m2": _k_tiles(d["w2"], HID // P), "b1": _vec(d["b1"]), "b2": _vec(d["b2"])}
    for n, x in enumerate("qkv"):
        w = d["w_q"] if x == "q" else d["w_kv"][:, (n - 1) * C:n * C]
        b = d["b_q"] if x == "q" else d["b_kv"][(n - 1) * C:n * C]
        for i, (wi, bi) in enumerate(((d["w_qkv"][:, n * C:(n + 1) * C], d["b_qkv"][n * C:(n + 1) * C]), (w, b))):
            part[f"{x}{i}"] = _k_tiles(np.ascontiguousarray(wi))
            part[f"{x}b{i}"] = all_rows(bi) if x == "v" else _vec(bi)
    for i, x in enumerate(("ao", "co")):
        part[f"o{i}"] = out_rows(d["w_" + x], paired)
        part[f"ob{i}"] = _vec(d["b_" + x])
    for n in (1, 2, 3):
        part[f"ln{n}_w"], part[f"ln{n}_b"] = _vec(d[f"ln{n}_s"]), _vec(d[f"ln{n}_b"])
    dec = _pack(DEC, part)

    arrays = {
        "x": tokens(a["x"]), "ctx": tokens(ctxt),
        "s0": np.ascontiguousarray(s0).reshape(GROUPS, P, NC_ * S8 * GB),
        "pmask": np.ascontiguousarray(a["mask_BxS2_ik0"].reshape(GROUPS, N)),
        "cross": np.ascontiguousarray(a["mask_Bx1xSxS2_ff1"].reshape(GROUPS, GB, T, T).transpose(0, 2, 1, 3)),
        "ltor": np.ascontiguousarray(a["mask_1x1xSxS2_fc1"].reshape(T, T)),
        "const": _constants(), "rwkv0": _rwkv_pack(layer(0), 0), "perc": perc, "dec": dec,
        "rwkv1": _rwkv_pack(layer(3), 1),
    }
    nc = _bacc.Bacc("TRN2", target_bir_lowering=False, num_devices=1)
    args = [nc.dram_tensor(f"in_{k}", v.shape, mybir.dt.from_np(v.dtype), kind="ExternalInput").ap()
            for k, v in arrays.items()]
    out = nc.dram_tensor("out_x", (GROUPS, P, NC_ * N), F32, kind="ExternalOutput").ap()
    build_program(nc, *args, out)
    r = _run(nc, [{f"in_{k}": v for k, v in arrays.items()}], core_ids=[0])
    got = r.results[0]["out_x"].reshape(GROUPS, P, NC_, N).transpose(0, 3, 2, 1)
    return np.ascontiguousarray(got).reshape(B, T, C)
```

```python
from contextlib import ExitStack

import numpy as np

import concourse.bass as bass
from concourse import mybir

F32 = mybir.dt.float32
F32R = mybir.dt.float32r
I32 = mybir.dt.int32
ALU = mybir.AluOpType
ACT = mybir.ActivationFunctionType
AX = mybir.AxisListType

P = 128
B, T, C = 16, 128, 256
NC_ = C // P
GB = 2
N = GB * T
GROUPS = B // GB
STREAMS = 2
ROUNDS = GROUPS // STREAMS
S8 = 8
RH = C // S8
NH, HD = 16, 16
HID = 4 * C
SLOT = 32
TQ = NH * SLOT // P
BLK = N // 4
MASKED = -1e30
LAG = 3



def _columns(fields):
    at, out = 0, {}
    for name, width in fields:
        out[name] = (at, width)
        at += width
    return out, at


CONST, CONST_W = _columns([
    ("mean", P), ("spread_ln", P), ("down", 2 * RH), ("all", 2 * P), ("head_mean", P), ("same", P), ("up", 2 * P),
    ("narrow_sm", TQ * SLOT), ("spread_sm", TQ * P),
    ("ident", P), ("block", 4), ("maskrow", P), ("eps5", 1), ("eps6", 1), ("even", 1), ("odd", 1)])
LIN = NC_ * C
RWKV, RWKV_W = _columns(
    [("w1", NC_ * 160), ("w2", C), ("w2b", C), ("td1", NC_ * 64), ("td2", C)]
    + [(w, LIN) for w in ("Wr", "Wk", "Wv", "Wg", "Wo", "Fk", "Fr", "Fv")]
    + [(v, NC_) for v in ("ln1_w", "ln1_b", "ln2_w", "ln2_b", "maa_x", "td", "u", "gn_w", "gn_b", "fk", "fr")]
    + [("maa", 5 * NC_)])
PERC, PERC_W = _columns([
    ("q", NC_ * TQ * P), ("k", NC_ * TQ * P), ("v", LIN), ("o", TQ * C), ("m1", NC_ * HID), ("m2", HID // P * C),
    ("qb", TQ), ("kb", TQ), ("vb", C), ("ob", NC_), ("norm_w", NC_), ("b1", HID // P), ("b2", NC_)])
DEC, DEC_W = _columns(
    [(f"{w}{a}", LIN) for a in (0, 1) for w in "qkv"] + [(f"o{a}", TQ * C) for a in (0, 1)]
    + [("m1", NC_ * HID), ("m2", HID // P * C)]
    + [(f"{w}b{a}", NC_) for a in (0, 1) for w in "qko"] + [(f"vb{a}", C) for a in (0, 1)]
    + [(f"ln{n}_{x}", NC_) for n in (1, 2, 3) for x in "wb"] + [("b1", HID // P), ("b2", NC_)])
ORDER = (("k", "w", "v", "r", "g"), ("w", "k", "v", "r", "g"))
STATE_W = 2 * NC_ * GB + NC_ * S8 * GB


def _constants():
    p = np.arange(P)[:, None]
    m = np.arange(P)[None, :]
    s = np.arange(SLOT)[None, :]
    part = {
        "mean": np.full((P, P), 1.0 / C),
        "spread_ln": np.full((P, P), 1.0 / SLOT),
        "down": np.concatenate([s == P // S8 * c + p // S8 for c in range(2)], 1),
        "all": np.concatenate([m % RH == P // S8 * c + p // S8 for c in range(2)], 1),
        "up": np.concatenate([p % RH == P // S8 * c + m // S8 for c in range(2)], 1),
        "same": p % RH == m % RH, "head_mean": (p % RH == m % RH) / S8,
        "narrow_sm": np.concatenate([(p % SLOT == HD) & (s % NH == 4 * t + p // SLOT) for t in range(TQ)], 1),
        "spread_sm": np.concatenate([p % SLOT == 4 * t + m // SLOT for t in range(TQ)], 1),
        "ident": p == m,
        "block": p // SLOT == np.arange(4)[None, :],
        "maskrow": np.broadcast_to(m % SLOT == HD, (P, P)),
        "eps5": np.full((P, 1), 1e-5), "eps6": np.full((P, 1), 1e-6),
        "even": (p // HD % 2 == 0) / 4.0, "odd": (p // HD % 2 == 1) / 4.0,
    }
    return np.concatenate([np.asarray(part[k], np.float32) for k in CONST], 1)



RWKV0, PERCEIVER, DECODER, RWKV1 = range(4)
LOOPS = 4


def in_turns(first, second):
    for _ in range(LAG):
        next(first)
    alive = [second, first]
    while alive:
        for program in list(alive):
            if next(program, "end") == "end":
                alive.remove(program)


def tiles_of(loop, add):

    def norm(i, mean=True):
        if mean:
            add(f"mean{i}", 1, "V")
            yield
        add(f"var{i}", 1, "A")
        yield
        add(f"scale{i}", 1, "V")
        yield

    def rwkv():
        yield from norm(0)
        add("mix", 1, "A")
        yield
        for f in range(5):
            add(f"maa.{f}", 1, "V")
        yield
        add("k", 1, "A")
        add("td1", 1, "A")
        yield
        add("v", 1, "A")
        add("td2", 1, "A")
        yield
        add("r", 1, "A")
        add("g", 1, "V")
        yield
        add("bonus", 1, "V")
        for c in range(2):
            for j in range(4):
                add(f"vb.{c}.{j}", 1, "V")
            yield
        add("y", 1, "V")
        yield
        add("gmean", 1, "V")
        yield
        add("gvar", 1, "A")
        yield
        add("gscale", 1, "V")
        yield
        add("wo", 1, "V")
        yield
        yield from norm(1)
        add("fr", 1, "A")
        add("fk", 1, "A")
        yield
        add("fv", 1, "V")
        yield

    def softmax(a):
        add(f"den{a}", 1, "V")
        yield
        for h in range(2):
            add(f"inv{a}.{h}", 1, "V")
        yield
        add(f"o{a}", 1, "V")
        yield

    def mlp():
        for n in range(HID // P // 2):
            add(f"hid.{n}", 1, "A")
        yield
        add("down", 1, "V")
        yield

    def perceiver():
        for h in range(2):
            add(f"pq{h}", 1, "A")
        yield
        for t in range(TQ):
            add(f"pk{t}", 1, "A")
        yield
        for b in range(GB):
            add(f"pv{b}", 1, "V")
        yield
        for b in range(GB):
            for u in range(2):
                add(f"ps{b}.{u}", 4, "V")
            yield
            add(f"pm{b}", 1, "V")
            yield
            for kt in range(2):
                add(f"pt{b}.{kt}", 4, "A")
            yield
            add(f"pc{b}", 1, "A")
            yield
        yield from softmax(0)
        yield from norm(0, mean=False)
        yield from mlp()

    def decoder():
        for a in range(2):
            yield from norm(a)
            add(f"dq{a}", 1, "A")
            add(f"dk{a}", 1, "A")
            add(f"dv{a}", 1, "V")
            yield
            for b in range(GB):
                add(f"ds{a}.{b}", 4, "V")
                yield
                add(f"dt{a}.{b}", 4, "A")
                yield
                add(f"dc{a}.{b}", 1, "A")
                yield
            yield from softmax(a)
        yield from norm(2)
        yield from mlp()

    return {RWKV0: rwkv, RWKV1: rwkv, PERCEIVER: perceiver, DECODER: decoder}[loop]()


class PsumPlan:

    def __init__(self, loop):
        order = []

        def adder(s):
            return lambda name, banks, reader: order.append(((s, name), banks, reader))

        in_turns(*[tiles_of(loop, adder(s)) for s in range(STREAMS)])
        self.bank, self.fill, self.read, self.before = {}, {}, {}, {}
        self.total = {"A": 0, "V": 0}
        self.fills = len(order)
        last, at = [None] * 8, 0
        for n, (name, banks, reader) in enumerate(order):
            at = -(-at // banks) * banks % 8
            need = {}
            for k in range(at, at + banks):
                if last[k] is not None:
                    need[last[k][0]] = max(need.get(last[k][0], 0), last[k][1])
            self.total[reader] += 1
            self.bank[name], self.fill[name], self.before[name] = at, n + 1, need
            self.read[name] = (reader, self.total[reader])
            for k in range(at, at + banks):
                last[k] = self.read[name]
            at = (at + banks) % 8


class Place:

    def __init__(self, loop, it, ahead=0):
        self.loop, self.it, self.ahead = loop, it, ahead


SQUARES = (3, 1, 3, 3)
SPREADS = (3, 2, 5, 3)
NORMED = (2, 0, 3, 2)


def build_program(nc, x_in, ctx_in, state_in_, pmask_in, cross_in, ltor_in, const_in, rwkv0_in, perc_in, dec_in,
                  rwkv1_in, between, out):
    plans = [PsumPlan(loop) for loop in range(LOOPS)]
    with ExitStack() as ctx:
        def sb(name, *shape, dt=F32):
            return ctx.enter_context(nc.sbuf_tensor(name, list(shape), dt))

        class Signal:

            def __init__(self, name, per=(1, 1, 1, 1), start=1):
                self.sem, self.per, self.start = ctx.enter_context(nc.semaphore(name)), per, start

            def first(self, h):
                return self.start + ROUNDS * sum(self.per[:h.loop]) + h.ahead * self.per[h.loop]

            def before(self, h):
                assert self.start > 0
                return self.sem, h.it * self.per[h.loop] + self.first(h)

            def __call__(self, h, n=0):
                assert n < self.per[h.loop]
                return self.sem, h.it * self.per[h.loop] + (self.first(h) + n + 1)

        wa = sb("wa", P, max(RWKV_W, DEC_W))
        wb = sb("wb", P, max(RWKV_W, PERC_W))
        weights = (wa, wb, wa, wb)
        cst = sb("cst", P, CONST_W)
        up_r = sb("up_r", P, 2 * P, dt=F32R)
        ltor = sb("ltor", P, T)
        ltor_add = sb("ltor_add", P, T)
        prep = sb("prep", P, TQ + 4 * NC_)
        ps = ctx.enter_context(nc.psum_tensor("ps", [P, 8, 512], F32))

        const_loaded = ctx.enter_context(nc.semaphore("const_loaded"))
        weights_loaded = [ctx.enter_context(nc.semaphore(f"weights_loaded{k}")) for k in range(LOOPS)]
        prepared = [ctx.enter_context(nc.semaphore(f"prepared{k}")) for k in range(LOOPS)]
        filled = Signal("filled", [p.fills for p in plans])
        act_read = Signal("act_read", [p.total["A"] for p in plans])
        dve_read = Signal("dve_read", [p.total["V"] for p in plans])

        class Stream:

            ARENA = 22 * NC_ * N

            def __init__(q, s):
                q.s = s

                def own(name, *shape, dt=F32):
                    return sb(f"{name}_{s}", *shape, dt=dt)

                q.xin, q.cin = own("xin", P, NC_, N), own("cin", P, NC_, N)
                q.stin, q.st = own("stin", P, STATE_W), own("st", P, STATE_W)
                q.mcin = own("mcin", P, GB, T)
                q.pmin = own("pmin", 1, N, dt=I32)
                q.X, q.xout = own("X", P, NC_, N), own("xout", P, NC_, N)
                q.xc, q.sq = own("xc", P, NC_, N), own("sq", P, NC_, N)
                q.sd, q.rs, q.rm = own("sd", P, BLK), own("rs", P, BLK), own("rm", P, 4, BLK)
                q.mx = own("mx", P, NH)
                q.vhi, q.vlo = own("vhi", P, NC_, N, dt=F32R), own("vlo", P, NC_, N, dt=F32R)
                arena = own("arena", P, q.ARENA)
                at = [0]

                def cut(*shape):
                    size = int(np.prod(shape))
                    flat = arena[:, at[0]:at[0] + size]
                    at[0] += size
                    assert at[0] <= q.ARENA, at[0]
                    if len(shape) == 1:
                        return flat
                    names = "abc"[:len(shape)]
                    return flat.rearrange(f"p ({' '.join(names)}) -> p {' '.join(names)}",
                                          **dict(zip(names[1:], shape[1:])))

                q.ws = cut(NC_, GB, T)
                q.xap = cut(NC_ * GB, T + 1)
                q.sx = cut(NC_ * GB, T)
                q.mi = cut(NC_, N)
                q.tm = cut(N)
                q.tmb = cut(N)
                q.tw, q.e1, q.og = q.tm, q.mi.rearrange("p c (b t) -> p (c b) t", b=GB), q.mi
                q.tmp = [cut(NC_, N), cut(NC_, N)]
                q.xf = [cut(NC_, N) for _ in range(5)]
                q.tg, q.ruk = q.tmp
                q.ff = q.tmp[0]
                q.kv = [cut(S8, N), cut(S8, N)]
                q.vv, q.rr, q.g2 = q.xf[2:]
                q.kk = (q.xf[0], None, None, q.xf[1])
                q.bv = (q.xf[1], None, None, q.xf[0])
                q.yy, q.yc, q.yn = q.kk, q.xf[2], q.xf[3]
                q.ki, q.ri, q.tr, q.rl, q.k2 = q.xf
                at[0] = 0
                q.pva = cut(2 * GB, NH, SLOT)
                q.xn = cut(NC_, N)
                q.mxp = cut(TQ, P)
                q.qa = cut(TQ, N)
                q.ka = cut(TQ, 2 * GB, T)
                q.pt = cut(2, NH, T)
                q.ca = cut(TQ, N)
                q.cn = q.qa
                q.phd = q.pt.rearrange("p a b c -> p (a b c)")[:, 0:HID // P * N].rearrange(
                    "p (a n) -> p a n", n=N)
                q.qb = q.sq[:, :, :].rearrange("p c n -> p (c n)").rearrange("p (t q) -> p t q", t=TQ)
                q.pmask = q.sq[0:1, 0, :]
                q.dva = q.pva[:, 0:GB]
                at[0] = GB * NH * SLOT
                ctx_d = cut(NC_, N)
                q.mc, q.mc_add = cut(GB, T), cut(GB, T)
                at[0] = 2 * GB * NH * SLOT + NC_ * N
                q.qe, q.qo, q.ks = [cut(NC_, N) for _ in range(3)]
                q.tt = cut(NH, T)
                q.p2 = cut(NH, T)
                q.dca = cut(TQ, N)
                q.dcn = cut(TQ, N)
                q.dhd = q.tt.rearrange("p h k -> p (h k)").rearrange("p (a n) -> p a n", n=N)
                q.CX = (None, q.xn, ctx_d, None)

                def signal(name, *per, start=1):
                    return Signal(f"{name}_{s}", per or (1, 1, 1, 1), start)

                q.inputs_in = signal("inputs_in", 32, 48, 48, 32, start=0)
                q.stored = signal("stored", 16, 16, 16, 16, start=16)
                q.x_ready = signal("x_ready")
                q.xout_ready = signal("xout_ready")
                q.ctx_ready = signal("ctx_ready")
                q.masks_ready = signal("masks_ready", 0, 1, 1, 0)
                q.squared = signal("squared", *SQUARES)
                q.inverted = signal("inverted", *SQUARES)
                q.spread = signal("spread", *SPREADS)
                q.normed = signal("normed", *NORMED)
                q.state_in = signal("state_in", 2, 0, 0, 2)
                q.shifted = signal("shifted", 2, 0, 0, 2)
                q.mixed_in = signal("mixed_in", 1, 0, 0, 1)
                q.xf_ready = signal("xf_ready", 5, 0, 0, 5)
                q.decay = signal("decay", 1, 0, 0, 1)
                q.v_high = signal("v_high", 1, 0, 0, 1)
                q.v_low = signal("v_low", 1, 0, 0, 1)
                q.g_tanh = signal("g_tanh", 1, 0, 0, 1)
                q.ruk_ready = signal("ruk_ready", 1, 0, 0, 1)
                q.s0_placed = signal("s0_placed", 2, 0, 0, 2)
                q.scanned = signal("scanned", 2, 0, 0, 2)
                q.r_state = signal("r_state", 2, 0, 0, 2)
                q.gated = signal("gated", 1, 0, 0, 1)
                q.ffn_in = signal("ffn_in", 2, 0, 0, 2)
                q.ffn_sq = signal("ffn_sq", 1, 0, 0, 1)
                q.max_ready = signal("max_ready", 0, 0, 2 * GB, 0)
                q.s_add = signal("s_add", 0, 0, 2 * GB, 0)
                q.s_sub = signal("s_sub", 0, 0, 2 * GB, 0)
                q.probs = signal("probs", 0, 0, 2 * GB, 0)

        streams = [Stream(s) for s in range(STREAMS)]

        def done(h, q, name):
            reader, count = plans[h.loop].read[q.s, name]
            return (act_read if reader == "A" else dve_read)(h, count - 1)

        def full(h, q, name):
            return filled(h, plans[h.loop].fill[q.s, name] - 1)

        def const(name, i=0, w=P, rows=slice(0, P)):
            a = CONST[name][0] + i * w
            return cst[rows, a:a + w]

        def vec(pack, fields, name, i=0):
            a = fields[name][0] + i
            return pack[:, a:a + 1]

        def tile_of(h, q, name, banks=1):
            b = plans[h.loop].bank[q.s, name]
            return ps[:, b, :] if banks == 1 else ps[:, b:b + banks, :]

        def pair(h, q, name):
            return tile_of(h, q, name).rearrange("p (c n) -> p c n", c=2)

        def wide(ap, k):
            n = ap.shape[-1]
            return ap.rearrange("p (o n) -> p o n", o=1).to_broadcast([ap.shape[0], k, n])

        def inner(ap, n):
            return ap.rearrange("p (k o) -> p k o", o=1).to_broadcast([ap.shape[0], ap.shape[-1], n])

        def by_row(ap):
            return ap.rearrange("p (b t) -> p b t", b=GB)

        def run(eng, loop, program):
            with eng.Fori(0, ROUNDS) as it:
                h = Place(loop, it)
                in_turns(*[program(h, q) for q in streams])

        block = ctx.enter_context(nc.Block())

        @block.sync
        def _(sp):
            def load_weights(k, dst, src):
                sp.dma_start(dst[:, 0:src.shape[1]], src).then_inc(weights_loaded[k], 16)

            def flat(ap):
                return ap[:, :, :].rearrange("p c n -> p (c n)")

            def of_group(ap, h, q):
                names = "pabc"[:len(ap.shape) - 1]
                group = ap.rearrange(f"(r s) {' '.join(names)} -> s r {' '.join(names)}", s=STREAMS)[
                    q.s, h.ahead:][h.it if isinstance(h.it, int) else bass.ds(h.it, 1)]
                if len(group.shape) == len(ap.shape):
                    group = group.rearrange(f"o {' '.join(names)} -> (o {names[0]}) {' '.join(names[1:])}")
                return group

            def known(*waits):
                for _, value in waits:
                    if not isinstance(value, int):
                        sp.compute_val(value)

            def load(h):
                for q in streams:
                    known(q.x_ready.before(h), q.ctx_ready.before(h), q.masks_ready.before(h))
                    if h.loop > 0:
                        known(q.stored(Place(h.loop - 1, h.it, h.ahead), 15))
                for q in streams:
                    src = x_in if h.loop == 0 else between[h.loop - 1]
                    sp.wait_ge(*q.x_ready.before(h))
                    if h.loop > 0:
                        sp.wait_ge(*q.stored(Place(h.loop - 1, h.it, h.ahead), 15))
                    sp.dma_start(flat(q.xin), of_group(src, h, q)).then_inc(q.inputs_in.sem, 16)
                    sp.wait_ge(*q.ctx_ready.before(h))
                    if h.loop in (RWKV0, RWKV1):
                        sp.dma_start(q.stin[:, :], of_group(state_in_, h, q)).then_inc(q.inputs_in.sem, 16)
                    else:
                        sp.dma_start(flat(q.cin), of_group(ctx_in, h, q)).then_inc(q.inputs_in.sem, 16)
                    if h.loop == PERCEIVER:
                        sp.wait_ge(*q.masks_ready.before(h))
                        sp.dma_start(q.pmin[:, :], of_group(pmask_in, h, q)).then_inc(q.inputs_in.sem, 16)
                    if h.loop == DECODER:
                        sp.dma_start(q.mcin[:, :, :], of_group(cross_in, h, q)).then_inc(q.inputs_in.sem, 16)

            def store(h):
                known(*[q.xout_ready(h) for q in streams], (None, h.it * (STREAMS * P * NC_ * N) * 4))
                for q in streams:
                    sp.wait_ge(*q.xout_ready(h))
                    dst = out if h.loop == LOOPS - 1 else between[h.loop]
                    sp.dma_start(of_group(dst, h, q), flat(q.xout)).then_inc(q.stored.sem, 16)

            for q in streams:
                sp.sem_inc(q.stored.sem, q.stored.start)
            sp.dma_start(cst[:, :], const_in).then_inc(const_loaded, 16)
            for q in streams:
                sp.dma_start(flat(q.xin), x_in[q.s]).then_inc(q.inputs_in.sem, 16)
                sp.dma_start(q.stin[:, :], state_in_[q.s]).then_inc(q.inputs_in.sem, 16)
            load_weights(0, wa, rwkv0_in)
            load_weights(1, wb, perc_in)
            sp.dma_start(ltor[:, :], ltor_in).then_inc(const_loaded, 16)
            for loop in range(LOOPS):
                with sp.Fori(0, ROUNDS - 1) as it:
                    load(Place(loop, it, 1))
                    store(Place(loop, it))
                if loop + 1 < LOOPS:
                    load(Place(loop + 1, 0))
                store(Place(loop, ROUNDS - 1))
                if loop + 2 < LOOPS:
                    load_weights(loop + 2, weights[loop], (dec_in, rwkv1_in)[loop])
            for q in streams:
                sp.wait_ge(*q.stored(Place(LOOPS - 1, ROUNDS - 1), 15))

        @block.tensor
        def _(pe):
            def fill(h, q, name, banks=1):
                for reader, count in plans[h.loop].before[q.s, name].items():
                    freed = act_read if reader == "A" else dve_read
                    pe.wait_ge(*freed(h, count - 1))
                return tile_of(h, q, name, banks)

            def mm(o, lhsT, rhs, start=True, stop=True):
                return pe.matmul(o, lhsT, rhs, start=start, stop=stop, skip_group_check=True)

            def linear(o, pack, fields, name, rhs, n_out, k_tiles=NC_):
                a, w = fields[name]
                width = w // k_tiles
                for m in range(n_out):
                    for k in range(k_tiles):
                        i = mm(o[:, m], pack[:, a + k * width + m * P:a + k * width + (m + 1) * P], rhs[:, k],
                               start=(k == 0), stop=(k == k_tiles - 1))
                return i

            def narrow(o, lhs, src, k_tiles):
                for k in range(k_tiles):
                    for j in range(4):
                        i = mm(o[SLOT * j:SLOT * (j + 1), 0:BLK], lhs(k), src[:, k, j * BLK:(j + 1) * BLK],
                               start=(k == 0), stop=(k == k_tiles - 1))
                return i

            def norm(h, q, i, n, z, mean=True):
                if mean:
                    o = fill(h, q, f"mean{i}")
                    for c in range(NC_):
                        m = mm(o[:, 0:N], const("mean"), q.X[:, c], start=(c == 0), stop=(c == 1))
                    m.then_inc(filled.sem, 1)
                    yield
                o = fill(h, q, f"var{i}")
                pe.wait_ge(*q.squared(h, n))
                narrow(o, lambda k: const("mean")[:, 0:SLOT], q.sq, NC_).then_inc(filled.sem, 1)
                yield
                o = fill(h, q, f"scale{i}")
                pe.wait_ge(*q.spread(h, z))
                mm(o[:, 0:N], const("spread_ln"), q.rm[:, :, :]).then_inc(filled.sem, 1)
                yield

            def rwkv(h, q):
                w, R, order = weights[h.loop], RWKV, ORDER[h.loop // RWKV1]
                at_f = {x: order.index(x) for x in order}
                pe.wait_ge(*q.x_ready(h))
                yield from norm(h, q, 0, 0, 0)
                o = fill(h, q, "mix")
                pe.wait_ge(*q.mixed_in(h))
                a = R["w1"][0]
                for k in range(NC_):
                    mm(o[:, 0:N], w[:, a + 160 * k:a + 160 * k + P], q.mi[:, k], start=(k == 0), stop=(k == 1))
                for k in range(NC_):
                    m = mm(o[0:32, N:2 * N], w[:, a + 160 * k + P:a + 160 * (k + 1)], q.mi[:, k], start=(k == 0),
                           stop=(k == 1))
                m.then_inc(filled.sem, 1)
                yield
                for f in range(5):
                    o = fill(h, q, f"maa.{f}")
                    if f == 0:
                        pe.wait_ge(*done(h, q, "mix"))
                    a = R["w2" if f < 4 else "w2b"][0]
                    r = slice(32 * f, 32 * f + 32) if f < 4 else slice(0, 32)
                    src = q.tm if f < 4 else q.tmb
                    for c in range(NC_):
                        m = mm(o[:, c * N:(c + 1) * N], w[r, a + c * P:a + (c + 1) * P], src[r, :])
                    m.then_inc(filled.sem, 1)
                yield

                def project(x):
                    fill(h, q, x)
                    pe.wait_ge(*q.xf_ready(h, at_f[x]))
                    linear(pair(h, q, x), w, R, "W" + x, q.xf[at_f[x]], 2).then_inc(filled.sem, 1)

                project("k")
                o = fill(h, q, "td1")
                pe.wait_ge(*q.xf_ready(h, at_f["w"]))
                a = R["td1"][0]
                for k in range(NC_):
                    m = mm(o[0:64, 0:N], w[:, a + 64 * k:a + 64 * (k + 1)], q.xf[at_f["w"]][:, k], start=(k == 0),
                           stop=(k == 1))
                m.then_inc(filled.sem, 1)
                yield
                project("v")
                o = fill(h, q, "td2")
                pe.wait_ge(*done(h, q, "td1"))
                a = R["td2"][0]
                for c in range(NC_):
                    m = mm(o[:, c * N:(c + 1) * N], w[0:64, a + c * P:a + (c + 1) * P], q.tw[0:64, :])
                m.then_inc(filled.sem, 1)
                yield
                project("r")
                project("g")
                yield
                o = fill(h, q, "bonus")
                pe.wait_ge(*q.ruk_ready(h))
                for c in range(NC_):
                    m = mm(o[:, 0:N], const("all", c), q.ruk[:, c], start=(c == 0), stop=(c == 1))
                m.then_inc(filled.sem, 1)
                pe.wait_ge(*q.v_high(h))
                pe.wait_ge(*q.v_low(h))
                for c in range(NC_):
                    for j in range(4):
                        o = fill(h, q, f"vb.{c}.{j}")
                        r = slice(RH * j, RH * (j + 1))
                        for n, part in enumerate((q.vhi, q.vlo)):
                            m = mm(o, up_r[r, c * P:(c + 1) * P], part[r, :, :], start=(n == 0), stop=(n == 1))
                        m.then_inc(filled.sem, 1)
                    yield
                fill(h, q, "y")
                o = pair(h, q, "y")
                for c in range(NC_):
                    pe.wait_ge(*q.r_state(h, c))
                    for j in range(4):
                        m = mm(o[RH * j:RH * (j + 1)], const("down", c, RH), q.kv[c][:, j::4, :], start=(c == 0),
                               stop=(c == 1))
                m.then_inc(filled.sem, 1)
                yield
                o = fill(h, q, "gmean")
                pe.wait_ge(*done(h, q, "y"))
                for c in range(NC_):
                    m = mm(o[:, 0:N], const("head_mean"), q.yy[h.loop][:, c], start=(c == 0), stop=(c == 1))
                m.then_inc(filled.sem, 1)
                yield
                o = fill(h, q, "gvar")
                pe.wait_ge(*q.squared(h, 1))
                narrow(o, lambda k: const("head_mean")[:, 0:SLOT], q.sq, NC_).then_inc(filled.sem, 1)
                yield
                o = fill(h, q, "gscale")
                pe.wait_ge(*q.spread(h, 1))
                mm(o[:, 0:N], const("same"), q.rm[:, :, :]).then_inc(filled.sem, 1)
                yield
                fill(h, q, "wo")
                pe.wait_ge(*q.gated(h))
                linear(pair(h, q, "wo"), w, R, "Wo", q.og, 2).then_inc(filled.sem, 1)
                yield
                pe.wait_ge(*done(h, q, "wo"))
                yield from norm(h, q, 1, 2, 2)
                fill(h, q, "fr")
                pe.wait_ge(*q.ffn_in(h, 0))
                linear(pair(h, q, "fr"), w, R, "Fr", q.ri, 2).then_inc(filled.sem, 1)
                fill(h, q, "fk")
                pe.wait_ge(*q.ffn_in(h, 1))
                linear(pair(h, q, "fk"), w, R, "Fk", q.ki, 2).then_inc(filled.sem, 1)
                yield
                fill(h, q, "fv")
                pe.wait_ge(*q.ffn_sq(h))
                linear(pair(h, q, "fv"), w, R, "Fv", q.k2, 2).then_inc(filled.sem, 1)
                yield

            def softmax_out(h, q, a, z, ready, ca, cn, fields, name):
                o = fill(h, q, f"den{a}")
                pe.wait_ge(*done(h, q, ready))
                narrow(o, lambda k: const("narrow_sm", k, SLOT), ca, TQ).then_inc(filled.sem, 1)
                yield
                for n in range(2):
                    fill(h, q, f"inv{a}.{n}")
                    if n == 0:
                        pe.wait_ge(*q.spread(h, z))
                    o = pair(h, q, f"inv{a}.{n}")
                    for t in range(2):
                        m = mm(o[:, t], const("spread_sm", 2 * n + t), q.rm[:, :, :])
                    m.then_inc(filled.sem, 1)
                yield
                fill(h, q, f"o{a}")
                pe.wait_ge(*done(h, q, f"inv{a}.1"))
                linear(pair(h, q, f"o{a}"), weights[h.loop], fields, name, cn, 2, k_tiles=TQ).then_inc(filled.sem, 1)
                yield

            def mlp(h, q, fields, hd):
                pack = weights[h.loop]
                a = fields["m1"][0]
                for n in range(HID // P // 2):
                    fill(h, q, f"hid.{n}")
                    o = pair(h, q, f"hid.{n}")
                    for e in range(2):
                        for k in range(NC_):
                            w0 = a + k * HID + (2 * n + e) * P
                            i = mm(o[:, e], pack[:, w0:w0 + P], q.xn[:, k], start=(k == 0), stop=(k == 1))
                    i.then_inc(filled.sem, 1)
                yield
                fill(h, q, "down")
                pe.wait_ge(*done(h, q, "hid.3"))
                linear(pair(h, q, "down"), pack, fields, "m2", hd, 2, k_tiles=HID // P).then_inc(filled.sem, 1)
                yield

            def values(h, q, name, src, fields, wname):
                fill(h, q, name)
                o = pair(h, q, name)
                a = fields[wname][0]
                for s, (buf, b) in enumerate(src):
                    for k in range(NC_):
                        m = mm(o[:, s], buf[:, k, b * T:(b + 1) * T], weights[h.loop][:, a + k * C:a + (k + 1) * C],
                               start=(k == 0), stop=(k == 1))
                m.then_inc(filled.sem, 1)

            def perceiver(h, q):
                w = weights[h.loop]
                pe.wait_ge(*q.x_ready(h))
                a = PERC["q"][0]
                for n in range(2):
                    fill(h, q, f"pq{n}")
                    o = pair(h, q, f"pq{n}")
                    for t in range(2):
                        for k in range(NC_):
                            w0 = a + k * TQ * P + (2 * n + t) * P
                            m = mm(o[:, t], w[:, w0:w0 + P], q.X[:, k], start=(k == 0), stop=(k == 1))
                    m.then_inc(filled.sem, 1)
                yield
                a = PERC["k"][0]
                pe.wait_ge(*q.ctx_ready(h))
                pe.wait_ge(*q.masks_ready(h))
                for t in range(TQ):
                    fill(h, q, f"pk{t}")
                    o = pair(h, q, f"pk{t}")
                    for s, buf in enumerate((q.CX[h.loop], q.X)):
                        for k in range(NC_):
                            w0 = a + k * TQ * P + t * P
                            m = mm(o[:, s], w[:, w0:w0 + P], buf[:, k], start=(k == 0), stop=(s == 1 and k == 1))
                        if s == 0:
                            mm(o[:, s], const("maskrow", rows=slice(0, 1)), q.pmask, start=False)
                    m.then_inc(filled.sem, 1)
                yield
                for b in range(GB):
                    values(h, q, f"pv{b}", ((q.CX[h.loop], b), (q.X, b)), PERC, "v")
                yield
                pe.wait_ge(*done(h, q, "pq1"))
                pe.wait_ge(*done(h, q, "pk3"))
                for b in range(GB):
                    for u in range(2):
                        o = fill(h, q, f"ps{b}.{u}", 4)
                        for t in range(2):
                            for j in range(4):
                                r = slice(SLOT * j, SLOT * (j + 1))
                                m = mm(o[:, j, t * 2 * T:(t + 1) * 2 * T], q.qa[r, 2 * u + t, b * T:(b + 1) * T],
                                       q.ka[r, 2 * u + t, 2 * b:2 * b + 2, :])
                        m.then_inc(filled.sem, 1)
                    yield
                    o = fill(h, q, f"pm{b}")
                    pe.wait_ge(*done(h, q, f"ps{b}.1"))
                    for t in range(TQ):
                        m = pe.transpose(o[:, t * T:(t + 1) * T], q.mxp[:, t, :], const("ident"))
                    m.then_inc(filled.sem, 1)
                    yield
                    for kt in range(2):
                        o = fill(h, q, f"pt{b}.{kt}", 4)
                        if kt == 0:
                            pe.wait_ge(*done(h, q, f"pm{b}"))
                        for t in range(TQ):
                            for j in range(4):
                                r = slice(SLOT * j, SLOT * (j + 1))
                                m = mm(o[:, j, t * T:(t + 1) * T], q.ka[r, t, 2 * b + kt, :], q.qb[r, t, :])
                        m.then_inc(filled.sem, 1)
                    yield
                    o = fill(h, q, f"pc{b}")
                    pe.wait_ge(*done(h, q, f"pv{b}"))
                    pe.wait_ge(*done(h, q, f"pt{b}.1"))
                    for t in range(TQ):
                        for kt in range(2):
                            for j in range(4):
                                m = mm(o[SLOT * j:SLOT * (j + 1), t * T:(t + 1) * T],
                                       q.pva[:, 2 * b + kt, 4 * t + j, :], q.pt[:, kt, 4 * j + t, :],
                                       start=(kt == 0), stop=(kt == 1))
                    m.then_inc(filled.sem, 1)
                    yield
                yield from softmax_out(h, q, 0, 0, "pc1", q.ca, q.cn, PERC, "o")
                yield from norm(h, q, 0, 0, 1, mean=False)
                pe.wait_ge(*done(h, q, "scale0"))
                yield from mlp(h, q, PERC, q.phd)

            def decoder(h, q):
                for a in range(2):
                    pe.wait_ge(*(q.x_ready(h) if a == 0 else done(h, q, "o0")))
                    yield from norm(h, q, a, a, 2 * a)
                    src = q.xn if a == 0 else q.CX[h.loop]
                    pe.wait_ge(*q.normed(h, a))
                    if a == 1:
                        pe.wait_ge(*q.ctx_ready(h))
                    fill(h, q, f"dq{a}")
                    linear(pair(h, q, f"dq{a}"), weights[h.loop], DEC, f"q{a}", q.xn, 2).then_inc(filled.sem, 1)
                    fill(h, q, f"dk{a}")
                    linear(pair(h, q, f"dk{a}"), weights[h.loop], DEC, f"k{a}", src, 2).then_inc(filled.sem, 1)
                    values(h, q, f"dv{a}", ((src, 0), (src, 1)), DEC, f"v{a}")
                    yield
                    pe.wait_ge(*done(h, q, f"dq{a}"))
                    pe.wait_ge(*done(h, q, f"dk{a}"))
                    for b in range(GB):
                        o = fill(h, q, f"ds{a}.{b}", 4)
                        for t in range(TQ):
                            for j in range(4):
                                r = slice(SLOT * j, SLOT * (j + 1))
                                m = mm(o[:, j, t * T:(t + 1) * T],
                                       (q.qe, q.qo)[t % 2][r, t // 2, b * T:(b + 1) * T],
                                       q.ks[r, t // 2, b * T:(b + 1) * T])
                        m.then_inc(filled.sem, 1)
                        yield
                        o = fill(h, q, f"dt{a}.{b}", 4)
                        pe.wait_ge(*q.probs(h, GB * a + b))
                        for n in range(NH):
                            m = pe.transpose(o[:, n // 4, (n % 4) * T:(n % 4 + 1) * T], q.tt[:, n, :], const("ident"))
                        m.then_inc(filled.sem, 1)
                        yield
                        o = fill(h, q, f"dc{a}.{b}")
                        pe.wait_ge(*done(h, q, f"dt{a}.{b}"))
                        if b == 0:
                            pe.wait_ge(*done(h, q, f"dv{a}"))
                        for t in range(TQ):
                            for j in range(4):
                                n = 8 * (t // 2) + 2 * j + t % 2
                                m = mm(o[SLOT * j:SLOT * (j + 1), t * T:(t + 1) * T], q.dva[:, b, n, :],
                                       q.p2[:, 4 * j + t, :])
                        m.then_inc(filled.sem, 1)
                        yield
                    yield from softmax_out(h, q, a, 2 * a + 1, f"dc{a}.1", q.dca, q.dcn, DEC, f"o{a}")
                pe.wait_ge(*done(h, q, "o1"))
                yield from norm(h, q, 2, 2, 4)
                pe.wait_ge(*q.normed(h, 2))
                yield from mlp(h, q, DEC, q.dhd)

            pe.wait_ge(const_loaded, 32)
            pe.sem_inc(filled.sem, filled.start)
            for loop, program in enumerate((rwkv, perceiver, decoder, rwkv)):
                pe.wait_ge(weights_loaded[loop], 16)
                pe.wait_ge(prepared[loop], 2 if loop == 0 else 1)

                def from_start(h, q, program=program):
                    if q.s == 0:
                        pe.wait_ge(*act_read.before(h))
                        pe.wait_ge(*dve_read.before(h))
                    yield from program(h, q)

                run(pe, loop, from_start)

        @block.scalar
        def _(act):
            def f(o, i, fn, **kw):
                return nc.scalar.activation(o, i, fn, **kw)

            def norm(h, q, i, bias, dst, src=None, mean=True):
                if mean:
                    act.wait_ge(*done(h, q, f"mean{i}"))
                f(q.sq[:, :, :], q.xc[:, :, :], ACT.Square).then_inc(q.squared.sem, 1)
                if mean:
                    yield
                act.wait_ge(*full(h, q, f"var{i}"))
                f(q.sd[:, :], tile_of(h, q, f"var{i}")[:, 0:BLK], ACT.Sqrt,
                  bias=const("eps5" if mean else "eps6", w=1)).then_inc(act_read.sem, 1)
                yield
                if bias is not None:
                    act.wait_ge(*done(h, q, f"scale{i}"))
                    for c in range(NC_):
                        m = f(dst(c), dst(c), ACT.Identity, bias=bias(c))
                    m.then_inc(q.normed.sem, 1)
                yield

            def padded(q):
                return lambda c: q.xap[:, c * GB:(c + 1) * GB, 1:T + 1]

            def rwkv(h, q):
                w, R = weights[h.loop], RWKV

                def state(part):
                    a = (1 - part) * NC_ * GB
                    f(q.xap[:, :, 0:1], q.st[:, a:a + NC_ * GB].rearrange("p (c o) -> p c o", o=1),
                      ACT.Copy).then_inc(q.state_in.sem, 1)

                act.wait_ge(*q.xout_ready.before(h))
                act.wait_ge(*q.inputs_in(h, 31))
                f(q.st[:, :], q.stin[:, :], ACT.Copy).then_inc(q.ctx_ready.sem, 1)
                act.wait_ge(*q.ctx_ready(h))
                state(0)
                for c in range(NC_):
                    a = 2 * NC_ * GB + c * GB * S8
                    f(q.kv[c].rearrange("p j (b t) -> p j b t", b=GB)[:, :, :, 0],
                      q.st[:, a:a + GB * S8].rearrange("p (j b) -> p j b", b=GB), ACT.Copy).then_inc(
                        q.s0_placed.sem, 1)
                yield from norm(h, q, 0, lambda c: vec(w, R, "ln1_b", c), padded(q))
                o = tile_of(h, q, "mix")
                act.wait_ge(*full(h, q, "mix"))
                f(q.tm, o[:, 0:N], ACT.Tanh)
                f(q.tmb[0:32, :], o[0:32, N:2 * N], ACT.Tanh).then_inc(act_read.sem, 1)
                yield
                yield

                def take(x, dst):
                    act.wait_ge(*full(h, q, x))
                    f(dst, pair(h, q, x), ACT.Copy).then_inc(act_read.sem, 1)

                take("k", q.kk[h.loop])
                act.wait_ge(*full(h, q, "td1"))
                f(q.tw[0:64, :], tile_of(h, q, "td1")[0:64, 0:N], ACT.Tanh).then_inc(act_read.sem, 1)
                yield
                act.wait_ge(*full(h, q, "v"))
                f(q.vhi[:, :, :], pair(h, q, "v"), ACT.Copy).then_inc(q.v_high.sem, 1)
                take("v", q.vv)
                act.wait_ge(*full(h, q, "td2"))
                for c in range(NC_):
                    m = f(q.e1[:, c * GB:(c + 1) * GB, :].rearrange("p b t -> p (b t)"), pair(h, q, "td2")[:, c],
                          ACT.Exp, bias=vec(w, R, "td", c))
                m.then_inc(act_read.sem, 1)
                act.wait_ge(*done(h, q, "td2"))
                f(q.ws[:, :, :, 1:T].rearrange("p c b t -> p (c b) t"), q.e1[:, :, 0:T - 1], ACT.Exp,
                  scale=-1.0).then_inc(q.decay.sem, 1)
                yield
                take("r", q.rr)
                act.wait_ge(*full(h, q, "g"))
                f(q.tg, pair(h, q, "g"), ACT.Tanh, scale=0.5).then_inc(q.g_tanh.sem, 1)
                yield
                yield
                yield
                yield
                act.wait_ge(*done(h, q, "gmean"))
                f(q.sq[:, :, :], q.yc, ACT.Square).then_inc(q.squared.sem, 1)
                yield
                act.wait_ge(*full(h, q, "gvar"))
                f(q.sd[:, :], tile_of(h, q, "gvar")[:, 0:BLK], ACT.Sqrt, bias=const("eps5", w=1)).then_inc(
                    act_read.sem, 1)
                yield
                yield
                yield
                act.wait_ge(*done(h, q, "wo"))
                state(1)
                yield from norm(h, q, 1, lambda c: vec(w, R, "ln2_b", c), padded(q))
                act.wait_ge(*full(h, q, "fr"))
                f(q.tr, pair(h, q, "fr"), ACT.Tanh, scale=0.5).then_inc(act_read.sem, 1)
                act.wait_ge(*full(h, q, "fk"))
                f(q.rl, pair(h, q, "fk"), ACT.Relu).then_inc(act_read.sem, 1)
                act.wait_ge(*done(h, q, "fk"))
                f(q.k2, q.rl, ACT.Square).then_inc(q.ffn_sq.sem, 1)
                yield
                yield

            def mlp(h, q, fields, hd):
                for n in range(HID // P // 2):
                    act.wait_ge(*full(h, q, f"hid.{n}"))
                    for e in range(2):
                        i = f(hd[:, 2 * n + e], pair(h, q, f"hid.{n}")[:, e], ACT.Gelu_apprx_tanh,
                              bias=vec(weights[h.loop], fields, "b1", 2 * n + e))
                    i.then_inc(act_read.sem, 1)
                yield
                yield

            def heads_out(h, q, name, b, ca):
                act.wait_ge(*full(h, q, name))
                f(ca[:, :, b * T:(b + 1) * T], tile_of(h, q, name).rearrange("p (t q) -> p t q", t=TQ),
                  ACT.Copy).then_inc(act_read.sem, 1)

            def take_context(h, q):
                act.wait_ge(*q.xout_ready.before(h))
                act.wait_ge(*q.inputs_in(h, 47))
                if h.loop == DECODER:
                    f(q.mc, q.mcin[:, :, :], ACT.Copy)
                f(q.CX[h.loop], q.cin[:, :, :], ACT.Copy).then_inc(q.ctx_ready.sem, 1)

            def perceiver(h, q):
                w = weights[h.loop]
                take_context(h, q)
                for n in range(2):
                    act.wait_ge(*full(h, q, f"pq{n}"))
                    for t in range(2):
                        m = f(q.qa[:, 2 * n + t], pair(h, q, f"pq{n}")[:, t], ACT.Identity, scale=1.0 / HD,
                              bias=prep[:, 2 * n + t:2 * n + t + 1])
                    m.then_inc(act_read.sem, 1)
                yield
                for t in range(TQ):
                    act.wait_ge(*full(h, q, f"pk{t}"))
                    for s in range(2):
                        m = f(q.ka[:, t, s::2, :], by_row(pair(h, q, f"pk{t}")[:, s]), ACT.Identity,
                              bias=vec(w, PERC, "kb", t))
                    m.then_inc(act_read.sem, 1)
                yield
                yield
                for b in range(GB):
                    yield
                    yield
                    for kt in range(2):
                        act.wait_ge(*full(h, q, f"pt{b}.{kt}"))
                        f(q.pt[:, kt].rearrange("p h q -> p (h q)"),
                          tile_of(h, q, f"pt{b}.{kt}", 4).rearrange("p j n -> p (j n)"), ACT.Exp).then_inc(
                            act_read.sem, 1)
                    yield
                    heads_out(h, q, f"pc{b}", b, q.ca)
                    yield
                yield
                yield
                act.wait_ge(*done(h, q, "o0"))
                yield
                yield from norm(h, q, 0, None, None, mean=False)
                yield from mlp(h, q, PERC, q.phd)

            def decoder(h, q):
                w = weights[h.loop]
                take_context(h, q)

                def plain(c):
                    return q.xn[:, c]

                for a in range(2):
                    yield from norm(h, q, a, lambda c: vec(w, DEC, f"ln{1 + a}_b", c), plain)
                    act.wait_ge(*full(h, q, f"dq{a}"))
                    for c in range(NC_):
                        for e, (dst, mask) in enumerate(((q.qe, "even"), (q.qo, "odd"))):
                            n = TQ + (2 * a + e) * NC_ + c
                            m = f(dst[:, c], pair(h, q, f"dq{a}")[:, c], ACT.Identity, scale=const(mask, w=1),
                                  bias=prep[:, n:n + 1])
                    m.then_inc(act_read.sem, 1)
                    act.wait_ge(*full(h, q, f"dk{a}"))
                    for c in range(NC_):
                        m = f(q.ks[:, c], pair(h, q, f"dk{a}")[:, c], ACT.Identity, bias=vec(w, DEC, f"kb{a}", c))
                    m.then_inc(act_read.sem, 1)
                    yield
                    for b in range(GB):
                        act.wait_ge(*q.s_sub(h, GB * a + b))
                        f(q.tt, q.tt, ACT.Exp).then_inc(q.probs.sem, 1)
                        yield
                        act.wait_ge(*full(h, q, f"dt{a}.{b}"))
                        f(q.p2.rearrange("p h q -> p (h q)"),
                          tile_of(h, q, f"dt{a}.{b}", 4).rearrange("p j n -> p (j n)"), ACT.Copy).then_inc(
                            act_read.sem, 1)
                        yield
                        heads_out(h, q, f"dc{a}.{b}", b, q.dca)
                        yield
                    yield
                    yield
                    yield
                yield from norm(h, q, 2, lambda c: vec(w, DEC, "ln3_b", c), plain)
                yield from mlp(h, q, DEC, q.dhd)

            act.sem_inc(act_read.sem, act_read.start)
            for q in streams:
                for signal in (q.ctx_ready, q.squared, q.normed, q.state_in, q.decay, q.v_high, q.g_tanh, q.s0_placed,
                               q.ffn_sq, q.probs):
                    act.sem_inc(signal.sem, signal.start)
            act.wait_ge(const_loaded, 32)
            for loop, program in enumerate((rwkv, perceiver, decoder, rwkv)):
                act.wait_ge(weights_loaded[loop], 16)
                if loop == 0:
                    f(up_r[:, :], const("up", w=2 * P), ACT.Copy).then_inc(prepared[0], 1)
                act.wait_ge(prepared[loop], 2 if loop == 0 else 1)
                run(act, loop, program)

        @block.vector
        def _(dve):
            V = nc.vector

            def spread_out(h, q):
                V.tensor_tensor(q.rm[:, :, :], wide(q.rs[:, :], 4), inner(const("block", w=4), BLK),
                                ALU.mult).then_inc(q.spread.sem, 1)

            def norm(h, q, i, n, weight, dst, mean=True):
                if mean:
                    dve.wait_ge(*full(h, q, f"mean{i}"))
                    V.tensor_tensor(q.xc[:, :, :], q.X[:, :, :], wide(tile_of(h, q, f"mean{i}")[:, 0:N], NC_),
                                    ALU.subtract).then_inc(dve_read.sem, 1)
                    yield
                dve.wait_ge(*done(h, q, f"var{i}"))
                V.reciprocal(q.rs[:, :], q.sd[:, :]).then_inc(q.inverted.sem, 1)
                dve.wait_ge(*q.inverted(h, n))
                spread_out(h, q)
                yield
                dve.wait_ge(*full(h, q, f"scale{i}"))
                for c in range(NC_):
                    m = V.scalar_tensor_tensor(dst(c), by_row(q.xc[:, c]), weight(c),
                                               by_row(tile_of(h, q, f"scale{i}")[:, 0:N]), ALU.mult, ALU.mult)
                m.then_inc(dve_read.sem, 1)

            def take_input(h, q, n):
                dve.wait_ge(*q.inputs_in(h, n - 1))
                V.tensor_copy(q.X[:, :, :], q.xin[:, :, :]).then_inc(q.x_ready.sem, 1)
                dve.wait_ge(*q.x_ready(h))

            def rwkv(h, q):
                w, R = weights[h.loop], RWKV

                def sxc(c):
                    return q.sx[:, c * GB:(c + 1) * GB, :]

                def xac(c):
                    return q.xap[:, c * GB:(c + 1) * GB, 1:T + 1]

                def shift(n):
                    dve.wait_ge(*q.normed(h, n))
                    dve.wait_ge(*q.state_in(h, n))
                    V.tensor_tensor(q.sx, q.xap[:, :, 0:T], q.xap[:, :, 1:T + 1], ALU.subtract).then_inc(
                        q.shifted.sem, 1)
                    dve.wait_ge(*q.shifted(h, n))

                take_input(h, q, 32)
                yield from norm(h, q, 0, 0, lambda c: vec(w, R, "ln1_w", c), xac)
                yield
                shift(0)
                for c in range(NC_):
                    m = V.scalar_tensor_tensor(by_row(q.mi[:, c]), sxc(c), vec(w, R, "maa_x", c), xac(c), ALU.mult,
                                               ALU.add)
                m.then_inc(q.mixed_in.sem, 1)
                yield
                for n in range(5):
                    dve.wait_ge(*full(h, q, f"maa.{n}"))
                    if n >= 2:
                        dve.wait_ge(*q.xf_ready(h, n - 2))
                    for c in range(NC_):
                        m = V.scalar_tensor_tensor(by_row(q.tmp[n % 2][:, c]), by_row(pair(h, q, f"maa.{n}")[:, c]),
                                                   vec(w, R, "maa", 2 * n + c), sxc(c), ALU.add, ALU.mult)
                    m.then_inc(dve_read.sem, 1)
                yield
                yield
                yield
                dve.wait_ge(*done(h, q, "r"))
                dve.wait_ge(*done(h, q, "k"))
                for c in range(NC_):
                    m = V.scalar_tensor_tensor(q.ruk[:, c], q.rr[:, c], vec(w, R, "u", c), q.kk[h.loop][:, c], ALU.mult,
                                               ALU.mult)
                m.then_inc(q.ruk_ready.sem, 1)
                dve.wait_ge(*full(h, q, "g"))
                dve.wait_ge(*q.g_tanh(h))
                V.scalar_tensor_tensor(q.g2, q.tg, 1.0, pair(h, q, "g"), ALU.add, ALU.mult).then_inc(dve_read.sem, 1)
                yield
                dve.wait_ge(*full(h, q, "bonus"))
                dve.wait_ge(*done(h, q, "v"))
                V.tensor_tensor(q.bv[h.loop], q.vv, wide(tile_of(h, q, "bonus")[:, 0:N], 2), ALU.mult).then_inc(
                    dve_read.sem, 1)
                for c in range(NC_):
                    for j in range(4):
                        dve.wait_ge(*full(h, q, f"vb.{c}.{j}"))
                        V.tensor_tensor(
                            q.kv[c][:, j::4].rearrange("p j (b t) -> p j b t", b=GB)[:, :, :, 1:T],
                            by_row(q.kk[h.loop][:, c])[:, :, 0:T - 1].rearrange("p (o b) t -> p o b t", o=1).to_broadcast(
                                [P, 2, GB, T - 1]),
                            tile_of(h, q, f"vb.{c}.{j}").rearrange("p (j b t) -> p j b t", j=2, b=GB)[:, :, :,
                                                                                                      0:T - 1],
                            ALU.mult).then_inc(dve_read.sem, 1)
                    dve.wait_ge(*done(h, q, f"vb.{c}.3"))
                    dve.wait_ge(*q.s0_placed(h, c))
                    dve.wait_ge(*q.decay(h))
                    for j in range(S8):
                        m = V.tensor_tensor_scan(q.kv[c][:, j], q.ws[:, c].rearrange("p b t -> p (b t)"),
                                                 q.kv[c][:, j], 0.0, ALU.mult, ALU.add)
                    m.then_inc(q.scanned.sem, 1)
                    dve.wait_ge(*q.scanned(h, c))
                    V.tensor_tensor(q.kv[c], q.kv[c], wide(q.rr[:, c], S8), ALU.mult).then_inc(q.r_state.sem, 1)
                    yield
                dve.wait_ge(*full(h, q, "y"))
                dve.wait_ge(*done(h, q, "bonus"))
                V.tensor_tensor(q.yy[h.loop], q.bv[h.loop], pair(h, q, "y"), ALU.add).then_inc(dve_read.sem, 1)
                yield
                dve.wait_ge(*full(h, q, "gmean"))
                dve.wait_ge(*done(h, q, "y"))
                V.tensor_tensor(q.yc, q.yy[h.loop], wide(tile_of(h, q, "gmean")[:, 0:N], 2), ALU.subtract).then_inc(
                    dve_read.sem, 1)
                yield
                dve.wait_ge(*done(h, q, "gvar"))
                V.reciprocal(q.rs[:, :], q.sd[:, :]).then_inc(q.inverted.sem, 1)
                dve.wait_ge(*q.inverted(h, 1))
                spread_out(h, q)
                yield
                dve.wait_ge(*full(h, q, "gscale"))
                for c in range(NC_):
                    m = V.scalar_tensor_tensor(q.yn[:, c], q.yc[:, c], vec(w, R, "gn_w", c),
                                               tile_of(h, q, "gscale")[:, 0:N], ALU.mult, ALU.mult)
                m.then_inc(dve_read.sem, 1)
                dve.wait_ge(*done(h, q, "gscale"))
                for c in range(NC_):
                    m = V.scalar_tensor_tensor(q.og[:, c], q.yn[:, c], vec(w, R, "gn_b", c), q.g2[:, c], ALU.add,
                                               ALU.mult)
                m.then_inc(q.gated.sem, 1)
                yield
                dve.wait_ge(*full(h, q, "wo"))
                V.scalar_tensor_tensor(q.X[:, :, :], pair(h, q, "wo"), 0.5, q.X[:, :, :], ALU.mult,
                                       ALU.add).then_inc(dve_read.sem, 1)
                dve.wait_ge(*done(h, q, "wo"))
                yield
                yield from norm(h, q, 1, 2, lambda c: vec(w, R, "ln2_w", c), xac)
                yield
                shift(1)
                for dst, v in ((q.ri, "fr"), (q.ki, "fk")):
                    for c in range(NC_):
                        m = V.scalar_tensor_tensor(by_row(dst[:, c]), sxc(c), vec(w, R, v, c), xac(c), ALU.mult,
                                                   ALU.add)
                    m.then_inc(q.ffn_in.sem, 1)
                yield
                dve.wait_ge(*full(h, q, "fv"))
                dve.wait_ge(*done(h, q, "fr"))
                V.scalar_tensor_tensor(q.ff, q.tr, 1.0, pair(h, q, "fv"), ALU.add, ALU.mult).then_inc(
                    dve_read.sem, 1)
                dve.wait_ge(*done(h, q, "fv"))
                dve.wait_ge(*q.stored.before(h))
                V.scalar_tensor_tensor(q.xout[:, :, :], q.ff, 0.5, q.X[:, :, :], ALU.mult, ALU.add).then_inc(
                    q.xout_ready.sem, 1)
                yield

            def softmax_out(h, q, a, z, ca, cn, fields, bias, dst):
                dve.wait_ge(*full(h, q, f"den{a}"))
                V.reciprocal(q.rs[:, :], tile_of(h, q, f"den{a}")[:, 0:BLK]).then_inc(dve_read.sem, 1)
                dve.wait_ge(*done(h, q, f"den{a}"))
                spread_out(h, q)
                yield
                for n in range(2):
                    dve.wait_ge(*full(h, q, f"inv{a}.{n}"))
                    V.tensor_tensor(cn[:, 2 * n:2 * n + 2], ca[:, 2 * n:2 * n + 2], pair(h, q, f"inv{a}.{n}"),
                                    ALU.mult).then_inc(dve_read.sem, 1)
                yield
                add_out(h, q, f"o{a}", fields, bias, dst).then_inc(dve_read.sem, 1)
                dve.wait_ge(*done(h, q, f"o{a}"))
                yield

            def add_out(h, q, name, fields, bias, dst):
                dve.wait_ge(*full(h, q, name))
                for c in range(NC_):
                    m = V.scalar_tensor_tensor(dst[:, c], pair(h, q, name)[:, c],
                                               vec(weights[h.loop], fields, bias, c), q.X[:, c], ALU.add, ALU.add)
                return m

            def mlp(h, q, fields):
                yield
                dve.wait_ge(*q.stored.before(h))
                add_out(h, q, "down", fields, "b2", q.xout).then_inc(dve_read.sem, 1)
                dve.wait_ge(*done(h, q, "down"))
                dve.sem_inc(q.xout_ready.sem, 1)
                yield

            def values(h, q, name, va, slots, fields, vb):
                dve.wait_ge(*full(h, q, name))
                o = tile_of(h, q, name).rearrange("p (s h d) -> p s h d", s=2, h=NH)
                a = fields[vb][0]
                for s in range(2):
                    m = V.tensor_tensor(va[:, slots + s, :, 0:HD], o[:, s],
                                        weights[h.loop][:, a:a + C].rearrange("p (h d) -> p h d", h=NH), ALU.add)
                m.then_inc(dve_read.sem, 1)

            def perceiver(h, q):
                take_input(h, q, 48)
                V.tensor_scalar(q.pmask, q.pmin[:, :], 0, MASKED, ALU.is_equal, ALU.mult).then_inc(
                    q.masks_ready.sem, 1)
                yield
                yield
                for b in range(GB):
                    values(h, q, f"pv{b}", q.pva, 2 * b, PERC, "vb")
                yield
                for b in range(GB):
                    for u in range(2):
                        dve.wait_ge(*full(h, q, f"ps{b}.{u}"))
                        V.tensor_reduce(q.mxp[:, 2 * u:2 * u + 2, HD + 1::SLOT].rearrange("p t j -> p j t"),
                                        tile_of(h, q, f"ps{b}.{u}", 4).rearrange("p j (t k) -> p j t k", t=2), AX.X,
                                        ALU.max, negate=True).then_inc(dve_read.sem, 1)
                    yield
                    dve.wait_ge(*full(h, q, f"pm{b}"))
                    if b == 0:
                        dve.wait_ge(*done(h, q, "pq1"))
                    else:
                        dve.wait_ge(*full(h, q, f"pt{b - 1}.1"))
                    V.tensor_tensor(q.qb, q.qa[:, :, b * T:(b + 1) * T],
                                    tile_of(h, q, f"pm{b}").rearrange("p (t q) -> p t q", t=TQ), ALU.add).then_inc(
                        dve_read.sem, 1)
                    yield
                    yield
                    yield
                yield from softmax_out(h, q, 0, 0, q.ca, q.cn, PERC, "ob", q.xc)
                yield from norm(h, q, 0, 0, lambda c: vec(weights[h.loop], PERC, "norm_w", c),
                                lambda c: by_row(q.xn[:, c]), mean=False)
                yield
                yield from mlp(h, q, PERC)

            def decoder(h, q):
                w = weights[h.loop]
                take_input(h, q, 48)
                dve.wait_ge(*q.ctx_ready(h))
                V.tensor_scalar(q.mc_add, q.mc, -1.0, 10000.0, ALU.add, ALU.mult).then_inc(q.masks_ready.sem, 1)
                for a in range(2):
                    yield from norm(h, q, a, a, lambda c: vec(w, DEC, f"ln{1 + a}_w", c),
                                    lambda c: by_row(q.xn[:, c]))
                    yield
                    values(h, q, f"dv{a}", q.dva, 0, DEC, f"vb{a}")
                    yield
                    for b in range(GB):
                        m = ltor[:, :] if a == 0 else q.mc[:, b, :]
                        n = GB * a + b
                        dve.wait_ge(*full(h, q, f"ds{a}.{b}"))
                        if b > 0:
                            dve.wait_ge(*full(h, q, f"dt{a}.{b - 1}"))
                        V.tensor_tensor(q.tt, tile_of(h, q, f"ds{a}.{b}", 4).rearrange("p j (t k) -> p (j t) k", t=TQ),
                                        wide(m, NH), ALU.mult).then_inc(dve_read.sem, 1)
                        dve.wait_ge(*q.s_add(h, n))
                        V.tensor_reduce(q.mx[:, :], q.tt, AX.X, ALU.max).then_inc(q.max_ready.sem, 1)
                        dve.wait_ge(*q.max_ready(h, n))
                        V.tensor_tensor(q.tt, q.tt, inner(q.mx[:, :], T), ALU.subtract).then_inc(q.s_sub.sem, 1)
                        yield
                        yield
                        yield
                    yield from softmax_out(h, q, a, 2 * a + 1, q.dca, q.dcn, DEC, f"ob{a}", q.X)
                yield from norm(h, q, 2, 2, lambda c: vec(w, DEC, "ln3_w", c), lambda c: by_row(q.xn[:, c]))
                yield
                yield from mlp(h, q, DEC)

            dve.sem_inc(dve_read.sem, dve_read.start)
            for q in streams:
                for signal in (q.x_ready, q.xout_ready, q.masks_ready, q.inverted, q.spread, q.shifted, q.mixed_in,
                               q.ruk_ready, q.scanned, q.r_state, q.gated, q.ffn_in, q.max_ready, q.s_sub):
                    dve.sem_inc(signal.sem, signal.start)
            dve.wait_ge(const_loaded, 32)
            for loop, program in enumerate((rwkv, perceiver, decoder, rwkv)):
                dve.wait_ge(weights_loaded[loop], 16)
                w = weights[loop]
                if loop > 0:
                    for q in streams:
                        dve.wait_ge(*q.xout_ready(Place(loop - 1, ROUNDS - 1)))
                if loop == PERCEIVER:
                    a = PERC["qb"][0]
                    V.tensor_scalar(prep[:, 0:TQ], w[:, a:a + TQ], 1.0 / HD, None, ALU.mult)
                if loop == DECODER:
                    for i in range(2):
                        a = DEC[f"qb{i}"][0]
                        for e, m in enumerate(("even", "odd")):
                            s = TQ + (2 * i + e) * NC_
                            V.tensor_scalar(prep[:, s:s + NC_], w[:, a:a + NC_], const(m, w=1), None, ALU.mult)
                    V.tensor_scalar(ltor_add[:, :], ltor[:, :], -1.0, 10000.0, ALU.add, ALU.mult)
                for q in streams:
                    if loop in (RWKV0, RWKV1):
                        m = V.memset(q.ws[:, :, :, 0:1], 0.0)
                    else:
                        if loop == PERCEIVER:
                            V.memset(q.mxp, 0.0)
                        V.memset(q.pva[:, :, :, HD:HD + 1], 1.0)
                        m = V.memset(q.pva[:, :, :, HD + 1:], 0.0)
                m.then_inc(prepared[loop], 1)
                dve.wait_ge(prepared[loop], 2 if loop == 0 else 1)
                run(dve, loop, program)

        @block.gpsimd
        def _(pool):
            G = nc.gpsimd

            def rows(ap):
                return ap.rearrange("p c (b t) -> p (c b) t", b=GB)

            def rwkv(h, q):
                for _ in range(4):
                    yield
                for n in range(5):
                    pool.wait_ge(*done(h, q, f"maa.{n}"))
                    G.tensor_tensor(rows(q.xf[n]), rows(q.tmp[n % 2]), q.xap[:, :, 1:T + 1], ALU.add).then_inc(
                        q.xf_ready.sem, 1)
                yield
                yield
                pool.wait_ge(*q.v_high(h))
                pool.wait_ge(*done(h, q, "v"))
                G.tensor_tensor(q.vlo[:, :, :], q.vv, q.vhi[:, :, :].bitcast(F32), ALU.subtract).then_inc(
                    q.v_low.sem, 1)
                for _ in range(14):
                    yield

            def decoder(h, q):
                for a in range(2):
                    for _ in range(4):
                        yield
                    for b in range(GB):
                        pool.wait_ge(*done(h, q, f"ds{a}.{b}"))
                        if a == 1 and b == 0:
                            pool.wait_ge(*q.masks_ready(h))
                        m = ltor_add[:, :] if a == 0 else q.mc_add[:, b, :]
                        G.tensor_tensor(q.tt, q.tt, wide(m, NH), ALU.add).then_inc(q.s_add.sem, 1)
                        for _ in range(3):
                            yield
                    for _ in range(3):
                        yield
                for _ in range(5):
                    yield

            for q in streams:
                for signal in (q.xf_ready, q.v_low, q.s_add):
                    pool.sem_inc(signal.sem, signal.start)
            for loop, program in ((RWKV0, rwkv), (DECODER, decoder), (RWKV1, rwkv)):
                pool.wait_ge(prepared[loop], 2 if loop == 0 else 1)
                run(pool, loop, program)




HEAD_ROWS = np.array([S8 * (p % RH) + 4 * t + p // RH for t in range(NC_) for p in range(P)])


def _k_tiles(w, k=NC_):
    return np.ascontiguousarray(w.reshape(k, P, -1).transpose(1, 0, 2)).reshape(P, -1)


def _vec(v):
    return np.ascontiguousarray(v.reshape(-1, P).T)


def _rows(w):
    return np.concatenate([w, np.zeros((P - w.shape[0], w.shape[1]), np.float32)], 0)


def _pack(fields, part):
    for name, (_, width) in fields.items():
        assert part[name].shape == (P, width), (name, part[name].shape, width)
    return np.ascontiguousarray(np.concatenate([part[name] for name in fields], 1))


def _slots(w, heads, fill=None):
    out = np.zeros((w.shape[0], NH, SLOT), np.float32)
    out[:, :, :HD] = w.reshape(-1, NH, HD)[:, heads]
    if fill:
        for k, v in fill.items():
            out[:, :, k] = v
    return out.reshape(-1, NH * SLOT)


def _rwkv_pack(a, l):
    names = dict(zip(("td1", "td2", "u", "fk", "fr", "Fk", "Fr", "Fv"),
                     ("td_w1", "td_w2", "u", "ffn_maa_k", "ffn_maa_r", "Wfk", "Wfr", "Wfv") if l == 0 else
                     ("decay_w1", "decay_w2", "faaaa", "fmaa_k", "fmaa_r", "fWk", "fWr", "fWv")))
    if l == 0:
        maa = a["maa_stack"].reshape(5, C)
    else:
        maa = np.stack([a["maa_" + x] for x in ORDER[1]])
    w2 = a["maa_w2"].reshape(160, C)
    part = {
        "w1": _k_tiles(a["maa_w1"]), "w2": w2[:P], "w2b": _rows(w2[P:]), "td1": _k_tiles(a[names["td1"]]),
        "td2": _rows(a[names["td2"]]), "maa": _vec(maa), "td": _vec(a["time_decay"]), "u": _vec(a[names["u"]]),
        "fk": _vec(a[names["fk"]]), "fr": _vec(a[names["fr"]]),
    }
    part["Wr"], part["Wk"] = _k_tiles(a["Wr"].T), _k_tiles(a["Wk"].T)
    part["Wv"], part["Wg"] = _k_tiles(a["Wv"].T[:, HEAD_ROWS]), _k_tiles(a["Wg"].T[:, HEAD_ROWS])
    part["Wo"] = _k_tiles(a["Wo"].T[HEAD_ROWS])
    for w in ("Fk", "Fr", "Fv"):
        part[w] = _k_tiles(a[names[w]].T)
    for v in ("ln1_w", "ln1_b", "ln2_w", "ln2_b", "maa_x"):
        part[v] = _vec(a[v])
    for v in ("gn_w", "gn_b"):
        part[v] = _vec(a[v][HEAD_ROWS])
    return _pack(RWKV, part)


def kernel(**inputs):
    import concourse.bacc as _bacc
    from concourse.bass_utils import run_bass_kernel_spmd as _run

    a = {k: np.asarray(v) for k, v in inputs.items()}

    def layer(n):
        return {k.split("_xattn_")[1]: v for k, v in a.items() if k.startswith(f"L{n}_")}

    def tokens(v):
        v = v.reshape(GROUPS, N, NC_, P).transpose(0, 3, 2, 1)
        return np.ascontiguousarray(v).reshape(GROUPS, P, NC_ * N)

    ctxt = a["ctx_2048"]
    rows = ctxt[:, 0:2].reshape(GROUPS, GB, 2, NC_, P).transpose(0, 4, 2, 3, 1).reshape(GROUPS, P, -1)
    s0 = ctxt[:, 2:2 + S8].reshape(GROUPS, GB, NC_, P, S8).transpose(0, 3, 2, 4, 1).reshape(GROUPS, P, -1)

    plain = list(range(NH))
    paired = [8 * (t // 2) + 2 * j + t % 2 for t in range(TQ) for j in range(4)]

    def out_rows(w, heads):
        return _k_tiles(np.ascontiguousarray(_slots(np.ascontiguousarray(w.T), heads).T), TQ)

    p1 = layer(1)
    kvw = p1["kv_w"].reshape(C, NH * HD, 2)
    kvb = p1["kv_b"].reshape(NH * HD, 2)

    def all_rows(v):
        return np.ascontiguousarray(np.broadcast_to(v.reshape(1, -1), (P, v.size)))

    perc = _pack(PERC, {
        "q": _k_tiles(_slots(p1["q_w"], plain)), "k": _k_tiles(_slots(kvw[..., 0], plain)),
        "v": _k_tiles(np.ascontiguousarray(kvw[..., 1])), "o": out_rows(p1["out_w"], plain),
        "m1": _k_tiles(p1["mlp_w1"]), "m2": _k_tiles(p1["mlp_w2"], HID // P),
        "qb": _vec(_slots(p1["q_b"].reshape(1, -1), plain, {HD: float(HD)})),
        "kb": _vec(_slots(kvb[:, 0].reshape(1, -1), plain, {HD + 1: 1.0})),
        "vb": all_rows(kvb[:, 1]), "ob": _vec(p1["out_b"]), "norm_w": _vec(p1["postnorm_w"]),
        "b1": _vec(p1["mlp_b1"]), "b2": _vec(p1["mlp_b2"])})
    d = layer(2)
    part = {"m1": _k_tiles(d["w1"]), "m2": _k_tiles(d["w2"], HID // P), "b1": _vec(d["b1"]), "b2": _vec(d["b2"])}
    for n, x in enumerate("qkv"):
        w = d["w_q"] if x == "q" else d["w_kv"][:, (n - 1) * C:n * C]
        b = d["b_q"] if x == "q" else d["b_kv"][(n - 1) * C:n * C]
        for i, (wi, bi) in enumerate(((d["w_qkv"][:, n * C:(n + 1) * C], d["b_qkv"][n * C:(n + 1) * C]), (w, b))):
            part[f"{x}{i}"] = _k_tiles(np.ascontiguousarray(wi))
            part[f"{x}b{i}"] = all_rows(bi) if x == "v" else _vec(bi)
    for i, x in enumerate(("ao", "co")):
        part[f"o{i}"] = out_rows(d["w_" + x], paired)
        part[f"ob{i}"] = _vec(d["b_" + x])
    for n in (1, 2, 3):
        part[f"ln{n}_w"], part[f"ln{n}_b"] = _vec(d[f"ln{n}_s"]), _vec(d[f"ln{n}_b"])
    dec = _pack(DEC, part)

    arrays = {
        "x": tokens(a["x"]), "ctx": tokens(ctxt),
        "state": np.ascontiguousarray(np.concatenate([rows, s0], 2)),
        "pmask": np.ascontiguousarray(a["mask_BxS2_ik0"].reshape(GROUPS, N)),
        "cross": np.ascontiguousarray(a["mask_Bx1xSxS2_ff1"].reshape(GROUPS, GB, T, T).transpose(0, 2, 1, 3)),
        "ltor": np.ascontiguousarray(a["mask_1x1xSxS2_fc1"].reshape(T, T)),
        "const": _constants(), "rwkv0": _rwkv_pack(layer(0), 0), "perc": perc, "dec": dec,
        "rwkv1": _rwkv_pack(layer(3), 1),
    }
    nc = _bacc.Bacc("TRN2", target_bir_lowering=False, num_devices=1)
    args = [nc.dram_tensor(f"in_{k}", v.shape, mybir.dt.from_np(v.dtype), kind="ExternalInput").ap()
            for k, v in arrays.items()]
    out = nc.dram_tensor("out_x", (GROUPS, P, NC_ * N), F32, kind="ExternalOutput").ap()
    between = [nc.dram_tensor(f"between{k}", (GROUPS, P, NC_ * N), F32, kind="Internal").ap() for k in range(LOOPS - 1)]
    build_program(nc, *args, between, out)
    r = _run(nc, [{f"in_{k}": v for k, v in arrays.items()}], core_ids=[0])
    got = r.results[0]["out_x"].reshape(GROUPS, P, NC_, N).transpose(0, 3, 2, 1)
    return np.ascontiguousarray(got).reshape(B, T, C)
```

```python
from contextlib import ExitStack

import numpy as np

import concourse.bass as bass
from concourse import mybir

F32 = mybir.dt.float32
F32R = mybir.dt.float32r
I32 = mybir.dt.int32
ALU = mybir.AluOpType
ACT = mybir.ActivationFunctionType
AX = mybir.AxisListType

P = 128
B, T, C = 16, 128, 256
NC_ = C // P
GB = 1
N = GB * T
GROUPS = B // GB
STREAMS = 4
ROUNDS = GROUPS // STREAMS
S8 = 8
RH = C // S8
NH, HD = 16, 16
HID = 4 * C
SLOT = 32
TQ = NH * SLOT // P
BLK = N // 4
MASKED = -1e30
BEHIND = ((0, 2, 6, 8), (0, 2, 8, 10), (0, 2, 8, 10), (0, 2, 6, 8))



def _columns(fields):
    at, out = 0, {}
    for name, width in fields:
        out[name] = (at, width)
        at += width
    return out, at


CONST, CONST_W = _columns([
    ("mean", P), ("spread_ln", P), ("down", 2 * RH), ("all", 2 * P), ("head_mean", P), ("same", P), ("up", 2 * P),
    ("narrow_sm", TQ * SLOT), ("spread_sm", TQ * P),
    ("ident", P), ("block", 4), ("maskrow", P), ("eps5", 1), ("eps6", 1), ("even", 1), ("odd", 1)])
LIN = NC_ * C
RWKV, RWKV_W = _columns(
    [("w1", NC_ * 160), ("w2", C), ("w2b", C), ("td1", NC_ * 64), ("td2", C)]
    + [(w, LIN) for w in ("Wr", "Wk", "Wv", "Wg", "Wo", "Fk", "Fr", "Fv")]
    + [(v, NC_) for v in ("ln1_w", "ln1_b", "ln2_w", "ln2_b", "maa_x", "td", "u", "gn_w", "gn_b", "fk", "fr")]
    + [("maa", 5 * NC_)])
PERC, PERC_W = _columns([
    ("q", NC_ * TQ * P), ("k", NC_ * TQ * P), ("v", LIN), ("o", TQ * C), ("m1", NC_ * HID), ("m2", HID // P * C),
    ("qb", TQ), ("kb", TQ), ("vb", C), ("ob", NC_), ("norm_w", NC_), ("b1", HID // P), ("b2", NC_)])
DEC, DEC_W = _columns(
    [(f"{w}{a}", LIN) for a in (0, 1) for w in "qkv"] + [(f"o{a}", TQ * C) for a in (0, 1)]
    + [("m1", NC_ * HID), ("m2", HID // P * C)]
    + [(f"{w}b{a}", NC_) for a in (0, 1) for w in "qko"] + [(f"vb{a}", C) for a in (0, 1)]
    + [(f"ln{n}_{x}", NC_) for n in (1, 2, 3) for x in "wb"] + [("b1", HID // P), ("b2", NC_)])
ORDER = (("k", "w", "v", "r", "g"), ("w", "k", "v", "r", "g"))
STATE_W = 2 * NC_ * GB + NC_ * S8 * GB


def _constants():
    p = np.arange(P)[:, None]
    m = np.arange(P)[None, :]
    s = np.arange(SLOT)[None, :]
    part = {
        "mean": np.full((P, P), 1.0 / C),
        "spread_ln": np.full((P, P), 1.0 / SLOT),
        "down": np.concatenate([s == P // S8 * c + p // S8 for c in range(2)], 1),
        "all": np.concatenate([m % RH == P // S8 * c + p // S8 for c in range(2)], 1),
        "up": np.concatenate([p % RH == P // S8 * c + m // S8 for c in range(2)], 1),
        "same": p % RH == m % RH, "head_mean": (p % RH == m % RH) / S8,
        "narrow_sm": np.concatenate([(p % SLOT == HD) & (s % NH == 4 * t + p // SLOT) for t in range(TQ)], 1),
        "spread_sm": np.concatenate([p % SLOT == 4 * t + m // SLOT for t in range(TQ)], 1),
        "ident": p == m,
        "block": p // SLOT == np.arange(4)[None, :],
        "maskrow": np.broadcast_to(m % SLOT == HD, (P, P)),
        "eps5": np.full((P, 1), 1e-5), "eps6": np.full((P, 1), 1e-6),
        "even": (p // HD % 2 == 0) / 4.0, "odd": (p // HD % 2 == 1) / 4.0,
    }
    return np.concatenate([np.asarray(part[k], np.float32) for k in CONST], 1)



RWKV0, PERCEIVER, DECODER, RWKV1 = range(4)
LOOPS = 4


class Place:

    def __init__(self, loop, it):
        self.loop, self.it, self.ahead = loop, it, 0

    def at(self, it, ahead):
        self.it, self.ahead = it, ahead
        return self


def in_turns(programs, steps, rounds):
    last, lacking, places = [None] * STREAMS, [0] * STREAMS, [None] * STREAMS

    def round_(loop, it):
        here = [Place(loop, it) for _ in range(STREAMS)]
        new = [programs[loop](here[s], s) for s in range(STREAMS)]
        left = [steps[loop] - BEHIND[loop][s] for s in range(STREAMS)]
        i = 0
        while any(left):
            for s in reversed(range(STREAMS)):
                if lacking[s]:
                    next(last[s])
                    lacking[s] -= 1
                elif left[s] and i >= BEHIND[loop][s]:
                    next(new[s])
                    left[s] -= 1
            i += 1
        for s in range(STREAMS):
            last[s], lacking[s], places[s] = new[s], BEHIND[loop][s], here[s]

    for loop in range(LOOPS):
        round_(loop, 0)
        for it in rounds(loop):
            for s in range(STREAMS):
                places[s].at(it, -1)
            round_(loop, it)
        for s in range(STREAMS):
            places[s].at(ROUNDS - 1, 0)
    while any(lacking):
        for s in reversed(range(STREAMS)):
            if lacking[s]:
                next(last[s])
                lacking[s] -= 1


def tiles_of(loop, add):

    def norm(i, mean=True):
        if mean:
            add(f"mean{i}", 1, "V")
            yield
        add(f"var{i}", 1, "A")
        yield
        add(f"scale{i}", 1, "V")
        yield

    def rwkv():
        yield from norm(0)
        add("mix", 1, "A")
        yield
        for f in range(5):
            add(f"maa.{f}", 1, "V")
        yield
        add("k", 1, "A")
        add("td1", 1, "A")
        yield
        add("v", 1, "A")
        add("td2", 1, "A")
        yield
        add("r", 1, "A")
        add("g", 1, "V")
        yield
        add("bonus", 1, "V")
        for c in range(2):
            for j in range(4):
                add(f"vb.{c}.{j}", 1, "V")
            yield
        add("y", 1, "V")
        yield
        add("gmean", 1, "V")
        yield
        add("gvar", 1, "A")
        yield
        add("gscale", 1, "V")
        yield
        add("wo", 1, "V")
        yield
        yield from norm(1)
        add("fr", 1, "A")
        add("fk", 1, "A")
        yield
        add("fv", 1, "V")
        yield

    def softmax(a):
        add(f"den{a}", 1, "V")
        yield
        add(f"inv{a}", 1, "V")
        yield
        add(f"o{a}", 1, "V")
        yield

    def mlp():
        for n in range(HID // P // 4):
            add(f"hid.{n}", 1, "A")
        yield
        add("down", 1, "V")
        yield

    def perceiver():
        for h in range(2):
            add(f"pq{h}", 1, "A")
        yield
        for t in range(TQ):
            add(f"pk{t}", 1, "A")
        yield
        for b in range(GB):
            add(f"pv{b}", 1, "V")
        yield
        for b in range(GB):
            for u in range(2):
                add(f"ps{b}.{u}", 4, "V")
                yield
            add(f"pm{b}", 1, "V")
            yield
            for kt, engine in enumerate("AV"):
                add(f"pt{b}.{kt}", 4, "A")
                yield
                add(f"pc{b}.{kt}", 1, engine)
            yield
        yield from softmax(0)
        yield from norm(0, mean=False)
        yield from mlp()

    def decoder():
        for a in range(2):
            yield from norm(a)
            add(f"dq{a}", 1, "A")
            add(f"dk{a}", 1, "A")
            add(f"dv{a}", 1, "V")
            yield
            for b in range(GB):
                add(f"ds{a}.{b}", 4, "V")
                yield
                yield
                yield
                add(f"dt{a}.{b}", 4, "A")
                yield
                add(f"dc{a}.{b}", 1, "A")
                yield
            yield from softmax(a)
        yield from norm(2)
        yield from mlp()

    return {RWKV0: rwkv, RWKV1: rwkv, PERCEIVER: perceiver, DECODER: decoder}[loop]()


class BankRing:

    def __init__(self):
        self.steps, self.tiles = [], [[] for _ in range(STREAMS)]
        self.takings = {engine: [[] for _ in range(STREAMS)] for engine in "AV"}
        for loop in range(LOOPS):
            engines = []
            self.steps.append(sum(1 for _ in tiles_of(loop, lambda name, banks, engine: engines.append(engine))))
            for s in range(STREAMS):
                self.tiles[s].append(len(engines))
                for engine in "AV":
                    self.takings[engine][s].append(engines.count(engine))
        order = []

        def tiles(loop):
            def program(h, s):
                def add(name, banks, engine):
                    order.append(((h.loop, h.it + h.ahead, s, name), banks, engine))
                return tiles_of(loop, add)
            return program

        starts = {}

        def rounds(loop):
            for it in range(1, ROUNDS):
                starts[loop, it] = len(order)
                yield it

        in_turns([tiles(loop) for loop in range(LOOPS)], self.steps, rounds)
        self.bank, self.number, self.taking, self.former = {}, {}, {}, {}
        for loop in range(LOOPS):
            at = 0
            for (_, _, s, name), banks, _ in order[starts[loop, 2]:starts[loop, 3]]:
                at = -(-at // banks) * banks % 8
                self.bank[loop, s, name] = at
                at = (at + banks) % 8
        count, holder = {}, [None] * 8
        for tile, banks, engine in order:
            loop, it, s, name = tile
            key = loop, s, name
            if it == 0:
                count[loop, s, ""] = self.number[key] = count.get((loop, s, ""), 0) + 1
                count[loop, s, engine] = count.get((loop, s, engine), 0) + 1
                self.taking[key] = engine, count[loop, s, engine]
            mine = slice(self.bank[key], self.bank[key] + banks)
            self.former[tile] = {t for t in holder[mine] if t is not None}
            holder[mine] = [tile] * banks


SQUARES = (3, 1, 3, 3)
SPREADS = (3, 2, 5, 3)
NORMED = (2, 0, 3, 2)


def build_program(nc, x_in, ctx_in, state_in_, pmask_in, cross_in, ltor_in, const_in, rwkv0_in, perc_in, dec_in,
                  rwkv1_in, between, out):
    ring = BankRing()
    with ExitStack() as ctx:
        def sb(name, *shape, dt=F32):
            return ctx.enter_context(nc.sbuf_tensor(name, list(shape), dt))

        class Signal:

            def __init__(self, name, per=(1, 1, 1, 1), start=1):
                self.sem, self.per, self.start = ctx.enter_context(nc.semaphore(name)), per, start

            def first(self, h):
                return self.start + ROUNDS * sum(self.per[:h.loop]) + h.ahead * self.per[h.loop]

            def before(self, h):
                assert self.start > 0
                return self.sem, h.it * self.per[h.loop] + self.first(h)

            def __call__(self, h, n=0):
                assert n < self.per[h.loop]
                return self.sem, h.it * self.per[h.loop] + (self.first(h) + n + 1)

        wa = sb("wa", P, max(RWKV_W, DEC_W))
        wb = sb("wb", P, max(RWKV_W, PERC_W))
        weights = (wa, wb, wa, wb)
        cst = sb("cst", P, CONST_W)
        up_r = sb("up_r", P, 2 * P, dt=F32R)
        ltor = sb("ltor", P, T)
        ltor_add = sb("ltor_add", P, T)
        prep = sb("prep", P, TQ + 4 * NC_)
        ps = ctx.enter_context(nc.psum_tensor("ps", [P, 8, 512], F32))

        const_loaded = ctx.enter_context(nc.semaphore("const_loaded"))
        weights_loaded = [ctx.enter_context(nc.semaphore(f"weights_loaded{k}")) for k in range(LOOPS)]
        up_written = ctx.enter_context(nc.semaphore("up_written"))

        class Stream:

            ARENA = 6016

            def __init__(q, s):
                q.s = s

                def own(name, *shape, dt=F32):
                    return sb(f"{name}_{s}", *shape, dt=dt)

                q.xin, q.cin = own("xin", P, NC_, N), own("cin", P, NC_, N)
                q.stin, q.st = own("stin", P, STATE_W), own("st", P, STATE_W)
                q.mc = own("mc", P, GB, T)
                q.pmin = q.mc[0:1, :, :].rearrange("p b t -> p (b t)").bitcast(I32)
                q.X = own("X", P, NC_, N)
                q.xc, q.sq = own("xc", P, NC_, N), own("sq", P, NC_, N)
                q.sd, q.rs, q.rm = own("sd", P, BLK), own("rs", P, BLK), own("rm", P, 4, BLK)
                q.mx = own("mx", P, NH)
                q.vhi, q.vlo = own("vhi", P, NC_, N, dt=F32R), own("vlo", P, NC_, N, dt=F32R)
                arena = own("arena", P, q.ARENA)
                at = [0]

                def cut(*shape):
                    size = int(np.prod(shape))
                    flat = arena[:, at[0]:at[0] + size]
                    at[0] += size
                    assert at[0] <= q.ARENA, at[0]
                    if len(shape) == 1:
                        return flat
                    names = "abc"[:len(shape)]
                    return flat.rearrange(f"p ({' '.join(names)}) -> p {' '.join(names)}",
                                          **dict(zip(names[1:], shape[1:])))

                q.ws = cut(NC_, GB, T)
                q.xap = cut(NC_ * GB, T + 1)
                q.sx = cut(NC_ * GB, T)
                q.mi = cut(NC_, N)
                q.tm = cut(N)
                q.tmb = cut(N)
                q.tw, q.e1, q.og = q.tm, q.mi.rearrange("p c (b t) -> p (c b) t", b=GB), q.mi
                q.tmp = [cut(NC_, N), cut(NC_, N)]
                q.xf = [cut(NC_, N) for _ in range(5)]
                q.tg, q.ruk = q.tmp
                q.ff = q.tmp[0]
                q.kv = [cut(S8, N), cut(S8, N)]
                q.vv, q.rr, q.g2 = q.xf[2:]
                q.kk = (q.xf[0], None, None, q.xf[1])
                q.bv = (q.xf[1], None, None, q.xf[0])
                q.yy, q.yc, q.yn = q.kk, q.xf[2], q.xf[3]
                q.ki, q.ri, q.tr, q.rl, q.k2 = q.xf
                at[0] = 0
                q.pva = cut(2 * GB, NH, SLOT)
                q.xn = cut(NC_, N)
                q.mxp = cut(TQ, P)
                q.qa = cut(TQ, N)
                q.ka = cut(TQ, 2 * GB, T)
                q.pt = cut(NH, T)
                q.ca = cut(TQ, N)
                q.qb, q.cn = q.qa.rearrange("p t (b q) -> p b t q", b=GB)[:, 0], q.qa
                q.phd = q.pt.rearrange("p b c -> p (b c)")[:, 0:HID // P * N].rearrange("p (a n) -> p a n", n=N)
                q.pmask = q.sq[0:1, 0, :]
                q.dva = q.pva[:, 0:GB]
                at[0] = GB * NH * SLOT
                ctx_d = cut(NC_, N)
                q.mc_add = cut(GB, T)
                q.ks = q.sq[:, :, :]
                assert at[0] <= 2 * GB * NH * SLOT
                at[0] = 2 * GB * NH * SLOT + NC_ * N
                q.dca = cut(TQ, N)
                q.qe, q.qo = q.dca[:, 0:NC_], q.dca[:, NC_:]
                q.tt = cut(NH, T)
                q.p2 = cut(NH, T)
                q.dcn = q.p2.rearrange("p h k -> p (h k)")[:, 0:TQ * N].rearrange("p (a n) -> p a n", n=N)
                q.dhd = q.tt.rearrange("p h k -> p (h k)")[:, 0:HID // P * N].rearrange("p (a n) -> p a n", n=N)
                q.CX = (None, q.xn, ctx_d, None)

                def signal(name, *per, start=1):
                    return Signal(f"{name}_{s}", per or (1, 1, 1, 1), start)

                q.filled = signal("filled", *ring.tiles[s], start=128 * (s + 1))
                q.act_took = signal("act_took", *ring.takings["A"][s], start=128 * (s + 1))
                q.dve_took = signal("dve_took", *ring.takings["V"][s], start=128 * (s + 1))
                q.prepared = ctx.enter_context(nc.semaphore(f"prepared_{s}"))
                q.inputs_in = signal("inputs_in", 32, 48, 32, 32, start=0)
                q.mask_in = signal("mask_in", 0, 0, 16, 0, start=0)
                q.stored = signal("stored", 16, 16, 16, 16, start=16)
                q.x_ready = signal("x_ready")
                q.xout_ready = signal("xout_ready")
                q.ctx_ready = signal("ctx_ready")
                q.masks_ready = signal("masks_ready", 0, 1, 1, 0)
                q.squared = signal("squared", *SQUARES)
                q.inverted = signal("inverted", *SQUARES)
                q.spread = signal("spread", *SPREADS)
                q.normed = signal("normed", *NORMED)
                q.state_in = signal("state_in", 2, 0, 0, 2)
                q.shifted = signal("shifted", 2, 0, 0, 2)
                q.mixed_in = signal("mixed_in", 1, 0, 0, 1)
                q.xf_ready = signal("xf_ready", 5, 0, 0, 5)
                q.decay = signal("decay", 1, 0, 0, 1)
                q.v_high = signal("v_high", 1, 0, 0, 1)
                q.v_low = signal("v_low", 1, 0, 0, 1)
                q.g_tanh = signal("g_tanh", 1, 0, 0, 1)
                q.ruk_ready = signal("ruk_ready", 1, 0, 0, 1)
                q.s0_placed = signal("s0_placed", 2, 0, 0, 2)
                q.scanned = signal("scanned", 2, 0, 0, 2)
                q.r_state = (signal("r_state_0", 1, 0, 0, 1),
                             signal("r_state_1", 1, 0, 0, 1))
                q.gated = signal("gated", 1, 0, 0, 1)
                q.ffn_in = signal("ffn_in", 2, 0, 0, 2)
                q.ffn_sq = signal("ffn_sq", 1, 0, 0, 1)
                q.max_ready = signal("max_ready", 0, 0, 2 * GB, 0)
                q.half_masked = signal("half_masked", 0, 0, 2 * GB, 0)
                q.half_added = signal("half_added", 0, 0, 2 * GB, 0)
                q.s_add = signal("s_add", 0, 0, 2 * GB, 0)
                q.s_sub = signal("s_sub", 0, 0, 2 * GB, 0)
                q.probs = signal("probs", 0, 0, 2 * GB, 0)

        streams = [Stream(s) for s in range(STREAMS)]

        def done(h, q, name):
            engine, count = ring.taking[h.loop, q.s, name]
            return (q.act_took if engine == "A" else q.dve_took)(h, count - 1)

        def full(h, q, name):
            return q.filled(h, ring.number[h.loop, q.s, name] - 1)

        def const(name, i=0, w=P, rows=slice(0, P)):
            a = CONST[name][0] + i * w
            return cst[rows, a:a + w]

        def vec(pack, fields, name, i=0):
            a = fields[name][0] + i
            return pack[:, a:a + 1]

        def tile_of(h, q, name, banks=1):
            b = ring.bank[h.loop, q.s, name]
            return ps[:, b, :] if banks == 1 else ps[:, b:b + banks, :]

        def pair(h, q, name):
            return tile_of(h, q, name)[:, 0:2 * N].rearrange("p (c n) -> p c n", c=2)

        def fours(h, q, name):
            return tile_of(h, q, name)[:, 0:4 * N].rearrange("p (c n) -> p c n", c=4)

        def wide(ap, k):
            n = ap.shape[-1]
            return ap.rearrange("p (o n) -> p o n", o=1).to_broadcast([ap.shape[0], k, n])

        def inner(ap, n):
            return ap.rearrange("p (k o) -> p k o", o=1).to_broadcast([ap.shape[0], ap.shape[-1], n])

        def by_row(ap):
            return ap.rearrange("p (b t) -> p b t", b=GB)

        def run(eng, programs):

            def rounds(loop):
                if programs[loop] is not idle:
                    with eng.Fori(1, ROUNDS) as it:
                        yield it

            in_turns([lambda h, s, program=program: program(h, streams[s]) for program in programs], ring.steps,
                     rounds)

        def idle(h, q):
            while True:
                yield

        block = ctx.enter_context(nc.Block())

        @block.sync
        def _(sp):
            def load_weights(k, dst, src):
                sp.dma_start(dst[:, 0:src.shape[1]], src).then_inc(weights_loaded[k], 16)

            def flat(ap):
                return ap[:, :, :].rearrange("p c n -> p (c n)")

            def of_group(ap, h, q):
                names = "pabc"[:len(ap.shape) - 1]
                group = ap.rearrange(f"(r s) {' '.join(names)} -> s r {' '.join(names)}", s=STREAMS)[
                    q.s, h.ahead:][h.it if isinstance(h.it, int) else bass.ds(h.it, 1)]
                if len(group.shape) == len(ap.shape):
                    group = group.rearrange(f"o {' '.join(names)} -> (o {names[0]}) {' '.join(names[1:])}")
                return group

            def known(*waits):
                for _, value in waits:
                    if not isinstance(value, int):
                        sp.compute_val(value)

            def load(h):
                for q in streams:
                    known(q.x_ready.before(h), q.ctx_ready.before(h), q.masks_ready.before(h))
                    if h.loop > 0:
                        known(q.stored(Place(h.loop - 1, h.it).at(h.it, h.ahead), 15))
                for q in streams:
                    src = x_in if h.loop == 0 else between[h.loop - 1]
                    sp.wait_ge(*q.x_ready.before(h))
                    if h.loop > 0:
                        sp.wait_ge(*q.stored(Place(h.loop - 1, h.it).at(h.it, h.ahead), 15))
                    sp.dma_start(flat(q.xin), of_group(src, h, q)).then_inc(q.inputs_in.sem, 16)
                    sp.wait_ge(*q.ctx_ready.before(h))
                    if h.loop in (RWKV0, RWKV1):
                        sp.dma_start(q.stin[:, :], of_group(state_in_, h, q)).then_inc(q.inputs_in.sem, 16)
                    else:
                        sp.dma_start(flat(q.cin), of_group(ctx_in, h, q)).then_inc(q.inputs_in.sem, 16)
                    if h.loop == PERCEIVER:
                        sp.wait_ge(*q.masks_ready.before(h))
                        sp.dma_start(q.pmin, of_group(pmask_in, h, q)).then_inc(q.inputs_in.sem, 16)

            def store(h):
                known(*[q.xout_ready(h) for q in streams], (None, h.it * (STREAMS * P * NC_ * N) * 4))
                for q in streams:
                    sp.wait_ge(*q.xout_ready(h))
                    dst = out if h.loop == LOOPS - 1 else between[h.loop]
                    sp.dma_start(of_group(dst, h, q), flat(q.X)).then_inc(q.stored.sem, 16)
                    after = Place(DECODER, 0) if h.loop == PERCEIVER else Place(h.loop, h.it).at(h.it, 1)
                    ends = isinstance(h.it, int)
                    if h.loop == PERCEIVER and ends or h.loop == DECODER and not ends:
                        sp.dma_start(q.mc[:, :, :], of_group(cross_in, after, q)).then_inc(q.mask_in.sem, 16)

            for q in streams:
                sp.sem_inc(q.stored.sem, q.stored.start)
            sp.dma_start(cst[:, :], const_in).then_inc(const_loaded, 16)
            for q in streams:
                sp.dma_start(flat(q.xin), x_in[q.s]).then_inc(q.inputs_in.sem, 16)
                sp.dma_start(q.stin[:, :], state_in_[q.s]).then_inc(q.inputs_in.sem, 16)
            load_weights(0, wa, rwkv0_in)
            load_weights(1, wb, perc_in)
            sp.dma_start(ltor[:, :], ltor_in).then_inc(const_loaded, 16)
            for loop in range(LOOPS):
                with sp.Fori(0, ROUNDS - 1) as it:
                    load(Place(loop, it).at(it, 1))
                    store(Place(loop, it))
                if loop + 1 < LOOPS:
                    load(Place(loop + 1, 0))
                store(Place(loop, ROUNDS - 1))
                if loop + 2 < LOOPS:
                    load_weights(loop + 2, weights[loop], (dec_in, rwkv1_in)[loop])
            for q in streams:
                sp.wait_ge(*q.stored(Place(LOOPS - 1, ROUNDS - 1), 15))

        @block.tensor
        def _(pe):
            def latest(h, name, s, counts):
                engine, count = ring.taking[h.loop, s, name]
                took = streams[s].act_took if engine == "A" else streams[s].dve_took
                new = (h.ahead if not isinstance(h.it, int) else h.it + h.ahead, count, h)
                key = took, h.loop
                if key not in counts or counts[key][:2] < new[:2]:
                    counts[key] = new

            def fill(h, q, name, banks=1, inputs=()):
                fixed = isinstance(h.it, int)
                counts = {}
                for tile in inputs:
                    latest(Place(h.loop, h.it).at(h.it, h.ahead), tile, q.s, counts)
                for it in ([h.it] if fixed else [2, 1]):
                    for loop, then, s, tile in ring.former[h.loop, it + h.ahead, q.s, name]:
                        now = Place(loop, then) if fixed or loop != h.loop else Place(loop, h.it).at(h.it, then - it)
                        if s != q.s or (loop, then) == (h.loop, it + h.ahead):
                            latest(now, tile, s, counts)
                for (took, _), (_, count, now) in counts.items():
                    pe.wait_ge(*took(now, count - 1))
                return tile_of(h, q, name, banks)

            def mm(o, lhsT, rhs, start=True, stop=True):
                return pe.matmul(o, lhsT, rhs, start=start, stop=stop, skip_group_check=True)

            def linear(o, pack, fields, name, rhs, n_out, k_tiles=NC_):
                a, w = fields[name]
                width = w // k_tiles
                for m in range(n_out):
                    for k in range(k_tiles):
                        i = mm(o[:, m], pack[:, a + k * width + m * P:a + k * width + (m + 1) * P], rhs[:, k],
                               start=(k == 0), stop=(k == k_tiles - 1))
                return i

            def narrow(o, lhs, src, k_tiles):
                for k in range(k_tiles):
                    for j in range(4):
                        i = mm(o[SLOT * j:SLOT * (j + 1), 0:BLK], lhs(k), src[:, k, j * BLK:(j + 1) * BLK],
                               start=(k == 0), stop=(k == k_tiles - 1))
                return i

            def norm(h, q, i, n, z, mean=True, inputs=()):
                if mean:
                    o = fill(h, q, f"mean{i}", inputs=inputs)
                    for c in range(NC_):
                        m = mm(o[:, 0:N], const("mean"), q.X[:, c], start=(c == 0), stop=(c == 1))
                    m.then_inc(q.filled.sem, 1)
                    yield
                o = fill(h, q, f"var{i}")
                pe.wait_ge(*q.squared(h, n))
                narrow(o, lambda k: const("mean")[:, 0:SLOT], q.sq, NC_).then_inc(q.filled.sem, 1)
                yield
                o = fill(h, q, f"scale{i}")
                pe.wait_ge(*q.spread(h, z))
                mm(o[:, 0:N], const("spread_ln"), q.rm[:, :, :]).then_inc(q.filled.sem, 1)
                yield

            def rwkv(h, q):
                w, R, order = weights[h.loop], RWKV, ORDER[h.loop // RWKV1]
                at_f = {x: order.index(x) for x in order}
                pe.wait_ge(*q.x_ready(h))
                yield from norm(h, q, 0, 0, 0)
                o = fill(h, q, "mix")
                pe.wait_ge(*q.mixed_in(h))
                a = R["w1"][0]
                for k in range(NC_):
                    mm(o[:, 0:N], w[:, a + 160 * k:a + 160 * k + P], q.mi[:, k], start=(k == 0), stop=(k == 1))
                for k in range(NC_):
                    m = mm(o[0:32, N:2 * N], w[:, a + 160 * k + P:a + 160 * (k + 1)], q.mi[:, k], start=(k == 0),
                           stop=(k == 1))
                m.then_inc(q.filled.sem, 1)
                yield
                for f in range(5):
                    o = fill(h, q, f"maa.{f}", inputs=("mix",) if f == 0 else ())
                    a = R["w2" if f < 4 else "w2b"][0]
                    r = slice(32 * f, 32 * f + 32) if f < 4 else slice(0, 32)
                    src = q.tm if f < 4 else q.tmb
                    for c in range(NC_):
                        m = mm(o[:, c * N:(c + 1) * N], w[r, a + c * P:a + (c + 1) * P], src[r, :])
                    m.then_inc(q.filled.sem, 1)
                yield

                def project(x):
                    fill(h, q, x)
                    pe.wait_ge(*q.xf_ready(h, at_f[x]))
                    linear(pair(h, q, x), w, R, "W" + x, q.xf[at_f[x]], 2).then_inc(q.filled.sem, 1)

                project("k")
                o = fill(h, q, "td1")
                pe.wait_ge(*q.xf_ready(h, at_f["w"]))
                a = R["td1"][0]
                for k in range(NC_):
                    m = mm(o[0:64, 0:N], w[:, a + 64 * k:a + 64 * (k + 1)], q.xf[at_f["w"]][:, k], start=(k == 0),
                           stop=(k == 1))
                m.then_inc(q.filled.sem, 1)
                yield
                project("v")
                o = fill(h, q, "td2", inputs=("td1",))
                a = R["td2"][0]
                for c in range(NC_):
                    m = mm(o[:, c * N:(c + 1) * N], w[0:64, a + c * P:a + (c + 1) * P], q.tw[0:64, :])
                m.then_inc(q.filled.sem, 1)
                yield
                project("r")
                project("g")
                yield
                o = fill(h, q, "bonus")
                pe.wait_ge(*q.ruk_ready(h))
                for c in range(NC_):
                    m = mm(o[:, 0:N], const("all", c), q.ruk[:, c], start=(c == 0), stop=(c == 1))
                m.then_inc(q.filled.sem, 1)
                pe.wait_ge(*q.v_high(h))
                pe.wait_ge(*q.v_low(h))
                for c in range(NC_):
                    for j in range(4):
                        o = fill(h, q, f"vb.{c}.{j}")[:, 0:2 * N]
                        r = slice(RH * j, RH * (j + 1))
                        for n, part in enumerate((q.vhi, q.vlo)):
                            m = mm(o, up_r[r, c * P:(c + 1) * P], part[r, :, :], start=(n == 0), stop=(n == 1))
                        m.then_inc(q.filled.sem, 1)
                    yield
                fill(h, q, "y")
                o = pair(h, q, "y")
                for c in range(NC_):
                    pe.wait_ge(*q.r_state[c](h))
                    for j in range(4):
                        m = mm(o[RH * j:RH * (j + 1)], const("down", c, RH), q.kv[c][:, j::4, :], start=(c == 0),
                               stop=(c == 1))
                m.then_inc(q.filled.sem, 1)
                yield
                o = fill(h, q, "gmean", inputs=("y",))
                for c in range(NC_):
                    m = mm(o[:, 0:N], const("head_mean"), q.yy[h.loop][:, c], start=(c == 0), stop=(c == 1))
                m.then_inc(q.filled.sem, 1)
                yield
                o = fill(h, q, "gvar")
                pe.wait_ge(*q.squared(h, 1))
                narrow(o, lambda k: const("head_mean")[:, 0:SLOT], q.sq, NC_).then_inc(q.filled.sem, 1)
                yield
                o = fill(h, q, "gscale")
                pe.wait_ge(*q.spread(h, 1))
                mm(o[:, 0:N], const("same"), q.rm[:, :, :]).then_inc(q.filled.sem, 1)
                yield
                fill(h, q, "wo")
                pe.wait_ge(*q.gated(h))
                linear(pair(h, q, "wo"), w, R, "Wo", q.og, 2).then_inc(q.filled.sem, 1)
                yield
                yield from norm(h, q, 1, 2, 2, inputs=("wo",))
                fill(h, q, "fr")
                pe.wait_ge(*q.ffn_in(h, 0))
                linear(pair(h, q, "fr"), w, R, "Fr", q.ri, 2).then_inc(q.filled.sem, 1)
                fill(h, q, "fk")
                pe.wait_ge(*q.ffn_in(h, 1))
                linear(pair(h, q, "fk"), w, R, "Fk", q.ki, 2).then_inc(q.filled.sem, 1)
                yield
                fill(h, q, "fv")
                pe.wait_ge(*q.ffn_sq(h))
                linear(pair(h, q, "fv"), w, R, "Fv", q.k2, 2).then_inc(q.filled.sem, 1)
                yield

            def softmax_out(h, q, a, z, ready, ca, cn, fields, name):
                o = fill(h, q, f"den{a}", inputs=(ready,))
                narrow(o, lambda k: const("narrow_sm", k, SLOT), ca, TQ).then_inc(q.filled.sem, 1)
                yield
                fill(h, q, f"inv{a}")
                pe.wait_ge(*q.spread(h, z))
                o = fours(h, q, f"inv{a}")
                for t in range(TQ):
                    m = mm(o[:, t], const("spread_sm", t), q.rm[:, :, :])
                m.then_inc(q.filled.sem, 1)
                yield
                fill(h, q, f"o{a}", inputs=(f"inv{a}",))
                linear(pair(h, q, f"o{a}"), weights[h.loop], fields, name, cn, 2, k_tiles=TQ).then_inc(q.filled.sem, 1)
                yield

            def mlp(h, q, fields, hd, inputs=()):
                pack = weights[h.loop]
                a = fields["m1"][0]
                for n in range(HID // P // 4):
                    fill(h, q, f"hid.{n}", inputs=inputs if n == 0 else ())
                    o = fours(h, q, f"hid.{n}")
                    for e in range(4):
                        for k in range(NC_):
                            w0 = a + k * HID + (4 * n + e) * P
                            i = mm(o[:, e], pack[:, w0:w0 + P], q.xn[:, k], start=(k == 0), stop=(k == 1))
                    i.then_inc(q.filled.sem, 1)
                yield
                fill(h, q, "down", inputs=("hid.1",))
                linear(pair(h, q, "down"), pack, fields, "m2", hd, 2, k_tiles=HID // P).then_inc(q.filled.sem, 1)
                yield

            def values(h, q, name, src, fields, wname):
                o = fill(h, q, name).rearrange("p (s c) -> p s c", s=2)
                a = fields[wname][0]
                for s, (buf, b) in enumerate(src):
                    for k in range(NC_):
                        m = mm(o[:, s], buf[:, k, b * T:(b + 1) * T], weights[h.loop][:, a + k * C:a + (k + 1) * C],
                               start=(k == 0), stop=(k == 1))
                m.then_inc(q.filled.sem, 1)

            def perceiver(h, q):
                w = weights[h.loop]
                pe.wait_ge(*q.x_ready(h))
                a = PERC["q"][0]
                for n in range(2):
                    fill(h, q, f"pq{n}")
                    o = pair(h, q, f"pq{n}")
                    for t in range(2):
                        for k in range(NC_):
                            w0 = a + k * TQ * P + (2 * n + t) * P
                            m = mm(o[:, t], w[:, w0:w0 + P], q.X[:, k], start=(k == 0), stop=(k == 1))
                    m.then_inc(q.filled.sem, 1)
                yield
                a = PERC["k"][0]
                pe.wait_ge(*q.ctx_ready(h))
                pe.wait_ge(*q.masks_ready(h))
                for t in range(TQ):
                    fill(h, q, f"pk{t}")
                    o = pair(h, q, f"pk{t}")
                    for s, buf in enumerate((q.CX[h.loop], q.X)):
                        for k in range(NC_):
                            w0 = a + k * TQ * P + t * P
                            m = mm(o[:, s], w[:, w0:w0 + P], buf[:, k], start=(k == 0), stop=(s == 1 and k == 1))
                        if s == 0:
                            mm(o[:, s], const("maskrow", rows=slice(0, 1)), q.pmask, start=False)
                    m.then_inc(q.filled.sem, 1)
                yield
                for b in range(GB):
                    values(h, q, f"pv{b}", ((q.CX[h.loop], b), (q.X, b)), PERC, "v")
                yield
                for b in range(GB):
                    for u in range(2):
                        o = fill(h, q, f"ps{b}.{u}", 4, inputs=("pq1", "pk3"))
                        for t in range(2):
                            for j in range(4):
                                r = slice(SLOT * j, SLOT * (j + 1))
                                m = mm(o[:, j, t * 2 * T:(t + 1) * 2 * T], q.qa[r, 2 * u + t, b * T:(b + 1) * T],
                                       q.ka[r, 2 * u + t, 2 * b:2 * b + 2, :])
                        m.then_inc(q.filled.sem, 1)
                        yield
                    o = fill(h, q, f"pm{b}", inputs=(f"ps{b}.1",))
                    for t in range(TQ):
                        m = pe.transpose(o[:, t * T:(t + 1) * T], q.mxp[:, t, :], const("ident"))
                    m.then_inc(q.filled.sem, 1)
                    yield
                    for kt in range(2):
                        o = fill(h, q, f"pt{b}.{kt}", 4, inputs=(f"pm{b}",))
                        for t in range(TQ):
                            for j in range(4):
                                r = slice(SLOT * j, SLOT * (j + 1))
                                m = mm(o[:, j, t * T:(t + 1) * T], q.ka[r, t, 2 * b + kt, :], q.qb[r, t, :])
                        m.then_inc(q.filled.sem, 1)
                        yield
                        o = fill(h, q, f"pc{b}.{kt}", inputs=(f"pv{b}", f"pt{b}.{kt}"))
                        for t in range(TQ):
                            for j in range(4):
                                m = mm(o[SLOT * j:SLOT * (j + 1), t * T:(t + 1) * T],
                                       q.pva[:, 2 * b + kt, 4 * t + j, :], q.pt[:, 4 * j + t, :])
                        m.then_inc(q.filled.sem, 1)
                    yield
                yield from softmax_out(h, q, 0, 0, f"pc{GB - 1}.1", q.ca, q.cn, PERC, "o")
                yield from norm(h, q, 0, 0, 1, mean=False)
                yield from mlp(h, q, PERC, q.phd, inputs=("scale0",))

            def decoder(h, q):
                pe.wait_ge(*q.x_ready(h))
                for a in range(2):
                    yield from norm(h, q, a, a, 2 * a, inputs=("o0",) if a == 1 else ())
                    src = q.xn if a == 0 else q.CX[h.loop]
                    pe.wait_ge(*q.normed(h, a))
                    if a == 1:
                        pe.wait_ge(*q.ctx_ready(h))
                    fill(h, q, f"dq{a}")
                    linear(pair(h, q, f"dq{a}"), weights[h.loop], DEC, f"q{a}", q.xn, 2).then_inc(q.filled.sem, 1)
                    fill(h, q, f"dk{a}")
                    linear(pair(h, q, f"dk{a}"), weights[h.loop], DEC, f"k{a}", src, 2).then_inc(q.filled.sem, 1)
                    values(h, q, f"dv{a}", [(src, b) for b in range(GB)], DEC, f"v{a}")
                    yield
                    for b in range(GB):
                        o = fill(h, q, f"ds{a}.{b}", 4, inputs=(f"dq{a}", f"dk{a}"))
                        for t in range(TQ):
                            for j in range(4):
                                r = slice(SLOT * j, SLOT * (j + 1))
                                m = mm(o[:, j, t * T:(t + 1) * T],
                                       (q.qe, q.qo)[t % 2][r, t // 2, b * T:(b + 1) * T],
                                       q.ks[r, t // 2, b * T:(b + 1) * T])
                        m.then_inc(q.filled.sem, 1)
                        yield
                        yield
                        yield
                        o = fill(h, q, f"dt{a}.{b}", 4)
                        pe.wait_ge(*q.probs(h, GB * a + b))
                        for n in range(NH):
                            m = pe.transpose(o[:, n // 4, (n % 4) * T:(n % 4 + 1) * T], q.tt[:, n, :], const("ident"))
                        m.then_inc(q.filled.sem, 1)
                        yield
                        o = fill(h, q, f"dc{a}.{b}", inputs=(f"dt{a}.{b}", f"dv{a}"))
                        for t in range(TQ):
                            for j in range(4):
                                n = 8 * (t // 2) + 2 * j + t % 2
                                m = mm(o[SLOT * j:SLOT * (j + 1), t * T:(t + 1) * T], q.dva[:, b, n, :],
                                       q.p2[:, 4 * j + t, :])
                        m.then_inc(q.filled.sem, 1)
                        yield
                    yield from softmax_out(h, q, a, 2 * a + 1, f"dc{a}.{GB - 1}", q.dca, q.dcn, DEC, f"o{a}")
                yield from norm(h, q, 2, 2, 4, inputs=("o1",))
                pe.wait_ge(*q.normed(h, 2))
                yield from mlp(h, q, DEC, q.dhd)

            def from_start(program):
                def started(h, q):
                    if isinstance(h.it, int) and h.it == 0:
                        pe.wait_ge(weights_loaded[h.loop], 16)
                        pe.wait_ge(q.prepared, h.loop + 1)
                    pe.wait_ge(*q.act_took.before(h))
                    pe.wait_ge(*q.dve_took.before(h))
                    yield from program(h, q)

                return started

            pe.wait_ge(const_loaded, 32)
            pe.wait_ge(up_written, 1)
            for q in streams:
                pe.sem_inc(q.filled.sem, q.filled.start)
            run(pe, [from_start(program) for program in (rwkv, perceiver, decoder, rwkv)])

        @block.scalar
        def _(act):
            def f(o, i, fn, **kw):
                return nc.scalar.activation(o, i, fn, **kw)

            def norm(h, q, i, bias, dst, src=None, mean=True):
                if mean:
                    act.wait_ge(*done(h, q, f"mean{i}"))
                f(q.sq[:, :, :], q.xc[:, :, :], ACT.Square).then_inc(q.squared.sem, 1)
                if mean:
                    yield
                act.wait_ge(*full(h, q, f"var{i}"))
                f(q.sd[:, :], tile_of(h, q, f"var{i}")[:, 0:BLK], ACT.Sqrt,
                  bias=const("eps5" if mean else "eps6", w=1)).then_inc(q.act_took.sem, 1)
                yield
                if bias is not None:
                    act.wait_ge(*done(h, q, f"scale{i}"))
                    for c in range(NC_):
                        m = f(dst(c), dst(c), ACT.Identity, bias=bias(c))
                    m.then_inc(q.normed.sem, 1)
                yield

            def padded(q):
                return lambda c: q.xap[:, c * GB:(c + 1) * GB, 1:T + 1]

            def rwkv(h, q):
                w, R = weights[h.loop], RWKV

                def state(part):
                    a = (1 - part) * NC_ * GB
                    f(q.xap[:, :, 0:1], q.st[:, a:a + NC_ * GB].rearrange("p (c o) -> p c o", o=1),
                      ACT.Copy).then_inc(q.state_in.sem, 1)

                act.wait_ge(*q.xout_ready.before(h))
                act.wait_ge(*q.inputs_in(h, 31))
                f(q.st[:, :], q.stin[:, :], ACT.Copy).then_inc(q.ctx_ready.sem, 1)
                act.wait_ge(*q.ctx_ready(h))
                state(0)
                for c in range(NC_):
                    a = 2 * NC_ * GB + c * GB * S8
                    f(q.kv[c].rearrange("p j (b t) -> p j b t", b=GB)[:, :, :, 0],
                      q.st[:, a:a + GB * S8].rearrange("p (j b) -> p j b", b=GB), ACT.Copy).then_inc(
                        q.s0_placed.sem, 1)
                yield from norm(h, q, 0, lambda c: vec(w, R, "ln1_b", c), padded(q))
                o = tile_of(h, q, "mix")
                act.wait_ge(*full(h, q, "mix"))
                f(q.tm, o[:, 0:N], ACT.Tanh)
                f(q.tmb[0:32, :], o[0:32, N:2 * N], ACT.Tanh).then_inc(q.act_took.sem, 1)
                yield
                yield

                def take(x, dst):
                    act.wait_ge(*full(h, q, x))
                    f(dst, pair(h, q, x), ACT.Copy).then_inc(q.act_took.sem, 1)

                take("k", q.kk[h.loop])
                act.wait_ge(*full(h, q, "td1"))
                f(q.tw[0:64, :], tile_of(h, q, "td1")[0:64, 0:N], ACT.Tanh).then_inc(q.act_took.sem, 1)
                yield
                act.wait_ge(*full(h, q, "v"))
                f(q.vhi[:, :, :], pair(h, q, "v"), ACT.Copy).then_inc(q.v_high.sem, 1)
                take("v", q.vv)
                act.wait_ge(*full(h, q, "td2"))
                for c in range(NC_):
                    m = f(q.e1[:, c * GB:(c + 1) * GB, :].rearrange("p b t -> p (b t)"), pair(h, q, "td2")[:, c],
                          ACT.Exp, bias=vec(w, R, "td", c))
                m.then_inc(q.act_took.sem, 1)
                act.wait_ge(*done(h, q, "td2"))
                f(q.ws[:, :, :, 1:T].rearrange("p c b t -> p (c b) t"), q.e1[:, :, 0:T - 1], ACT.Exp,
                  scale=-1.0).then_inc(q.decay.sem, 1)
                yield
                take("r", q.rr)
                act.wait_ge(*full(h, q, "g"))
                f(q.tg, pair(h, q, "g"), ACT.Tanh, scale=0.5).then_inc(q.g_tanh.sem, 1)
                yield
                yield
                yield
                yield
                act.wait_ge(*done(h, q, "gmean"))
                f(q.sq[:, :, :], q.yc, ACT.Square).then_inc(q.squared.sem, 1)
                yield
                act.wait_ge(*full(h, q, "gvar"))
                f(q.sd[:, :], tile_of(h, q, "gvar")[:, 0:BLK], ACT.Sqrt, bias=const("eps5", w=1)).then_inc(
                    q.act_took.sem, 1)
                yield
                yield
                yield
                act.wait_ge(*done(h, q, "wo"))
                state(1)
                yield from norm(h, q, 1, lambda c: vec(w, R, "ln2_b", c), padded(q))
                act.wait_ge(*full(h, q, "fr"))
                f(q.tr, pair(h, q, "fr"), ACT.Tanh, scale=0.5).then_inc(q.act_took.sem, 1)
                act.wait_ge(*full(h, q, "fk"))
                f(q.rl, pair(h, q, "fk"), ACT.Relu).then_inc(q.act_took.sem, 1)
                act.wait_ge(*done(h, q, "fk"))
                f(q.k2, q.rl, ACT.Square).then_inc(q.ffn_sq.sem, 1)
                yield
                yield

            def mlp(h, q, fields, hd):
                for n in range(HID // P // 4):
                    act.wait_ge(*full(h, q, f"hid.{n}"))
                    for e in range(4):
                        i = f(hd[:, 4 * n + e], fours(h, q, f"hid.{n}")[:, e], ACT.Gelu_apprx_tanh,
                              bias=vec(weights[h.loop], fields, "b1", 4 * n + e))
                    i.then_inc(q.act_took.sem, 1)
                yield
                yield

            def heads_out(h, q, name, b, ca):
                act.wait_ge(*full(h, q, name))
                f(ca[:, :, b * T:(b + 1) * T], tile_of(h, q, name).rearrange("p (t q) -> p t q", t=TQ),
                  ACT.Copy).then_inc(q.act_took.sem, 1)

            def take_context(h, q):
                act.wait_ge(*q.xout_ready.before(h))
                act.wait_ge(*q.inputs_in(h, 47 if h.loop == PERCEIVER else 31))
                f(q.CX[h.loop], q.cin[:, :, :], ACT.Copy).then_inc(q.ctx_ready.sem, 1)

            def perceiver(h, q):
                w = weights[h.loop]
                take_context(h, q)
                for n in range(2):
                    act.wait_ge(*full(h, q, f"pq{n}"))
                    for t in range(2):
                        m = f(q.qa[:, 2 * n + t], pair(h, q, f"pq{n}")[:, t], ACT.Identity, scale=1.0 / HD,
                              bias=prep[:, 2 * n + t:2 * n + t + 1])
                    m.then_inc(q.act_took.sem, 1)
                yield
                for t in range(TQ):
                    act.wait_ge(*full(h, q, f"pk{t}"))
                    for s in range(2):
                        m = f(q.ka[:, t, s::2, :], by_row(pair(h, q, f"pk{t}")[:, s]), ACT.Identity,
                              bias=vec(w, PERC, "kb", t))
                    m.then_inc(q.act_took.sem, 1)
                yield
                yield
                for b in range(GB):
                    yield
                    yield
                    yield
                    for kt in range(2):
                        act.wait_ge(*full(h, q, f"pt{b}.{kt}"))
                        f(q.pt.rearrange("p h q -> p (h q)"),
                          tile_of(h, q, f"pt{b}.{kt}", 4).rearrange("p j n -> p (j n)"), ACT.Exp).then_inc(
                            q.act_took.sem, 1)
                        yield
                        if kt == 0:
                            heads_out(h, q, f"pc{b}.0", b, q.ca)
                    yield
                yield
                yield
                act.wait_ge(*done(h, q, "o0"))
                yield
                yield from norm(h, q, 0, None, None, mean=False)
                yield from mlp(h, q, PERC, q.phd)

            def decoder(h, q):
                w = weights[h.loop]
                take_context(h, q)

                def plain(c):
                    return q.xn[:, c]

                for a in range(2):
                    yield from norm(h, q, a, lambda c: vec(w, DEC, f"ln{1 + a}_b", c), plain)
                    act.wait_ge(*full(h, q, f"dq{a}"))
                    for c in range(NC_):
                        for e, (dst, mask) in enumerate(((q.qe, "even"), (q.qo, "odd"))):
                            n = TQ + (2 * a + e) * NC_ + c
                            m = f(dst[:, c], pair(h, q, f"dq{a}")[:, c], ACT.Identity, scale=const(mask, w=1),
                                  bias=prep[:, n:n + 1])
                    m.then_inc(q.act_took.sem, 1)
                    act.wait_ge(*full(h, q, f"dk{a}"))
                    for c in range(NC_):
                        m = f(q.ks[:, c], pair(h, q, f"dk{a}")[:, c], ACT.Identity, bias=vec(w, DEC, f"kb{a}", c))
                    m.then_inc(q.act_took.sem, 1)
                    yield
                    for b in range(GB):
                        yield
                        yield
                        act.wait_ge(*q.s_sub(h, GB * a + b))
                        f(q.tt, q.tt, ACT.Exp).then_inc(q.probs.sem, 1)
                        yield
                        act.wait_ge(*full(h, q, f"dt{a}.{b}"))
                        f(q.p2.rearrange("p h q -> p (h q)"),
                          tile_of(h, q, f"dt{a}.{b}", 4).rearrange("p j n -> p (j n)"), ACT.Copy).then_inc(
                            q.act_took.sem, 1)
                        yield
                        heads_out(h, q, f"dc{a}.{b}", b, q.dca)
                        yield
                    yield
                    yield
                    yield
                yield from norm(h, q, 2, lambda c: vec(w, DEC, "ln3_b", c), plain)
                yield from mlp(h, q, DEC, q.dhd)

            def from_start(program):
                def started(h, q):
                    if isinstance(h.it, int) and h.it == 0:
                        act.wait_ge(weights_loaded[h.loop], 16)
                        act.wait_ge(q.prepared, h.loop + 1)
                    yield from program(h, q)

                return started

            for q in streams:
                for signal in (q.act_took, q.ctx_ready, q.squared, q.normed, q.state_in, q.decay, q.v_high, q.g_tanh,
                               q.s0_placed, q.ffn_sq, q.probs):
                    act.sem_inc(signal.sem, signal.start)
            act.wait_ge(const_loaded, 32)
            f(up_r[:, :], const("up", w=2 * P), ACT.Copy).then_inc(up_written, 1)
            run(act, [from_start(program) for program in (rwkv, perceiver, decoder, rwkv)])

        @block.vector
        def _(dve):
            V = nc.vector

            def spread_out(h, q):
                V.tensor_tensor(q.rm[:, :, :], wide(q.rs[:, :], 4), inner(const("block", w=4), BLK),
                                ALU.mult).then_inc(q.spread.sem, 1)

            def norm(h, q, i, n, weight, dst, mean=True):
                if mean:
                    dve.wait_ge(*full(h, q, f"mean{i}"))
                    V.tensor_tensor(q.xc[:, :, :], q.X[:, :, :], wide(tile_of(h, q, f"mean{i}")[:, 0:N], NC_),
                                    ALU.subtract).then_inc(q.dve_took.sem, 1)
                    yield
                dve.wait_ge(*done(h, q, f"var{i}"))
                V.reciprocal(q.rs[:, :], q.sd[:, :]).then_inc(q.inverted.sem, 1)
                dve.wait_ge(*q.inverted(h, n))
                spread_out(h, q)
                yield
                dve.wait_ge(*full(h, q, f"scale{i}"))
                for c in range(NC_):
                    m = V.scalar_tensor_tensor(dst(c), by_row(q.xc[:, c]), weight(c),
                                               by_row(tile_of(h, q, f"scale{i}")[:, 0:N]), ALU.mult, ALU.mult)
                m.then_inc(q.dve_took.sem, 1)

            def take_input(h, q, n):
                dve.wait_ge(*q.inputs_in(h, n - 1))
                dve.wait_ge(*q.stored.before(h))
                V.tensor_copy(q.X[:, :, :], q.xin[:, :, :]).then_inc(q.x_ready.sem, 1)
                dve.wait_ge(*q.x_ready(h))

            def rwkv(h, q):
                w, R = weights[h.loop], RWKV

                def sxc(c):
                    return q.sx[:, c * GB:(c + 1) * GB, :]

                def xac(c):
                    return q.xap[:, c * GB:(c + 1) * GB, 1:T + 1]

                def shift(n):
                    dve.wait_ge(*q.normed(h, n))
                    dve.wait_ge(*q.state_in(h, n))
                    V.tensor_tensor(q.sx, q.xap[:, :, 0:T], q.xap[:, :, 1:T + 1], ALU.subtract).then_inc(
                        q.shifted.sem, 1)
                    dve.wait_ge(*q.shifted(h, n))

                take_input(h, q, 32)
                yield from norm(h, q, 0, 0, lambda c: vec(w, R, "ln1_w", c), xac)
                yield
                shift(0)
                for c in range(NC_):
                    m = V.scalar_tensor_tensor(by_row(q.mi[:, c]), sxc(c), vec(w, R, "maa_x", c), xac(c), ALU.mult,
                                               ALU.add)
                m.then_inc(q.mixed_in.sem, 1)
                yield
                for n in range(5):
                    dve.wait_ge(*full(h, q, f"maa.{n}"))
                    if n >= 2:
                        dve.wait_ge(*q.xf_ready(h, n - 2))
                    for c in range(NC_):
                        m = V.scalar_tensor_tensor(by_row(q.tmp[n % 2][:, c]), by_row(pair(h, q, f"maa.{n}")[:, c]),
                                                   vec(w, R, "maa", 2 * n + c), sxc(c), ALU.add, ALU.mult)
                    m.then_inc(q.dve_took.sem, 1)
                yield
                yield
                yield
                dve.wait_ge(*done(h, q, "r"))
                for c in range(NC_):
                    m = V.scalar_tensor_tensor(q.ruk[:, c], q.rr[:, c], vec(w, R, "u", c), q.kk[h.loop][:, c], ALU.mult,
                                               ALU.mult)
                m.then_inc(q.ruk_ready.sem, 1)
                dve.wait_ge(*full(h, q, "g"))
                dve.wait_ge(*q.g_tanh(h))
                V.scalar_tensor_tensor(q.g2, q.tg, 1.0, pair(h, q, "g"), ALU.add, ALU.mult).then_inc(q.dve_took.sem, 1)
                yield
                dve.wait_ge(*full(h, q, "bonus"))
                dve.wait_ge(*done(h, q, "v"))
                V.tensor_tensor(q.bv[h.loop], q.vv, wide(tile_of(h, q, "bonus")[:, 0:N], 2), ALU.mult).then_inc(
                    q.dve_took.sem, 1)
                for c in range(NC_):
                    for j in range(4):
                        dve.wait_ge(*full(h, q, f"vb.{c}.{j}"))
                        V.tensor_tensor(
                            q.kv[c][:, j::4].rearrange("p j (b t) -> p j b t", b=GB)[:, :, :, 1:T],
                            by_row(q.kk[h.loop][:, c])[:, :, 0:T - 1].rearrange("p (o b) t -> p o b t", o=1).to_broadcast(
                                [P, 2, GB, T - 1]),
                            tile_of(h, q, f"vb.{c}.{j}")[:, 0:2 * N].rearrange("p (j b t) -> p j b t", j=2, b=GB)[:, :, :,
                                                                                                      0:T - 1],
                            ALU.mult).then_inc(q.dve_took.sem, 1)
                    dve.wait_ge(*done(h, q, f"vb.{c}.3"))
                    dve.wait_ge(*q.s0_placed(h, c))
                    dve.wait_ge(*q.decay(h))
                    for j in range(S8):
                        m = V.tensor_tensor_scan(q.kv[c][:, j], q.ws[:, c].rearrange("p b t -> p (b t)"),
                                                 q.kv[c][:, j], 0.0, ALU.mult, ALU.add)
                    m.then_inc(q.scanned.sem, 1)
                    if c == 1:
                        dve.wait_ge(*q.scanned(h, 1))
                        V.tensor_tensor(q.kv[1], q.kv[1], wide(q.rr[:, 1], S8), ALU.mult).then_inc(
                            q.r_state[1].sem, 1)
                    yield
                dve.wait_ge(*full(h, q, "y"))
                dve.wait_ge(*done(h, q, "bonus"))
                V.tensor_tensor(q.yy[h.loop], q.bv[h.loop], pair(h, q, "y"), ALU.add).then_inc(q.dve_took.sem, 1)
                yield
                dve.wait_ge(*full(h, q, "gmean"))
                dve.wait_ge(*done(h, q, "y"))
                V.tensor_tensor(q.yc, q.yy[h.loop], wide(tile_of(h, q, "gmean")[:, 0:N], 2), ALU.subtract).then_inc(
                    q.dve_took.sem, 1)
                yield
                dve.wait_ge(*done(h, q, "gvar"))
                V.reciprocal(q.rs[:, :], q.sd[:, :]).then_inc(q.inverted.sem, 1)
                dve.wait_ge(*q.inverted(h, 1))
                spread_out(h, q)
                yield
                dve.wait_ge(*full(h, q, "gscale"))
                for c in range(NC_):
                    m = V.scalar_tensor_tensor(q.yn[:, c], q.yc[:, c], vec(w, R, "gn_w", c),
                                               tile_of(h, q, "gscale")[:, 0:N], ALU.mult, ALU.mult)
                m.then_inc(q.dve_took.sem, 1)
                dve.wait_ge(*done(h, q, "gscale"))
                for c in range(NC_):
                    m = V.scalar_tensor_tensor(q.og[:, c], q.yn[:, c], vec(w, R, "gn_b", c), q.g2[:, c], ALU.add,
                                               ALU.mult)
                m.then_inc(q.gated.sem, 1)
                yield
                dve.wait_ge(*full(h, q, "wo"))
                V.scalar_tensor_tensor(q.X[:, :, :], pair(h, q, "wo"), 0.5, q.X[:, :, :], ALU.mult,
                                       ALU.add).then_inc(q.dve_took.sem, 1)
                dve.wait_ge(*done(h, q, "wo"))
                yield
                yield from norm(h, q, 1, 2, lambda c: vec(w, R, "ln2_w", c), xac)
                yield
                shift(1)
                for dst, v in ((q.ri, "fr"), (q.ki, "fk")):
                    for c in range(NC_):
                        m = V.scalar_tensor_tensor(by_row(dst[:, c]), sxc(c), vec(w, R, v, c), xac(c), ALU.mult,
                                                   ALU.add)
                    m.then_inc(q.ffn_in.sem, 1)
                yield
                dve.wait_ge(*full(h, q, "fv"))
                dve.wait_ge(*done(h, q, "fr"))
                V.scalar_tensor_tensor(q.ff, q.tr, 1.0, pair(h, q, "fv"), ALU.add, ALU.mult).then_inc(
                    q.dve_took.sem, 1)
                dve.wait_ge(*done(h, q, "fv"))
                V.scalar_tensor_tensor(q.X[:, :, :], q.ff, 0.5, q.X[:, :, :], ALU.mult, ALU.add).then_inc(
                    q.xout_ready.sem, 1)
                yield

            def softmax_out(h, q, a, z, ca, cn, fields, bias, dst):
                dve.wait_ge(*full(h, q, f"den{a}"))
                V.reciprocal(q.rs[:, :], tile_of(h, q, f"den{a}")[:, 0:BLK]).then_inc(q.dve_took.sem, 1)
                dve.wait_ge(*done(h, q, f"den{a}"))
                spread_out(h, q)
                yield
                dve.wait_ge(*full(h, q, f"inv{a}"))
                V.tensor_tensor(cn, ca, fours(h, q, f"inv{a}"), ALU.mult).then_inc(q.dve_took.sem, 1)
                yield
                add_out(h, q, f"o{a}", fields, bias, dst).then_inc(q.dve_took.sem, 1)
                dve.wait_ge(*done(h, q, f"o{a}"))
                yield

            def add_out(h, q, name, fields, bias, dst):
                dve.wait_ge(*full(h, q, name))
                for c in range(NC_):
                    m = V.scalar_tensor_tensor(dst[:, c], pair(h, q, name)[:, c],
                                               vec(weights[h.loop], fields, bias, c), q.X[:, c], ALU.add, ALU.add)
                return m

            def mlp(h, q, fields):
                yield
                add_out(h, q, "down", fields, "b2", q.X).then_inc(q.dve_took.sem, 1)
                dve.wait_ge(*done(h, q, "down"))
                dve.sem_inc(q.xout_ready.sem, 1)
                yield

            def values(h, q, name, va, slots, fields, vb, count):
                dve.wait_ge(*full(h, q, name))
                o = tile_of(h, q, name).rearrange("p (s h d) -> p s h d", s=2, h=NH)
                a = fields[vb][0]
                for s in range(count):
                    m = V.tensor_tensor(va[:, slots + s, :, 0:HD], o[:, s],
                                        weights[h.loop][:, a:a + C].rearrange("p (h d) -> p h d", h=NH), ALU.add)
                m.then_inc(q.dve_took.sem, 1)

            def perceiver(h, q):
                take_input(h, q, 48)
                V.tensor_scalar(q.pmask, q.pmin, 0, MASKED, ALU.is_equal, ALU.mult).then_inc(
                    q.masks_ready.sem, 1)
                yield
                yield
                for b in range(GB):
                    values(h, q, f"pv{b}", q.pva, 2 * b, PERC, "vb", 2)
                yield
                for b in range(GB):
                    for u in range(2):
                        dve.wait_ge(*full(h, q, f"ps{b}.{u}"))
                        V.tensor_reduce(q.mxp[:, 2 * u:2 * u + 2, HD + 1::SLOT].rearrange("p t j -> p j t"),
                                        tile_of(h, q, f"ps{b}.{u}", 4).rearrange("p j (t k) -> p j t k", t=2), AX.X,
                                        ALU.max, negate=True).then_inc(q.dve_took.sem, 1)
                        yield
                    dve.wait_ge(*full(h, q, f"pm{b}"))
                    if b == 0:
                        dve.wait_ge(*done(h, q, "pq1"))
                    else:
                        dve.wait_ge(*full(h, q, f"pt{b - 1}.1"))
                    V.tensor_tensor(q.qb, q.qa[:, :, b * T:(b + 1) * T],
                                    tile_of(h, q, f"pm{b}").rearrange("p (t q) -> p t q", t=TQ), ALU.add).then_inc(
                        q.dve_took.sem, 1)
                    yield
                    yield
                    yield
                    dve.wait_ge(*full(h, q, f"pc{b}.1"))
                    dve.wait_ge(*done(h, q, f"pc{b}.0"))
                    out_b = q.ca[:, :, b * T:(b + 1) * T]
                    V.tensor_tensor(out_b, out_b, tile_of(h, q, f"pc{b}.1").rearrange("p (t q) -> p t q", t=TQ),
                                    ALU.add).then_inc(q.dve_took.sem, 1)
                    dve.wait_ge(*done(h, q, f"pc{b}.1"))
                    yield
                yield from softmax_out(h, q, 0, 0, q.ca, q.cn, PERC, "ob", q.xc)
                yield from norm(h, q, 0, 0, lambda c: vec(weights[h.loop], PERC, "norm_w", c),
                                lambda c: by_row(q.xn[:, c]), mean=False)
                yield
                yield from mlp(h, q, PERC)

            def decoder(h, q):
                w = weights[h.loop]
                take_input(h, q, 32)
                for a in range(2):
                    if a == 1:
                        dve.wait_ge(*q.mask_in(h, 15))
                        V.tensor_scalar(q.mc_add, q.mc[:, :, :], -1.0, 10000.0, ALU.add, ALU.mult).then_inc(
                            q.masks_ready.sem, 1)
                    yield from norm(h, q, a, a, lambda c: vec(w, DEC, f"ln{1 + a}_w", c),
                                    lambda c: by_row(q.xn[:, c]))
                    yield
                    values(h, q, f"dv{a}", q.dva, 0, DEC, f"vb{a}", GB)
                    yield
                    for b in range(GB):
                        m = ltor[:, :] if a == 0 else q.mc[:, b, :]
                        n = GB * a + b
                        if a == 1 and b == 0:
                            dve.wait_ge(*q.masks_ready(h))
                        dve.wait_ge(*full(h, q, f"ds{a}.{b}"))
                        if b > 0:
                            dve.wait_ge(*full(h, q, f"dt{a}.{b - 1}"))
                        scores = tile_of(h, q, f"ds{a}.{b}", 4).rearrange("p j (t k) -> p (j t) k", t=TQ)
                        V.tensor_tensor(q.tt[:, 0:NH // 2], scores[:, 0:NH // 2], wide(m, NH // 2), ALU.mult).then_inc(
                            q.half_masked.sem, 1)
                        V.tensor_tensor(q.tt[:, NH // 2:], scores[:, NH // 2:], wide(m, NH // 2), ALU.mult).then_inc(
                            q.dve_took.sem, 1)
                        dve.wait_ge(*done(h, q, f"ds{a}.{b}"))
                        V.tensor_tensor(q.tt[:, NH // 2:], q.tt[:, NH // 2:],
                                        wide(ltor_add[:, :] if a == 0 else q.mc_add[:, b, :], NH // 2),
                                        ALU.add).then_inc(q.half_added.sem, 1)
                        yield
                        dve.wait_ge(*q.half_added(h, n))
                        dve.wait_ge(*q.s_add(h, n))
                        V.tensor_reduce(q.mx[:, :], q.tt, AX.X, ALU.max).then_inc(q.max_ready.sem, 1)
                        dve.wait_ge(*q.max_ready(h, n))
                        V.tensor_tensor(q.tt, q.tt, inner(q.mx[:, :], T), ALU.subtract).then_inc(q.s_sub.sem, 1)
                        yield
                        yield
                        yield
                        yield
                    yield from softmax_out(h, q, a, 2 * a + 1, q.dca, q.dcn, DEC, f"ob{a}", q.X)
                yield from norm(h, q, 2, 2, lambda c: vec(w, DEC, "ln3_w", c), lambda c: by_row(q.xn[:, c]))
                yield
                yield from mlp(h, q, DEC)

            def prepare(h, q):
                w = weights[h.loop]
                if q.s == 0:
                    dve.wait_ge(weights_loaded[h.loop], 16)
                    if h.loop == PERCEIVER:
                        a = PERC["qb"][0]
                        V.tensor_scalar(prep[:, 0:TQ], w[:, a:a + TQ], 1.0 / HD, None, ALU.mult)
                    if h.loop == DECODER:
                        for i in range(2):
                            a = DEC[f"qb{i}"][0]
                            for e, m in enumerate(("even", "odd")):
                                s = TQ + (2 * i + e) * NC_
                                V.tensor_scalar(prep[:, s:s + NC_], w[:, a:a + NC_], const(m, w=1), None, ALU.mult)
                        V.tensor_scalar(ltor_add[:, :], ltor[:, :], -1.0, 10000.0, ALU.add, ALU.mult)
                if h.loop > 0:
                    dve.wait_ge(*q.xout_ready(Place(h.loop - 1, ROUNDS - 1)))
                if h.loop in (RWKV0, RWKV1):
                    m = V.memset(q.ws[:, :, :, 0:1], 0.0)
                else:
                    if h.loop == PERCEIVER:
                        V.memset(q.mxp, 0.0)
                    V.memset(q.pva[:, :, :, HD:HD + 1], 1.0)
                    m = V.memset(q.pva[:, :, :, HD + 1:], 0.0)
                m.then_inc(q.prepared, 1)
                dve.wait_ge(q.prepared, h.loop + 1)

            def from_start(program):
                def started(h, q):
                    if isinstance(h.it, int) and h.it == 0:
                        prepare(h, q)
                    dve.wait_ge(*q.xout_ready.before(h))
                    yield from program(h, q)

                return started

            for q in streams:
                for signal in (q.dve_took, q.x_ready, q.xout_ready, q.masks_ready, q.inverted, q.spread, q.shifted,
                               q.mixed_in, q.ruk_ready, q.scanned, q.r_state[1], q.gated, q.ffn_in, q.max_ready,
                               q.half_masked, q.half_added, q.s_sub):
                    dve.sem_inc(signal.sem, signal.start)
            dve.wait_ge(const_loaded, 32)
            run(dve, [from_start(program) for program in (rwkv, perceiver, decoder, rwkv)])

        @block.gpsimd
        def _(pool):
            G = nc.gpsimd

            def rows(ap):
                return ap.rearrange("p c (b t) -> p (c b) t", b=GB)

            def rwkv(h, q):
                for _ in range(4):
                    yield
                for n in range(5):
                    pool.wait_ge(*done(h, q, f"maa.{n}"))
                    G.tensor_tensor(rows(q.xf[n]), rows(q.tmp[n % 2]), q.xap[:, :, 1:T + 1], ALU.add).then_inc(
                        q.xf_ready.sem, 1)
                yield
                yield
                pool.wait_ge(*q.v_high(h))
                pool.wait_ge(*done(h, q, "v"))
                G.tensor_tensor(q.vlo[:, :, :], q.vv, q.vhi[:, :, :].bitcast(F32), ALU.subtract).then_inc(
                    q.v_low.sem, 1)
                yield
                yield
                pool.wait_ge(*q.scanned(h, 0))
                G.tensor_tensor(q.kv[0], q.kv[0], wide(q.rr[:, 0], S8), ALU.mult).then_inc(q.r_state[0].sem, 1)
                for _ in range(12):
                    yield

            def decoder(h, q):
                for a in range(2):
                    for _ in range(4):
                        yield
                    for b in range(GB):
                        pool.wait_ge(*q.half_masked(h, GB * a + b))
                        if a == 1 and b == 0:
                            pool.wait_ge(*q.masks_ready(h))
                        m = ltor_add[:, :] if a == 0 else q.mc_add[:, b, :]
                        G.tensor_tensor(q.tt[:, 0:NH // 2], q.tt[:, 0:NH // 2], wide(m, NH // 2), ALU.add).then_inc(
                            q.s_add.sem, 1)
                        for _ in range(5):
                            yield
                    for _ in range(3):
                        yield
                for _ in range(5):
                    yield

            for q in streams:
                for signal in (q.xf_ready, q.v_low, q.r_state[0], q.s_add):
                    pool.sem_inc(signal.sem, signal.start)
            run(pool, [rwkv, idle, decoder, rwkv])




HEAD_ROWS = np.array([S8 * (p % RH) + 4 * t + p // RH for t in range(NC_) for p in range(P)])


def _k_tiles(w, k=NC_):
    return np.ascontiguousarray(w.reshape(k, P, -1).transpose(1, 0, 2)).reshape(P, -1)


def _vec(v):
    return np.ascontiguousarray(v.reshape(-1, P).T)


def _rows(w):
    return np.concatenate([w, np.zeros((P - w.shape[0], w.shape[1]), np.float32)], 0)


def _pack(fields, part):
    for name, (_, width) in fields.items():
        assert part[name].shape == (P, width), (name, part[name].shape, width)
    return np.ascontiguousarray(np.concatenate([part[name] for name in fields], 1))


def _slots(w, heads, fill=None):
    out = np.zeros((w.shape[0], NH, SLOT), np.float32)
    out[:, :, :HD] = w.reshape(-1, NH, HD)[:, heads]
    if fill:
        for k, v in fill.items():
            out[:, :, k] = v
    return out.reshape(-1, NH * SLOT)


def _rwkv_pack(a, l):
    names = dict(zip(("td1", "td2", "u", "fk", "fr", "Fk", "Fr", "Fv"),
                     ("td_w1", "td_w2", "u", "ffn_maa_k", "ffn_maa_r", "Wfk", "Wfr", "Wfv") if l == 0 else
                     ("decay_w1", "decay_w2", "faaaa", "fmaa_k", "fmaa_r", "fWk", "fWr", "fWv")))
    if l == 0:
        maa = a["maa_stack"].reshape(5, C)
    else:
        maa = np.stack([a["maa_" + x] for x in ORDER[1]])
    w2 = a["maa_w2"].reshape(160, C)
    part = {
        "w1": _k_tiles(a["maa_w1"]), "w2": w2[:P], "w2b": _rows(w2[P:]), "td1": _k_tiles(a[names["td1"]]),
        "td2": _rows(a[names["td2"]]), "maa": _vec(maa), "td": _vec(a["time_decay"]), "u": _vec(a[names["u"]]),
        "fk": _vec(a[names["fk"]]), "fr": _vec(a[names["fr"]]),
    }
    part["Wr"], part["Wk"] = _k_tiles(a["Wr"].T), _k_tiles(a["Wk"].T)
    part["Wv"], part["Wg"] = _k_tiles(a["Wv"].T[:, HEAD_ROWS]), _k_tiles(a["Wg"].T[:, HEAD_ROWS])
    part["Wo"] = _k_tiles(a["Wo"].T[HEAD_ROWS])
    for w in ("Fk", "Fr", "Fv"):
        part[w] = _k_tiles(a[names[w]].T)
    for v in ("ln1_w", "ln1_b", "ln2_w", "ln2_b", "maa_x"):
        part[v] = _vec(a[v])
    for v in ("gn_w", "gn_b"):
        part[v] = _vec(a[v][HEAD_ROWS])
    return _pack(RWKV, part)


def kernel(**inputs):
    import concourse.bacc as _bacc
    from concourse.bass_utils import run_bass_kernel_spmd as _run

    a = {k: np.asarray(v) for k, v in inputs.items()}

    def layer(n):
        return {k.split("_xattn_")[1]: v for k, v in a.items() if k.startswith(f"L{n}_")}

    def tokens(v):
        v = v.reshape(GROUPS, N, NC_, P).transpose(0, 3, 2, 1)
        return np.ascontiguousarray(v).reshape(GROUPS, P, NC_ * N)

    ctxt = a["ctx_2048"]
    rows = ctxt[:, 0:2].reshape(GROUPS, GB, 2, NC_, P).transpose(0, 4, 2, 3, 1).reshape(GROUPS, P, -1)
    s0 = ctxt[:, 2:2 + S8].reshape(GROUPS, GB, NC_, P, S8).transpose(0, 3, 2, 4, 1).reshape(GROUPS, P, -1)

    plain = list(range(NH))
    paired = [8 * (t // 2) + 2 * j + t % 2 for t in range(TQ) for j in range(4)]

    def out_rows(w, heads):
        return _k_tiles(np.ascontiguousarray(_slots(np.ascontiguousarray(w.T), heads).T), TQ)

    p1 = layer(1)
    kvw = p1["kv_w"].reshape(C, NH * HD, 2)
    kvb = p1["kv_b"].reshape(NH * HD, 2)

    def all_rows(v):
        return np.ascontiguousarray(np.broadcast_to(v.reshape(1, -1), (P, v.size)))

    perc = _pack(PERC, {
        "q": _k_tiles(_slots(p1["q_w"], plain)), "k": _k_tiles(_slots(kvw[..., 0], plain)),
        "v": _k_tiles(np.ascontiguousarray(kvw[..., 1])), "o": out_rows(p1["out_w"], plain),
        "m1": _k_tiles(p1["mlp_w1"]), "m2": _k_tiles(p1["mlp_w2"], HID // P),
        "qb": _vec(_slots(p1["q_b"].reshape(1, -1), plain, {HD: float(HD)})),
        "kb": _vec(_slots(kvb[:, 0].reshape(1, -1), plain, {HD + 1: 1.0})),
        "vb": all_rows(kvb[:, 1]), "ob": _vec(p1["out_b"]), "norm_w": _vec(p1["postnorm_w"]),
        "b1": _vec(p1["mlp_b1"]), "b2": _vec(p1["mlp_b2"])})
    d = layer(2)
    part = {"m1": _k_tiles(d["w1"]), "m2": _k_tiles(d["w2"], HID // P), "b1": _vec(d["b1"]), "b2": _vec(d["b2"])}
    for n, x in enumerate("qkv"):
        w = d["w_q"] if x == "q" else d["w_kv"][:, (n - 1) * C:n * C]
        b = d["b_q"] if x == "q" else d["b_kv"][(n - 1) * C:n * C]
        for i, (wi, bi) in enumerate(((d["w_qkv"][:, n * C:(n + 1) * C], d["b_qkv"][n * C:(n + 1) * C]), (w, b))):
            part[f"{x}{i}"] = _k_tiles(np.ascontiguousarray(wi))
            part[f"{x}b{i}"] = all_rows(bi) if x == "v" else _vec(bi)
    for i, x in enumerate(("ao", "co")):
        part[f"o{i}"] = out_rows(d["w_" + x], paired)
        part[f"ob{i}"] = _vec(d["b_" + x])
    for n in (1, 2, 3):
        part[f"ln{n}_w"], part[f"ln{n}_b"] = _vec(d[f"ln{n}_s"]), _vec(d[f"ln{n}_b"])
    dec = _pack(DEC, part)

    arrays = {
        "x": tokens(a["x"]), "ctx": tokens(ctxt),
        "state": np.ascontiguousarray(np.concatenate([rows, s0], 2)),
        "pmask": np.ascontiguousarray(a["mask_BxS2_ik0"].reshape(GROUPS, N)),
        "cross": np.ascontiguousarray(a["mask_Bx1xSxS2_ff1"].reshape(GROUPS, GB, T, T).transpose(0, 2, 1, 3)),
        "ltor": np.ascontiguousarray(a["mask_1x1xSxS2_fc1"].reshape(T, T)),
        "const": _constants(), "rwkv0": _rwkv_pack(layer(0), 0), "perc": perc, "dec": dec,
        "rwkv1": _rwkv_pack(layer(3), 1),
    }
    nc = _bacc.Bacc("TRN2", target_bir_lowering=False, num_devices=1)
    args = [nc.dram_tensor(f"in_{k}", v.shape, mybir.dt.from_np(v.dtype), kind="ExternalInput").ap()
            for k, v in arrays.items()]
    out = nc.dram_tensor("out_x", (GROUPS, P, NC_ * N), F32, kind="ExternalOutput").ap()
    between = [nc.dram_tensor(f"between{k}", (GROUPS, P, NC_ * N), F32, kind="Internal").ap() for k in range(LOOPS - 1)]
    build_program(nc, *args, between, out)
    r = _run(nc, [{f"in_{k}": v for k, v in arrays.items()}], core_ids=[0])
    got = r.results[0]["out_x"].reshape(GROUPS, P, NC_, N).transpose(0, 3, 2, 1)
    return np.ascontiguousarray(got).reshape(B, T, C)
```
